# Optimizing a Trainium2 kernel written in Bass

```python
import numpy as np
import jax
import jax.numpy as jnp

def _softmax(x, axis=-1):
    return jax.nn.softmax(x, axis=axis)

def _gelu(x):
    return jax.nn.gelu(x, approximate=True)

def _silu(x):
    return jax.nn.silu(x)

def _sigmoid(x):
    return jax.nn.sigmoid(x)

def _layernorm(x, axis=-1, eps=1e-05):
    m = jnp.mean(x, axis=axis, keepdims=True)
    v = jnp.var(x, axis=axis, keepdims=True)
    return (x - m) / jnp.sqrt(v + eps)

def _scatter_add(tgt, idx, src, axis=0):
    return tgt.at[idx].add(src)

def _segment_sum(src, seg, n):
    return jax.ops.segment_sum(src, seg, n)
kernel_name = 'mk_decoder_preln_d1_seqx_r4_7224eb'

def setup_inputs(seed: int=0):
    np.random.seed(seed)
    _w = jnp.asarray

    def _rec_inputs():
        import jax
        import jax.numpy as jnp
        _rk = jax.random.key(seed)
        x = -0.0002928 + 1 * jax.random.normal(jax.random.fold_in(_rk, 1), (8, 512, 256), jnp.float32)
        _lenS = 512 - jax.random.randint(jax.random.fold_in(_rk, 7), (8,), 0, max(1, 512 // 4) + 1, jnp.int32)
        _lenS2 = 1601 - jax.random.randint(jax.random.fold_in(_rk, 8), (8,), 0, max(1, 1601 // 4) + 1, jnp.int32)
        _ctx_512P = jax.random.normal(jax.random.fold_in(_rk, 11), (8, 16, 128), jnp.float32)
        _ctx_512c = jax.random.dirichlet(jax.random.fold_in(_rk, 511), 0.3 * jnp.ones((16,), jnp.float32), (8, 1601))
        _ctx_512t = jnp.einsum('bsk,bkd->bsd', _ctx_512c, _ctx_512P)
        _ctx_512t = _ctx_512t * jax.lax.rsqrt(jnp.mean(jnp.square(_ctx_512t)) + 1e-12) * 0.953939
        ctx_512 = 0.00222621 + 0.99962 * (_ctx_512t + 0.3 * jax.random.normal(jax.random.fold_in(_rk, 611), (8, 1601, 128), jnp.float32))
        return (x, ctx_512)
    x, ctx_512 = _rec_inputs()

    def _L0_attn_setup():
        import jax, jax.numpy as jnp
        import numpy as np
        B, L, D = (2, 512, 256)
        H, HD = (16, 64)
        LD = 64
        key = jax.random.key(seed)
        ks = jax.random.split(key, 6)
        s = lambda fan_in: 1.0 / np.sqrt(fan_in)
        x_bld = jax.random.normal(ks[0], (B, L, D), dtype=jnp.float32)
        Wq = jax.random.normal(ks[1], (D, H, HD), dtype=jnp.float32) * s(D)
        Wkv_down = jax.random.normal(ks[2], (D, LD), dtype=jnp.float32) * s(D)
        Wk_up = jax.random.normal(ks[3], (LD, H, HD), dtype=jnp.float32) * s(LD)
        Wv_up = jax.random.normal(ks[4], (LD, H, HD), dtype=jnp.float32) * s(LD)
        Wout = jax.random.normal(ks[5], (H, HD, D), dtype=jnp.float32) * s(H * HD)
        return {'x_bld': x_bld, 'Wq': Wq, 'Wkv_down': Wkv_down, 'Wk_up': Wk_up, 'Wv_up': Wv_up, 'Wout': Wout}
    _L0_attn_all = _L0_attn_setup()
    _L0_attn_in = {k: v for k, v in _L0_attn_all.items() if k in ('Wq', 'Wkv_down', 'Wk_up', 'Wv_up', 'Wout')}
    del _L0_attn_all

    def _L0_xattn_setup():
        import jax, jax.numpy as jnp
        import numpy as np
        B, T, TC, C, CC, H = (2, 512, 128, 256, 128, 16)
        D = C // H

        def _heads(t):
            b, l, _ = t.shape
            return t.reshape(b, l, H, D).transpose(0, 2, 1, 3)
        key = jax.random.key(seed)
        ks = jax.random.split(key, 18)
        w = lambda k, i, o: jax.random.normal(k, (i, o), jnp.float32) / np.sqrt(i).astype(np.float32)
        return {'x': jax.random.normal(ks[0], (B, T, C), jnp.float32), 'cross_input': jax.random.normal(ks[1], (B, TC, CC), jnp.float32), 'Wk': w(ks[2], C, C), 'bk': jnp.zeros((C,), jnp.float32), 'Wq': w(ks[3], C, C), 'bq': jnp.zeros((C,), jnp.float32), 'Wv': w(ks[4], C, C), 'bv': jnp.zeros((C,), jnp.float32), 'Wck': w(ks[5], CC, C), 'bck': jnp.zeros((C,), jnp.float32), 'Wcq': w(ks[6], C, C), 'bcq': jnp.zeros((C,), jnp.float32), 'Wcv': w(ks[7], CC, C), 'bcv': jnp.zeros((C,), jnp.float32), 'Wp': w(ks[8], C, C), 'bp': jnp.zeros((C,), jnp.float32)}
    _L0_xattn_all = _L0_xattn_setup()
    _L0_xattn_in = {k: v for k, v in _L0_xattn_all.items() if k in ('Wk', 'bk', 'Wq', 'bq', 'Wv', 'bv', 'Wck', 'bck', 'Wcq', 'bcq', 'Wcv', 'bcv', 'Wp', 'bp')}
    del _L0_xattn_all

    def _L0_ffn_setup():
        import math
        import jax, jax.numpy as jnp
        import numpy as np
        NUM_EXPERTS = 8
        TOP_K = 2
        CAPACITY_FACTOR = 1.0
        B, S, H, I = (4, 512, 256, 1024)
        key = jax.random.key(seed)
        k_x, k_rw, k_wi, k_wo = jax.random.split(key, 4)
        x = jax.random.normal(k_x, (B, S, H), dtype=jnp.float32)
        lim = math.sqrt(6.0 / (H + NUM_EXPERTS))
        router_w = jax.random.uniform(k_rw, (NUM_EXPERTS, H), minval=-lim, maxval=lim, dtype=jnp.float32)
        router_b = jnp.zeros((NUM_EXPERTS,), dtype=jnp.float32)
        experts_inter = jax.random.normal(k_wi, (NUM_EXPERTS - 1, H, I), dtype=jnp.float32) / math.sqrt(H)
        experts_out = jax.random.normal(k_wo, (NUM_EXPERTS - 1, I, H), dtype=jnp.float32) / math.sqrt(I)
        return {'x': x, 'router_w': router_w, 'router_b': router_b, 'experts_inter': experts_inter, 'experts_out': experts_out}
    _L0_ffn_all = _L0_ffn_setup()
    _L0_ffn_in = {k: v for k, v in _L0_ffn_all.items() if k in ('router_w', 'router_b', 'experts_inter', 'experts_out')}
    del _L0_ffn_all
    return {'x': x, 'ctx_512': ctx_512, 'L0_attn_Wq': _L0_attn_in['Wq'], 'L0_attn_Wkv_down': _L0_attn_in['Wkv_down'], 'L0_attn_Wk_up': _L0_attn_in['Wk_up'], 'L0_attn_Wv_up': _L0_attn_in['Wv_up'], 'L0_attn_Wout': _L0_attn_in['Wout'], 'L0_xattn_Wk': _L0_xattn_in['Wk'], 'L0_xattn_bk': _L0_xattn_in['bk'], 'L0_xattn_Wq': _L0_xattn_in['Wq'], 'L0_xattn_bq': _L0_xattn_in['bq'], 'L0_xattn_Wv': _L0_xattn_in['Wv'], 'L0_xattn_bv': _L0_xattn_in['bv'], 'L0_xattn_Wck': _L0_xattn_in['Wck'], 'L0_xattn_bck': _L0_xattn_in['bck'], 'L0_xattn_Wcq': _L0_xattn_in['Wcq'], 'L0_xattn_bcq': _L0_xattn_in['bcq'], 'L0_xattn_Wcv': _L0_xattn_in['Wcv'], 'L0_xattn_bcv': _L0_xattn_in['bcv'], 'L0_xattn_Wp': _L0_xattn_in['Wp'], 'L0_xattn_bp': _L0_xattn_in['bp'], 'L0_ffn_router_w': _L0_ffn_in['router_w'], 'L0_ffn_router_b': _L0_ffn_in['router_b'], 'L0_ffn_experts_inter': _L0_ffn_in['experts_inter'], 'L0_ffn_experts_out': _L0_ffn_in['experts_out']}

def reference(x, ctx_512, L0_attn_Wq, L0_attn_Wkv_down, L0_attn_Wk_up, L0_attn_Wv_up, L0_attn_Wout, L0_xattn_Wk, L0_xattn_bk, L0_xattn_Wq, L0_xattn_bq, L0_xattn_Wv, L0_xattn_bv, L0_xattn_Wck, L0_xattn_bck, L0_xattn_Wcq, L0_xattn_bcq, L0_xattn_Wcv, L0_xattn_bcv, L0_xattn_Wp, L0_xattn_bp, L0_ffn_router_w, L0_ffn_router_b, L0_ffn_experts_inter, L0_ffn_experts_out):
    import jax
    import jax.numpy as jnp

    def _L0_attn_ref(x_bld, Wq, Wkv_down, Wk_up, Wv_up, Wout):
        import jax, jax.numpy as jnp
        import numpy as np
        B, L, D = (2, 512, 256)
        H, HD = (16, 64)
        LD = 64
        q_blhd = jnp.einsum('bld,dhk->blhk', x_bld, Wq)
        latent_bll = jnp.einsum('bld,dc->blc', x_bld, Wkv_down)
        k_blhd = jnp.einsum('blc,chk->blhk', latent_bll, Wk_up)
        v_blhd = jnp.einsum('blc,chk->blhk', latent_bll, Wv_up)
        attn = jnp.einsum('bqhd,bkhd->bhqk', q_blhd, k_blhd) / jnp.sqrt(jnp.asarray(HD, dtype=x_bld.dtype))
        l = x_bld.shape[1]
        mask = (jnp.arange(l)[None, :] <= jnp.arange(l)[:, None])[None, None]
        neg_inf = jnp.finfo(attn.dtype).min
        attn = jax.nn.softmax(jnp.where(mask, attn, neg_inf), axis=-1)
        y_blhd = jnp.einsum('bhqk,bkhd->bqhd', attn, v_blhd)
        return jnp.einsum('bqhd,hdo->bqo', y_blhd, Wout)

    def _L0_xattn_ref(x, cross_input, Wk, bk, Wq, bq, Wv, bv, Wck, bck, Wcq, bcq, Wcv, bcv, Wp, bp):
        import jax, jax.numpy as jnp
        import numpy as np
        B, T, TC, C, CC, H = (2, 512, 128, 256, 128, 16)
        D = C // H

        def _heads(t):
            b, l, _ = t.shape
            return t.reshape(b, l, H, D).transpose(0, 2, 1, 3)
        scale = np.float32(1.0 / np.sqrt(D))
        q = _heads(x @ Wq + bq)
        k = _heads(x @ Wk + bk)
        v = _heads(x @ Wv + bv)
        att = jnp.einsum('bhqd,bhkd->bhqk', q, k) * scale
        causal = jnp.tril(jnp.ones((T, T), bool))
        att = jnp.where(causal[None, None], att, -jnp.inf)
        y = jnp.einsum('bhqk,bhkd->bhqd', jax.nn.softmax(att, axis=-1), v)
        qc = _heads(x @ Wcq + bcq)
        kc = _heads(cross_input @ Wck + bck)
        vc = _heads(cross_input @ Wcv + bcv)
        attc = jnp.einsum('bhqd,bhkd->bhqk', qc, kc) * scale
        y = y + jnp.einsum('bhqk,bhkd->bhqd', jax.nn.softmax(attc, axis=-1), vc)
        y = y.transpose(0, 2, 1, 3).reshape(x.shape[0], T, C)
        return y @ Wp + bp

    def _L0_ffn_ref(x, router_w, router_b, experts_inter, experts_out):
        import math
        import jax, jax.numpy as jnp
        import numpy as np
        NUM_EXPERTS = 8
        TOP_K = 2
        CAPACITY_FACTOR = 1.0
        B, S, H, I = (4, 512, 256, 1024)
        batch, seq, hidden = x.shape
        n_exp = router_w.shape[0]
        n_tok = batch * seq
        cap = math.ceil(n_tok / n_exp * CAPACITY_FACTOR)
        logits = jnp.einsum('bsh,eh->bse', x, router_w) + router_b
        weights_flat = jax.nn.softmax(logits, axis=-1).reshape(n_tok, n_exp)
        x_flat = x.reshape(n_tok, hidden)
        topk_vals, topk_idx = jax.lax.top_k(weights_flat, TOP_K)
        rows = jnp.arange(n_tok)[:, None]
        topk_flat = jnp.zeros_like(weights_flat).at[rows, topk_idx].set(topk_vals)
        routing_mask = (topk_flat > 0).astype(jnp.int32)
        noop_w = topk_flat[:, -1]
        noop_mask = routing_mask[:, -1].astype(x.dtype)
        expert_w = topk_flat[:, :-1]
        expert_mask = routing_mask[:, :-1]
        sorted_indices = jnp.argsort(-expert_mask, axis=0)[:cap]
        sorted_mask = jnp.take_along_axis(expert_mask, sorted_indices, axis=0)
        used_idx = (sorted_indices * sorted_mask).reshape(-1)
        inputs = x_flat[used_idx] * sorted_mask.reshape(-1).astype(x.dtype)[:, None]
        inputs = inputs.reshape(cap, n_exp - 1, hidden)
        in_w = jnp.take_along_axis(expert_w, sorted_indices, axis=0)
        h = jax.nn.relu(jnp.einsum('ceh,ehi->cei', inputs, experts_inter))
        out = jnp.einsum('cei,eih->ceh', h, experts_out) * in_w[..., None]
        combined = jnp.zeros_like(x_flat).at[used_idx].add(out.reshape(-1, hidden))
        combined = combined + x_flat * (noop_w * noop_mask)[:, None]
        return combined.reshape(batch, seq, hidden)
    x = x + _L0_attn_ref(_layernorm(x, axis=-1), L0_attn_Wq, L0_attn_Wkv_down, L0_attn_Wk_up, L0_attn_Wv_up, L0_attn_Wout)
    x = x + _L0_xattn_ref(_layernorm(x, axis=-1), ctx_512, L0_xattn_Wk, L0_xattn_bk, L0_xattn_Wq, L0_xattn_bq, L0_xattn_Wv, L0_xattn_bv, L0_xattn_Wck, L0_xattn_bck, L0_xattn_Wcq, L0_xattn_bcq, L0_xattn_Wcv, L0_xattn_bcv, L0_xattn_Wp, L0_xattn_bp)
    x = x + _L0_ffn_ref(_layernorm(x, axis=-1), L0_ffn_router_w, L0_ffn_router_b, L0_ffn_experts_inter, L0_ffn_experts_out)
    return x

_drawn_inputs = setup_inputs


def setup_inputs(seed=0):
    import zlib

    import numpy as np

    out = dict(_drawn_inputs(seed))
    spreads = {'L0_xattn_bk': (0.0, 0.8),
     'L0_xattn_bq': (0.0, 0.277),
     'L0_xattn_bv': (0.0, 0.1),
     'L0_xattn_bck': (0.0, 0.8),
     'L0_xattn_bcq': (0.0, 0.1),
     'L0_xattn_bcv': (0.0, 0.1),
     'L0_xattn_bp': (0.0, 0.1),
     'L0_ffn_router_b': (0.0, 0.1)}
    factors = {}
    for name, (base, spread) in spreads.items():
        noise = np.random.default_rng([zlib.crc32(name.encode()), seed]).standard_normal(out[name].shape)
        drawn = base * np.exp(spread * noise) if base else spread * noise
        out[name] = jnp.asarray(drawn.astype(out[name].dtype))
    for name, factor in factors.items():
        out[name] = (out[name] * factor).astype(out[name].dtype)
    return out
```

```python
from contextlib import ExitStack

import concourse.bass as bass
from concourse import mybir

F32 = mybir.dt.float32
F32R = mybir.dt.float32r
BF16 = mybir.dt.bfloat16
I32 = mybir.dt.int32
U32 = mybir.dt.uint32
ALU = mybir.AluOpType
ACT = mybir.ActivationFunctionType
AX = mybir.AxisListType

P = 128
B, S, D = 8, 512, 256
DC = D // P
TT = S // P
H0, HD, LD = 16, 64, 64
PAIRS = H0 // 2
H1, HW = 16, 16
QUADS = H1 // 4
SC, CW = 1601, 128
SCP = SC + 1
CT = -(-SC // P)
LAST = SC - (CT - 1) * P
CH = TT + CT
NE, NX, FI = 8, 7, 1024
FC = FI // P
CAP = (B * S) // NE
SLOTS = NX * CAP
ROW = D + 4
FAR = 65536
MASKED = -1e30
EPS = 1e-5
RSQRT_SEED = 0x5F3759DF
KCOLS = [(0, 400), (400, 400), (800, 400), (1200, 402)]


class Resources:
    def __init__(self, nc, ctx):
        self.nc, self.ctx = nc, ctx

    def sb(self, name, shape, dt):
        return self.ctx.enter_context(self.nc.sbuf_tensor(name, shape, dt))

    def ps(self, name, shape, dt=F32):
        return self.ctx.enter_context(self.nc.psum_tensor(name, shape, dt))

    def sem(self, name):
        return self.ctx.enter_context(self.nc.semaphore(name))


class Chain:

    def __init__(self, engine, sem, first, passed=None):
        self.engine, self.sem, self.first, self.n, self.passed = engine, sem, first, 0, passed

    def link(self, ins, apart=False):
        self.n += 1
        ins.then_inc(self.sem, 1)
        self.engine.wait_ge(self.sem, self.first + self.n)
        if apart:
            self.engine.sem_inc(self.passed, 1)


LN_LINKS = 14


def layer_norm(nc, chain, x, xn, w):
    n0 = chain.n
    link = chain.link
    for t in range(TT):
        last = nc.vector.bn_stats(w["stats"][:, t, :], x[:, t, :])
    link(last, apart=True)
    for t in range(TT):
        last = nc.vector.bn_aggr(w["mv"][:, t, :], w["stats"][:, t, :])
    link(last)
    var, y, a = w["var"][:, :], w["rstd"][:, :], w["newton"][:, :]
    link(nc.vector.tensor_scalar_add(var, w["mv"][:, :, 1], EPS))
    link(nc.vector.tensor_scalar(a.bitcast(I32), var.bitcast(I32), 1, None, ALU.logical_shift_right))
    link(nc.vector.tensor_scalar(y.bitcast(I32), a.bitcast(I32), -1.0, float(RSQRT_SEED), ALU.mult, ALU.add))
    for _ in range(3):
        link(nc.vector.scalar_tensor_tensor(out=a, in0=y, scalar=-0.5, in1=y, op0=ALU.mult, op1=ALU.mult))
        link(nc.vector.tensor_tensor(a, a, var, ALU.mult))
        link(nc.vector.scalar_tensor_tensor(out=y, in0=a, scalar=1.5, in1=y, op0=ALU.add, op1=ALU.mult))
    for t in range(TT):
        last = nc.vector.tensor_scalar(xn[:, t, :], x[:, t, :], w["mv"][:, t, 0:1], w["rstd"][:, t:t + 1],
                                       ALU.subtract, ALU.mult)
    assert chain.n - n0 == LN_LINKS
    return last


def ln_work(r, tag):
    return {"stats": r.sb(f"stats_{tag}", [P, TT, 6], F32), "mv": r.sb(f"mv_{tag}", [P, TT, 2], F32),
            "var": r.sb(f"var_{tag}", [P, TT], F32), "rstd": r.sb(f"rstd_{tag}", [P, TT], F32),
            "newton": r.sb(f"newton_{tag}", [P, TT], F32)}


def transpose_tokens(nc, xn, ident, pT):
    for d in range(DC):
        for t in range(TT):
            last = nc.tensor.transpose(pT[:, d, t * P:(t + 1) * P], xn[:, t, d * P:(d + 1) * P], ident[:, :])
    return last


def prepare(nc, g, i):
    with ExitStack() as ctx:
        r = Resources(nc, ctx)
        wq = r.sb("p_wq", [P, DC, H0 * HD], F32)
        wk = r.sb("p_wk", [LD, H0 * HD], F32)
        wv = r.sb("p_wv", [LD, H0 * HD], F32)
        wo = r.sb("p_wo", [P, PAIRS, D], F32)
        wqT = r.sb("p_wqT", [P, PAIRS, D], F32)
        wkB = r.sb("p_wkB", [P, PAIRS, P], F32)
        wvB = r.sb("p_wvB", [P, PAIRS, P], F32)
        rw = r.sb("p_rw", [NE, D], F32)
        none_tok = r.sb("p_none_tok", [P, SLOTS // P, 1], I32)
        empty = r.sb("p_empty", [P, SLOTS // P, ROW], F32)
        pA = r.ps("p_pA", [P, 4, 512])
        pB = r.ps("p_pB", [P, 4, 512])
        in_wq, in_up, in_wo, in_x, in_rw = (r.sem(n) for n in ("in_wq", "in_up", "in_wo", "in_x", "in_rw"))
        id_set, const_set, zero_set, empty_set = (r.sem(n) for n in ("id_set", "const_set", "zero_set", "empty_set"))
        empty_out = r.sem("empty_out")
        wqT_tr, wqT_done, up_tr, up_done, rw_tr, rw_done = (r.sem(n) for n in (
            "wqT_tr", "wqT_done", "up_tr", "up_done", "rw_tr", "rw_done"))
        wt_mm, wt_done, wvo_mm, wvo_done = (r.sem(n) for n in ("wt_mm", "wt_done", "wvo_mm", "wvo_done"))
        block = ctx.enter_context(nc.Block())

        @block.sync
        def _(sp):
            sp.dma_start(wq[:, :, :], i["Wq"].rearrange("(c p) h k -> p c (h k)", p=P)).then_inc(in_wq, 16)
            sp.dma_start(wk[:, :], i["Wk_up"].rearrange("c h k -> c (h k)")).then_inc(in_up, 16)
            sp.dma_start(wv[:, :], i["Wv_up"].rearrange("c h k -> c (h k)")).then_inc(in_up, 16)
            sp.dma_start(rw[:, :], i["router_w"]).then_inc(in_rw, 16)
            sp.dma_start(wo[:, :, :], i["Wout"].rearrange("(g a) k o -> (a k) g o", a=2)).then_inc(in_wo, 16)
            for half in range(2):
                sp.dma_start(g["wdd"][:, :, half, :], i["Wkv_down"].rearrange("(c p) n -> p c n", p=P)).then_inc(in_x, 16)
            for name in ("xWq", "xWk", "xWcq", "xWv"):
                sp.dma_start(g[name][:, :, :], i[name].rearrange("(c p) n -> p c n", p=P)).then_inc(in_x, 16)
            for name in ("xWck", "xWcv"):
                sp.dma_start(g[name][:, :], i[name]).then_inc(in_x, 16)
            for n, name in enumerate(("xbq", "xbk", "xbcq", "xbck")):
                sp.dma_start(g["bias_col"][:, n, :], i[name].rearrange("(c p) -> p c", p=P),
                             allow_slow_non_contiguous=True).then_inc(in_x, 16)
            for n, name in enumerate(("xbv", "xbcv", "xbp")):
                sp.dma_start(g["bias_row"][:, n, :], i[name].partition_broadcast(P)).then_inc(in_x, 16)
            sp.dma_start(g["router_bias"][:, :], i["router_b"].partition_broadcast(P)).then_inc(in_x, 16)
            sp.wait_ge(zero_set, 1)
            for n in range(4):
                sp.dma_start(g["wp"][32 * n:32 * n + HW, :, :],
                             i["xWp"].rearrange("(q n r) o -> n r q o", n=4, r=HW)[n]).then_inc(in_x, 16)
            sp.wait_ge(empty_set, 2)
            sp.dma_start(g["slot_rows"].rearrange("(p n) c -> p n c", p=P), empty[:, :, :]).then_inc(empty_out, 16)
            sp.dma_start(g["acc"][B * S:B * S + SLOTS].rearrange("(p n) c -> p n c", p=P), empty[:, :, 0:D]).then_inc(empty_out, 16)
            sp.wait_ge(in_x, 16 * 20)
            sp.wait_ge(empty_out, 32)

        @block.gpsimd
        def _(pool):
            nc.gpsimd.memset(g["ident"][:, :], 0.0).then_inc(id_set, 1)
            nc.gpsimd.memset(g["identb"][:, :], 0.0).then_inc(id_set, 1)
            nc.gpsimd.memset(g["mask_t"][:, :], 0.0).then_inc(id_set, 1)
            nc.gpsimd.memset(g["mask_n"][:, :], 0.0).then_inc(id_set, 1)
            nc.gpsimd.memset(g["before"][:, :], 1.0).then_inc(id_set, 1)
            pool.wait_ge(id_set, 5)
            for m in ("ident", "identb"):
                nc.gpsimd.affine_select(out=g[m][:, :], in_=g[m][:, :], compare_op=ALU.not_equal, fill=1.0, base=0,
                                        pattern=[[-1, P]], channel_multiplier=1).then_inc(const_set, 1)
            nc.gpsimd.affine_select(out=g["mask_t"][:, :], in_=g["mask_t"][:, :], compare_op=ALU.is_ge, fill=MASKED,
                                    base=0, pattern=[[1, P]], channel_multiplier=-1).then_inc(const_set, 1)
            nc.gpsimd.affine_select(out=g["mask_n"][:, :], in_=g["mask_n"][:, :], compare_op=ALU.is_ge, fill=MASKED,
                                    base=0, pattern=[[-1, P]], channel_multiplier=1).then_inc(const_set, 1)
            nc.gpsimd.affine_select(out=g["before"][:, :], in_=g["before"][:, :], compare_op=ALU.is_gt, fill=0.0,
                                    base=0, pattern=[[1, P]], channel_multiplier=-1).then_inc(const_set, 1)
            nc.gpsimd.iota(g["tok"][:, :], pattern=[[P, TT]], base=0, channel_multiplier=1).then_inc(const_set, 1)
            nc.gpsimd.iota(g["slot0"][:, :, :], pattern=[[0, TT], [CAP, NE]], base=-FAR, channel_multiplier=0).then_inc(const_set, 1)
            nc.gpsimd.iota(g["prio"][:, :, :], pattern=[[0, TT], [-1, NE]], base=NE, channel_multiplier=0).then_inc(const_set, 1)
            nc.gpsimd.iota(none_tok[:, :, :], pattern=[[1, SLOTS // P], [0, 1]], base=B * S,
                           channel_multiplier=SLOTS // P).then_inc(const_set, 1)
            pool.wait_ge(const_set, 9)

        @block.vector
        def _(dve):
            nc.vector.memset(g["wp"][:, :, :], 0.0).then_inc(zero_set, 1)
            nc.vector.memset(empty[:, :, :], 0.0).then_inc(empty_set, 1)
            dve.wait_ge(empty_set, 1)
            dve.wait_ge(const_set, 9)
            nc.vector.tensor_copy(empty[:, :, D + 1:D + 2].bitcast(I32), none_tok[:, :, :]).then_inc(empty_set, 1)
            nc.vector.memset(wkB[:, :, :], 0.0)
            nc.vector.memset(wvB[:, :, :], 0.0).then_inc(zero_set, 1)
            nc.vector.memset(g["ones"][:, :], 1.0)
            nc.vector.memset(g["onesb"][:, :], 1.0).then_inc(zero_set, 1)
            for n in range(4):
                dve.wait_ge(wqT_tr, n + 1)
                nc.vector.tensor_copy(wqT[:, 2 * n:2 * n + 2, :], pA[:, n, :].rearrange("p (a b) -> p a b", a=2)).then_inc(wqT_done, 1)
            dve.wait_ge(zero_set, 2)
            for n, dst in enumerate((wkB, wvB)):
                dve.wait_ge(up_tr, n + 1)
                for a in range(2):
                    last = nc.vector.tensor_copy(dst[a * HD:(a + 1) * HD, :, a * LD:(a + 1) * LD],
                                                 pB[a * HD:(a + 1) * HD, n, :].rearrange("p (g c) -> p g c", g=PAIRS))
                last.then_inc(up_done, 1)
            dve.wait_ge(rw_tr, 1)
            nc.vector.tensor_copy(g["rwT"][:, :, :], pB[:, 2, 0:DC * NE].rearrange("p (c e) -> p c e", c=DC)).then_inc(rw_done, 1)
            for n in range(4):
                dve.wait_ge(wt_mm, n + 1)
                nc.vector.tensor_copy(g["wt"][:, n // 2, (n % 2) * 512:(n % 2) * 512 + 512], pA[:, n, :]).then_inc(wt_done, 1)
            for n in range(4):
                dve.wait_ge(wvo_mm, n + 1)
                nc.vector.tensor_copy(g["wvo"][:, 2 * n:2 * n + 2, :], pB[:, n, :].rearrange("p (a b) -> p a b", a=2)).then_inc(wvo_done, 1)
            dve.wait_ge(wvo_done, 4)

        @block.tensor
        def _(pe):
            pe.wait_ge(const_set, 2)
            pe.wait_ge(in_wq, 16)
            for n in range(4):
                for a in range(2):
                    for c in range(DC):
                        last = nc.tensor.transpose(pA[:, n, a * D + c * P:a * D + (c + 1) * P],
                                                   wq[:, c, (2 * n + a) * P:(2 * n + a + 1) * P], g["ident"][:, :])
                last.then_inc(wqT_tr, 1)
            pe.wait_ge(in_up, 32)
            for n, w in enumerate((wk, wv)):
                for q in range(PAIRS):
                    last = nc.tensor.transpose(pB[:, n, q * LD:(q + 1) * LD], w[:, q * P:(q + 1) * P], g["ident"][0:LD, 0:LD])
                last.then_inc(up_tr, 1)
            pe.wait_ge(in_rw, 16)
            for c in range(DC):
                last = nc.tensor.transpose(pB[:, 2, c * NE:(c + 1) * NE], rw[:, c * P:(c + 1) * P], g["ident"][0:NE, 0:NE])
            last.then_inc(rw_tr, 1)
            pe.wait_ge(wqT_done, 4)
            pe.wait_ge(up_done, 2)
            for n in range(4):
                for q in range(4):
                    pair = (n % 2) * 4 + q
                    last = nc.tensor.matmul(pA[:, n, q * P:(q + 1) * P], wqT[:, pair, (n // 2) * P:(n // 2 + 1) * P],
                                            wkB[:, pair, :], start=True, stop=True)
                last.then_inc(wt_mm, 1)
            pe.wait_ge(in_wo, 16)
            pe.wait_ge(rw_done, 1)
            for n in range(4):
                for a in range(2):
                    last = nc.tensor.matmul(pB[:, n, a * D:(a + 1) * D], wvB[:, 2 * n + a, :], wo[:, 2 * n + a, :],
                                            start=True, stop=True)
                last.then_inc(wvo_mm, 1)


def latent_stage(nc, g, i):
    with ExitStack() as ctx:
        r = Resources(nc, ctx)
        x = r.sb("a_x", [P, TT, D], F32)
        xn = r.sb("a_xn", [P, TT, D], F32)
        xnT = r.sb("a_xnT", [P, DC, S], F32)
        w = ln_work(r, "a")
        qh = r.sb("a_qh", [P, PAIRS, S], F32R)
        ql = r.sb("a_ql", [P, PAIRS, S], F32R)
        lh = r.sb("a_lh", [P, S], F32R)
        ll = r.sb("a_ll", [LD, S], F32R)
        v = r.sb("a_v", [P, TT, LD], F32)
        pT = r.ps("a_pT", [P, DC, S])
        pL = r.ps("a_pL", [P, S])
        pV = r.ps("a_pV", [P, TT, LD])
        pQ = r.ps("a_pQ", [P, 4, S])
        x_in, chain_s, xn_ready, tr_done, xnT_ready = (r.sem(n) for n in ("a_x_in", "a_chain", "a_xn_ready", "a_tr_done", "a_xnT_ready"))
        lat_done, v_done, q_done, high, low, v_ready = (r.sem(n) for n in ("a_lat_done", "a_v_done", "a_q_done", "a_high", "a_low", "a_v_ready"))
        stored, passed = r.sem("a_stored"), r.sem("a_passed")
        block = ctx.enter_context(nc.Block())
        JOBS = PAIRS + 1
        STORES = 5

        @block.sync
        def _(sp):
            with sp.Fori(0, B) as b:
                sp.wait_ge(xn_ready, b)
                sp.dma_start(x[:, :, :], i["x"][b].rearrange("(t p) d -> p t d", p=P)).then_inc(x_in, 16)

        @block.vector
        def _(dve):
            with dve.Fori(0, B) as b:
                chain = Chain(dve, chain_s, b * LN_LINKS, passed)
                dve.wait_ge(x_in, b * 16 + 16)
                dve.wait_ge(tr_done, b)
                layer_norm(nc, chain, x, xn, w).then_inc(xn_ready, 1)
                dve.wait_ge(stored, b * 16 * STORES)
                dve.wait_ge(high, b * JOBS + 1)
                nc.vector.tensor_tensor(ll[:, :], pL[0:LD, :], lh[0:LD, :].bitcast(F32), ALU.subtract).then_inc(low, 1)
                dve.wait_ge(v_done, b + 1)
                nc.vector.tensor_copy(v[:, :, :], pV[:, :, :]).then_inc(v_ready, 1)
                for q in range(PAIRS):
                    dve.wait_ge(high, b * JOBS + q + 2)
                    nc.vector.tensor_tensor(ql[:, q, :], pQ[:, q % 4, :], qh[:, q, :].bitcast(F32), ALU.subtract).then_inc(low, 1)

        @block.scalar
        def _(act):
            with act.Fori(0, B) as b:
                act.wait_ge(tr_done, b + 1)
                act.wait_ge(q_done, b * PAIRS)
                for d in range(DC):
                    nc.scalar.activation(xnT[:, d, :], pT[:, d, :], ACT.Copy).then_inc(xnT_ready, 1)
                act.wait_ge(stored, b * 16 * STORES)
                act.wait_ge(lat_done, b + 1)
                nc.scalar.activation(lh[:, :], pL[:, :], ACT.Copy).then_inc(high, 1)
                for q in range(PAIRS):
                    act.wait_ge(q_done, b * PAIRS + q + 1)
                    nc.scalar.activation(qh[:, q, :], pQ[:, q % 4, :], ACT.Copy).then_inc(high, 1)

        @block.tensor
        def _(pe):
            with pe.Fori(0, B) as b:
                pe.wait_ge(xn_ready, b + 1)
                pe.wait_ge(xnT_ready, b * DC)
                transpose_tokens(nc, xn, g["ident"], pT).then_inc(tr_done, 1)
                pe.wait_ge(xnT_ready, b * DC + DC)
                pe.wait_ge(low, b * JOBS)
                for d in range(DC):
                    last = nc.tensor.matmul(pL[:, :], g["wdd"][:, d, :, :], xnT[:, d, :], start=d == 0, stop=d == DC - 1)
                last.then_inc(lat_done, 1)
                pe.wait_ge(v_ready, b)
                for t in range(TT):
                    for d in range(DC):
                        last = nc.tensor.matmul(pV[:, t, :], xnT[:, d, t * P:(t + 1) * P], g["wdd"][:, d, 0, :],
                                                start=d == 0, stop=d == DC - 1)
                last.then_inc(v_done, 1)
                for q in range(PAIRS):
                    if q >= 4:
                        pe.wait_ge(low, b * JOBS + q - 2)
                    for d in range(DC):
                        last = nc.tensor.matmul(pQ[:, q % 4, :], g["wt"][:, d, q * P:(q + 1) * P], xnT[:, d, :],
                                                start=d == 0, stop=d == DC - 1)
                    last.then_inc(q_done, 1)

        @block.gpsimd
        def _(pool):
            with pool.Fori(0, B) as b:
                pool.wait_ge(v_ready, b + 1)
                pool.dma_start(g["lat_h"][b], lh[:, :].bitcast(F32)).then_inc(stored, 16)
                pool.dma_start(g["lat_l"][b], ll[:, :].bitcast(F32)).then_inc(stored, 16)
                pool.dma_start(g["lat_v"][b], v[:, :, :]).then_inc(stored, 16)
                pool.wait_ge(low, b * JOBS + JOBS)
                pool.dma_start(g["q0h"][bass.ds(b * PAIRS, PAIRS)].rearrange("q p n -> p q n"), qh[:, :, :].bitcast(F32)).then_inc(stored, 16)
                pool.dma_start(g["q0l"][bass.ds(b * PAIRS, PAIRS)].rearrange("q p n -> p q n"), ql[:, :, :].bitcast(F32)).then_inc(stored, 16)
            pool.wait_ge(stored, B * 16 * STORES)


def latent_attention(nc, g):
    with ExitStack() as ctx:
        r = Resources(nc, ctx)
        K = 4
        q1 = [r.sb(f"b_q1_{k}", [P, 2, S], F32R) for k in range(K)]
        q2 = [r.sb(f"b_q2_{k}", [LD + 1, 2, S], F32R) for k in range(K)]
        k1 = [r.sb(f"b_k1_{k}", [P, S], F32R) for k in range(K)]
        k2 = [r.sb(f"b_k2_{k}", [LD + 1, S], F32R) for k in range(K)]
        v = [r.sb(f"b_v_{k}", [P, TT, LD], F32) for k in range(K)]
        negm = [r.sb(f"b_negm_{k}", [P, 2 * TT], F32) for k in range(K)]
        mT = [r.sb(f"b_mT_{k}", [2 * TT, P], F32R) for k in range(K)]
        z = [r.sb(f"b_z_{k}", [P, S], F32) for k in range(K)]
        prob = r.sb("b_prob", [P, TT, 2, S], F32)
        rec = [r.sb(f"b_rec_{k}", [P, S], F32) for k in range(2)]
        pM = r.ps("b_pM", [P, 2, S])
        pS = r.ps("b_pS", [P, 2, 2, S])
        pY = r.ps("b_pY", [P, 2, S])
        loaded, row_in, stored = ([r.sem(f"b_{n}_{k}") for k in range(K)] for n in ("loaded", "row_in", "stored"))
        ones_set, max_mm, max_red, mT_ready = (r.sem(n) for n in ("b_ones_set", "b_max_mm", "b_max_red", "b_mT_ready"))
        st_done, exp_done, pv_done, rec_done, z_ready = (r.sem(n) for n in ("b_st_done", "b_exp_done", "b_pv_done", "b_rec_done", "b_z_ready"))
        block = ctx.enter_context(nc.Block())
        STEPS = B * PAIRS
        MJ = 2 * TT + 1
        LOADS = 6

        def steps(engine, body):
            with engine.Fori(0, STEPS // K - 1) as m:
                for k in range(K):
                    body(m * K + k, k, K)
            for k in range(K):
                body(STEPS - K + k, k, K - 1 - k)

        @block.sync
        def _(sp):
            def load(it, k):
                for src, dst in ((g["q0h"], q1[k][0:LD]), (g["q0l"], q1[k][LD:P]), (g["q0h"], q2[k][0:LD])):
                    sp.dma_start(dst.bitcast(F32), src[it].rearrange("(a d) n -> d a n", a=2)).then_inc(loaded[k], 16)
                sp.dma_start(k1[k][:, :].bitcast(F32), g["lat_h"][it // PAIRS]).then_inc(loaded[k], 16)
                sp.dma_start(k2[k][0:LD, :].bitcast(F32), g["lat_l"][it // PAIRS]).then_inc(loaded[k], 16)
                sp.dma_start(v[k][:, :, :], g["lat_v"][it // PAIRS]).then_inc(loaded[k], 16)

            def row(it, k):
                sp.wait_ge(mT_ready, it + 1)
                sp.dma_start(q2[k][LD:LD + 1, :, :].bitcast(F32), mT[k][:, :].bitcast(F32)).then_inc(row_in[k], 16)

            sp.wait_ge(ones_set, 1)
            for n in range(3):
                load(n, n)
            row(0, 0)

            def body(it, k, follow):
                if follow >= 3:
                    sp.wait_ge(pv_done, it * TT)
                    load(it + 3, (k + 3) % K)
                if follow >= 1:
                    row(it + 1, (k + 1) % K)

            steps(sp, body)

        @block.gpsimd
        def _(pool):
            def body(it, k, follow):
                pool.wait_ge(z_ready, it + 1)
                pool.dma_start(g["z0"][it], z[k][:, :]).then_inc(stored[k], 16)

            steps(pool, body)
            for k in range(K):
                pool.wait_ge(stored[k], 16 * STEPS // K)

        @block.vector
        def _(dve):
            for k in range(K):
                last = nc.vector.memset(k2[k][LD:LD + 1, :].bitcast(F32), 1.0)
            last.then_inc(ones_set, 1)

            def maxima(it, k):
                for j in range(2 * TT):
                    w = P * (j % TT + 1)
                    slot = (k * MJ + j) % 2
                    dve.wait_ge(max_mm, it * MJ + j + 1)
                    nc.vector.tensor_reduce(negm[k][:, j:j + 1], pM[:, slot, 0:w], AX.X, ALU.max, negate=True).then_inc(max_red, 1)
                dve.wait_ge(max_mm, it * MJ + MJ)
                slot = (k * MJ + 2 * TT) % 2
                nc.vector.tensor_copy(mT[k][:, :], pM[0:2 * TT, slot, 0:P]).then_inc(mT_ready, 1)

            maxima(0, 0)

            def body(it, k, follow):
                if follow >= 1:
                    maxima(it + 1, (k + 1) % K)
                dve.wait_ge(pv_done, it * TT + TT)
                nc.vector.reciprocal(rec[k % 2][:, :], pY[:, 1, :]).then_inc(rec_done, 1)
                dve.wait_ge(rec_done, it + 1)
                dve.wait_ge(stored[k], (it // K) * 16)
                nc.vector.tensor_tensor(z[k][:, :], pY[:, 0, :], rec[k % 2][:, :], ALU.mult).then_inc(z_ready, 1)

            steps(dve, body)

        @block.scalar
        def _(act):
            def body(it, k, follow):
                for j in range(TT):
                    act.wait_ge(st_done, it * TT + j + 1)
                    nc.scalar.activation(prob[:, j, :, P * j:S], pS[:, j % 2, :, P * j:S], ACT.Exp, scale=HD ** -0.5).then_inc(exp_done, 1)

            steps(act, body)

        @block.tensor
        def _(pe):
            def max_job(it, k, j):
                slot = (k * MJ + j) % 2
                if j == 0:
                    pe.wait_ge(loaded[k], (it // K) * (16 * LOADS) + 16 * LOADS)
                if not (isinstance(it, int) and it == 0 and j < 2):
                    if j >= 2:
                        pe.wait_ge(max_red, it * (MJ - 1) + j - 1)
                    elif j == 1:
                        pe.wait_ge(mT_ready, it)
                    else:
                        pe.wait_ge(max_red, it * (MJ - 1))
                if j < 2 * TT:
                    h, t = j // TT, j % TT
                    nc.tensor.matmul(pM[:, slot, 0:P * (t + 1)], q1[k][:, h, t * P:(t + 1) * P], k1[k][:, 0:P * (t + 1)],
                                     start=True, stop=False)
                    nc.tensor.matmul(pM[:, slot, P * t:P * (t + 1)], g["identb"][:, :], g["mask_n"][:, :],
                                     start=False, stop=True).then_inc(max_mm, 1)
                else:
                    pe.wait_ge(max_red, it * (MJ - 1) + MJ - 1)
                    nc.tensor.transpose(pM[0:2 * TT, slot, 0:P], negm[k][:, :], g["ident"][:, :]).then_inc(max_mm, 1)

            for j in range(MJ):
                max_job(0, 0, j)

            def scores(it, k, j):
                if j == 0:
                    pe.wait_ge(row_in[k], (it // K) * 16 + 16)
                if j >= 2:
                    pe.wait_ge(exp_done, it * TT + j - 1)
                for h in range(2):
                    out = pS[:, j % 2, h, P * j:S]
                    nc.tensor.matmul(out, k1[k][:, P * j:P * (j + 1)], q1[k][:, h, P * j:S], start=True, stop=False)
                    nc.tensor.matmul(out, k2[k][:, P * j:P * (j + 1)], q2[k][:, h, P * j:S], start=False, stop=False)
                    last = nc.tensor.matmul(pS[:, j % 2, h, P * j:P * (j + 1)], g["identb"][:, :], g["mask_t"][:, :],
                                            start=False, stop=True)
                last.then_inc(st_done, 1)

            def values(it, k, j):
                pe.wait_ge(exp_done, it * TT + j + 1)
                if j == 0:
                    pe.wait_ge(z_ready, it)
                for n, w in enumerate((v[k][:, j, :], g["ones"][:, 0:LD])):
                    for h in range(2):
                        last = nc.tensor.matmul(pY[h * LD:(h + 1) * LD, n, P * j:S], w, prob[:, j, h, P * j:S],
                                                start=j == 0, stop=j == TT - 1)
                last.then_inc(pv_done, 1)

            def body(it, k, follow):
                jobs = list(range(MJ)) if follow >= 1 else []

                def some(n):
                    for _ in range(min(n, len(jobs))):
                        max_job(it + 1, (k + 1) % K, jobs.pop(0))

                scores(it, k, 0)
                some(2)
                scores(it, k, 1)
                some(2)
                values(it, k, 0)
                some(2)
                scores(it, k, 2)
                values(it, k, 1)
                some(2)
                scores(it, k, 3)
                values(it, k, 2)
                some(1)
                values(it, k, 3)

            steps(pe, body)


def cross_stage(nc, g, i):
    with ExitStack() as ctx:
        r = Resources(nc, ctx)
        z = r.sb("c_z", [P, PAIRS, S], F32)
        x = r.sb("c_x", [P, TT, D], F32)
        xn = r.sb("c_xn", [P, TT, D], F32)
        xnT = r.sb("c_xnT", [P, DC, S], F32)
        c = r.sb("c_ctx", [P, CT, CW], F32)
        cT = r.sb("c_ctxT", [P, SC], F32)
        w = ln_work(r, "c")
        sh = r.sb("c_sh", [P, 3, DC, S], F32R)
        sl = r.sb("c_sl", [P, 3, DC, S], F32R)
        ch = r.sb("c_ch", [P, DC, SCP], F32R)
        cl = r.sb("c_cl", [P, DC, SCP], F32R)
        vx = r.sb("c_vx", [P, CH, H1, 2 * HW], F32)
        pO = r.ps("c_pO", [P, TT, D])
        pT = r.ps("c_pT", [P, DC, S])
        pJ = r.ps("c_pJ", [P, 4, 512])
        z_in, x_in, c_in, chain_s, ones_set = (r.sem(n) for n in ("c_z_in", "c_x_in", "c_c_in", "c_chain", "c_ones_set"))
        o_done, xn_ready, tr_done, xnT_ready = (r.sem(n) for n in ("c_o_done", "c_xn_ready", "c_tr_done", "c_xnT_ready"))
        job_done, high, low, vals, ctr = (r.sem(n) for n in ("c_job_done", "c_high", "c_low", "c_vals", "c_ctr"))
        stored, passed = r.sem("c_stored"), r.sem("c_passed")
        block = ctx.enter_context(nc.Block())

        jobs = [("ctx", n) for n in range(-(-CT // 4))]
        jobs += [("key", m, n) for m in range(DC) for n in range(4)]
        jobs += [("cval", n) for n in range(-(-CT // 2))]
        jobs += [("split", t, m) for t in range(3) for m in range(DC)]
        jobs += [("val", n) for n in range(TT // 2)]
        NJ = len(jobs)
        kinds = {"ctx": ("ctx",), "split": ("key", "split"), "value": ("cval", "val")}

        def count(kind, upto):
            return sum(1 for q in jobs[:upto] if q[0] in kinds[kind])

        NCTX, NSPL, NVAL = (count(n, NJ) for n in ("ctx", "split", "value"))
        NCOL = [(0, 400), (400, 400), (800, 400), (1200, 401)]
        STORES = 6 + 4 + 8

        def freed(engine, b, n):
            kind = jobs[n][0]
            if kind == "ctx":
                engine.wait_ge(ctr, b * NCTX + count("ctx", n + 1))
            elif kind in ("key", "split"):
                engine.wait_ge(low, b * NSPL + count("split", n + 1))
            else:
                engine.wait_ge(vals, b * NVAL + count("value", n + 1))

        @block.sync
        def _(sp):
            with sp.Fori(0, B) as b:
                sp.wait_ge(ctr, b * NCTX)
                sp.dma_start(c[:, 0:CT - 1, :], i["ctx"][b, 0:(CT - 1) * P].rearrange("(t p) d -> p t d", p=P)).then_inc(c_in, 16)
                sp.dma_start(c[0:LAST, CT - 1, :], i["ctx"][b, (CT - 1) * P:SC]).then_inc(c_in, 16)
                sp.wait_ge(o_done, b)
                sp.dma_start(z[:, :, :], g["z0"][bass.ds(b * PAIRS, PAIRS)].rearrange("q p n -> p q n")).then_inc(z_in, 16)
                sp.wait_ge(xn_ready, b)
                sp.dma_start(x[:, :, :], i["x"][b].rearrange("(t p) d -> p t d", p=P)).then_inc(x_in, 16)

        @block.gpsimd
        def _(pool):
            nc.gpsimd.memset(vx[:, :, :, HW:2 * HW], 1.0).then_inc(ones_set, 1)
            with pool.Fori(0, B) as b:
                pool.wait_ge(low, b * NSPL + NSPL)
                pool.wait_ge(high, b * NSPL + NSPL)
                pool.wait_ge(vals, b * NVAL + NVAL)
                pool.wait_ge(ones_set, 1)
                for t in range(3):
                    for src, dst in ((sh, g["s1h"]), (sl, g["s1l"])):
                        pool.dma_start(dst[t, bass.ds(b * QUADS, QUADS)].rearrange("(m a) r n -> (a r) m n", a=2),
                                       src[:, t, :, :].bitcast(F32)).then_inc(stored, 16)
                for src, dst in ((ch, g["c1h"]), (cl, g["c1l"])):
                    view = dst[bass.ds(b * QUADS, QUADS)].rearrange("(m a) r n -> (a r) m n", a=2)
                    pool.dma_start(view[:, :, 0:SC], src[:, :, 0:SC].bitcast(F32)).then_inc(stored, 16)
                    pool.dma_start(view[:, :, SC:SCP], src[:, :, SC - 1:SC].bitcast(F32), allow_slow_non_contiguous=True).then_inc(stored, 16)
                for q in range(QUADS):
                    pool.dma_start(g["v1"][b * QUADS + q].rearrange("p c (h n) -> p c h n", h=4)[:, 0:CH - 1],
                                   vx[:, 0:CH - 1, 4 * q:4 * q + 4, :]).then_inc(stored, 16)
                    pool.dma_start(g["v1"][b * QUADS + q][0:LAST, CH - 1].rearrange("p (h n) -> p h n", h=4),
                                   vx[0:LAST, CH - 1, 4 * q:4 * q + 4, :]).then_inc(stored, 16)
            pool.wait_ge(stored, B * 16 * STORES)

        @block.scalar
        def _(act):
            with act.Fori(0, B) as b:
                for n, job in enumerate(jobs):
                    if job[0] == "ctx":
                        if n == 0:
                            act.wait_ge(job_done, b * NJ)
                        act.wait_ge(job_done, b * NJ + n + 1)
                        lo, hi = job[1] * 512, min(SC, job[1] * 512 + 512)
                        nc.scalar.activation(cT[:, lo:hi], pJ[:, n % 4, 0:hi - lo], ACT.Copy).then_inc(ctr, 1)
                    if n == 4:
                        act.wait_ge(stored, b * 16 * STORES)
                    if job == ("split", 0, 0):
                        act.wait_ge(tr_done, b + 1)
                        for d in range(DC):
                            nc.scalar.activation(xnT[:, d, :], pT[:, d, :], ACT.Copy).then_inc(xnT_ready, 1)
                    if job[0] in ("key", "split"):
                        act.wait_ge(job_done, b * NJ + n + 1)
                        if job[0] == "key":
                            lo, wd = NCOL[job[2]]
                            dst, src, bias = ch[:, job[1], lo:lo + wd], pJ[:, n % 4, 0:wd], g["bias_col"][:, 3, job[1]:job[1] + 1]
                        else:
                            dst, src, bias = sh[:, job[1], job[2], :], pJ[:, n % 4, :], g["bias_col"][:, job[1], job[2]:job[2] + 1]
                        nc.scalar.activation(dst, src, ACT.Identity, bias=bias).then_inc(high, 1)

        @block.vector
        def _(dve):
            dve.wait_ge(ones_set, 1)
            with dve.Fori(0, B) as b:
                chain = Chain(dve, chain_s, b * (LN_LINKS + 1), passed)

                def norm():
                    dve.wait_ge(x_in, b * 16 + 16)
                    dve.wait_ge(o_done, b + 1)
                    dve.wait_ge(tr_done, b)
                    res = g["x_res"][:, bass.ds(b * (TT * D), TT * D)]
                    chain.link(nc.vector.tensor_tensor(x[:, :, :].rearrange("p t d -> p (t d)"), x[:, :, :].rearrange("p t d -> p (t d)"),
                                                       pO[:, :, :].rearrange("p t d -> p (t d)"), ALU.add))
                    nc.vector.tensor_copy(res, x[:, :, :].rearrange("p t d -> p (t d)"))
                    layer_norm(nc, chain, x, xn, w).then_inc(xn_ready, 1)

                for n, job in enumerate(jobs):
                    if n == 4:
                        dve.wait_ge(stored, b * 16 * STORES)
                        norm()
                    if job[0] in ("key", "split"):
                        dve.wait_ge(high, b * NSPL + count("split", n + 1))
                        if job[0] == "key":
                            lo, wd = NCOL[job[2]]
                            dst, hi_, src, bias = (cl[:, job[1], lo:lo + wd], ch[:, job[1], lo:lo + wd], pJ[:, n % 4, 0:wd],
                                                   g["bias_col"][:, 3, job[1]:job[1] + 1])
                        else:
                            dst, hi_, src, bias = (sl[:, job[1], job[2], :], sh[:, job[1], job[2], :], pJ[:, n % 4, :],
                                                   g["bias_col"][:, job[1], job[2]:job[2] + 1])
                        nc.vector.scalar_tensor_tensor(out=dst, in0=src, scalar=bias, in1=hi_.bitcast(F32),
                                                       op0=ALU.add, op1=ALU.subtract).then_inc(low, 1)
                    if job[0] in ("cval", "val"):
                        dve.wait_ge(job_done, b * NJ + n + 1)
                        for a in range(2):
                            tile = 2 * job[1] + a
                            if job[0] == "cval" and tile >= CT:
                                continue
                            rows = LAST if job[0] == "cval" and tile == CT - 1 else P
                            at, row = (tile + TT, 1) if job[0] == "cval" else (tile, 0)
                            last = nc.vector.tensor_tensor(
                                vx[0:rows, at, :, 0:HW], pJ[0:rows, n % 4, a * D:(a + 1) * D].rearrange("p (h n) -> p h n", h=H1),
                                g["bias_row"][0:rows, row, :].rearrange("p (h n) -> p h n", h=H1), ALU.add)
                        last.then_inc(vals, 1)

        @block.tensor
        def _(pe):
            with pe.Fori(0, B) as b:
                for n, job in enumerate(jobs):
                    if n >= 4:
                        freed(pe, b, n - 4)
                    if n == 0:
                        pe.wait_ge(c_in, b * 32 + 32)
                        pe.wait_ge(low, b * NSPL)
                        pe.wait_ge(vals, b * NVAL)
                    slot = pJ[:, n % 4, :]
                    if job[0] == "ctx":
                        for q in range(4):
                            t = job[1] * 4 + q
                            if t < CT:
                                rows = P if t < CT - 1 else LAST
                                last = nc.tensor.transpose(slot[:, q * P:q * P + rows], c[0:rows, t, :], g["ident"][0:rows, 0:rows])
                        last.then_inc(job_done, 1)
                    if n == 3:
                        pe.wait_ge(z_in, b * 16 + 16)
                        pe.wait_ge(xn_ready, b)
                        for t in range(TT):
                            for q in range(PAIRS):
                                last = nc.tensor.matmul(pO[:, t, :], z[:, q, t * P:(t + 1) * P], g["wvo"][:, q, :],
                                                        start=q == 0, stop=q == PAIRS - 1)
                        last.then_inc(o_done, 1)
                    if job[0] == "key":
                        pe.wait_ge(ctr, b * NCTX + NCTX)
                        lo, wd = NCOL[job[2]]
                        nc.tensor.matmul(slot[:, 0:wd], g["xWck"][:, job[1] * P:(job[1] + 1) * P], cT[:, lo:lo + wd],
                                         start=True, stop=True).then_inc(job_done, 1)
                    if job[0] == "cval":
                        for a in range(2):
                            t = 2 * job[1] + a
                            if t < CT:
                                rows = P if t < CT - 1 else LAST
                                last = nc.tensor.matmul(slot[0:rows, a * D:(a + 1) * D], cT[:, t * P:t * P + rows], g["xWcv"][:, :],
                                                        start=True, stop=True)
                        last.then_inc(job_done, 1)
                    if job == ("split", 0, 0):
                        pe.wait_ge(xn_ready, b + 1)
                        pe.wait_ge(xnT_ready, b * DC)
                        transpose_tokens(nc, xn, g["ident"], pT).then_inc(tr_done, 1)
                        pe.wait_ge(xnT_ready, b * DC + DC)
                    if job[0] == "split":
                        wt = g[("xWq", "xWk", "xWcq")[job[1]]]
                        for d in range(DC):
                            last = nc.tensor.matmul(slot, wt[:, d, job[2] * P:(job[2] + 1) * P], xnT[:, d, :],
                                                    start=d == 0, stop=d == DC - 1)
                        last.then_inc(job_done, 1)
                    if job[0] == "val":
                        for a in range(2):
                            t = 2 * job[1] + a
                            for d in range(DC):
                                last = nc.tensor.matmul(slot[:, a * D:(a + 1) * D], xnT[:, d, t * P:(t + 1) * P], g["xWv"][:, d, :],
                                                        start=d == 0, stop=d == DC - 1)
                        last.then_inc(job_done, 1)


def mixed_attention(nc, g):
    with ExitStack() as ctx:
        r = Resources(nc, ctx)
        K = 2
        R = 4 * HW
        qs = [r.sb(f"d_qs_{k}", [R + 1, 4, S], F32R) for k in range(K)]
        ks = [r.sb(f"d_ks_{k}", [R + 1, 4, S], F32R) for k in range(K)]
        qc = [r.sb(f"d_qc_{k}", [R + 1, 4, S], F32R) for k in range(K)]
        kc = [r.sb(f"d_kc_{k}", [R + 1, 4, SCP], F32R) for k in range(K)]
        v = [r.sb(f"d_v_{k}", [P, CH, 4 * 2 * HW], F32) for k in range(K)]
        part = [r.sb(f"d_part_{k}", [P, 4 * TT, 4], F32) for k in range(K)]
        negm = [r.sb(f"d_negm_{k}", [P, 8 * TT], F32) for k in range(K)]
        mT = [r.sb(f"d_mT_{k}", [8 * TT, P], F32R) for k in range(K)]
        prob = r.sb("d_prob", [P, 2, 4, S], F32)
        y = [r.sb(f"d_y_{k}", [P, 2, S], F32) for k in range(K)]
        div = r.sb("d_div", [P, 2, S], F32)
        pM = r.ps("d_pM", [P, 2, S])
        pS = r.ps("d_pS", [P, 2, 2, S])
        pY = r.ps("d_pY", [P, 2, S])
        in_self, in_cross, in_v, row_in, stored = ([r.sem(f"d_{n}_{k}") for k in range(K)]
                                                   for n in ("in_self", "in_cross", "in_v", "row_in", "stored"))
        ones_set, max_mm, max_red, comb, mT_ready = (r.sem(n) for n in ("d_ones_set", "d_max_mm", "d_max_red", "d_comb", "d_mT_ready"))
        st_done, exp_done, pv_done, y_ready, div_done, scaled, z_ready = (r.sem(n) for n in (
            "d_st_done", "d_exp_done", "d_pv_done", "d_y_ready", "d_div_done", "d_scaled", "d_z_ready"))
        passed = r.sem("d_passed")
        block = ctx.enter_context(nc.Block())
        STEPS = B * QUADS
        MJ = 4 * TT + 4 * TT * len(KCOLS) + 1
        RED = MJ - 1

        def steps(engine, body):
            with engine.Fori(0, STEPS // K - 1) as m:
                for k in range(K):
                    body(m * K + k, k, K)
            for k in range(K):
                body(STEPS - K + k, k, K - 1 - k)

        @block.sync
        def _(sp):
            def stack(dst, parts, it, n, sem):
                for row, src in enumerate(parts):
                    sp.dma_start(dst[row * HW:(row + 1) * HW, :, :].bitcast(F32), src[it].rearrange("(h d) n -> d h n", h=4)).then_inc(sem, 16)

            def load_self(it, k):
                stack(qs[k], [g["s1h"][0], g["s1h"][0], g["s1l"][0], g["s1l"][0]], it, S, in_self[k])
                stack(ks[k], [g["s1h"][1], g["s1l"][1], g["s1h"][1], g["s1l"][1]], it, S, in_self[k])

            def load_cross(it, k):
                stack(qc[k], [g["s1h"][2], g["s1h"][2], g["s1l"][2], g["s1l"][2]], it, S, in_cross[k])
                stack(kc[k], [g["c1h"], g["c1l"], g["c1h"], g["c1l"]], it, SCP, in_cross[k])

            def load_v(it, k):
                sp.dma_start(v[k][:, 0:CH - 1, :], g["v1"][it][:, 0:CH - 1]).then_inc(in_v[k], 16)
                sp.dma_start(v[k][0:LAST, CH - 1, :], g["v1"][it][0:LAST, CH - 1]).then_inc(in_v[k], 16)

            def rows(it, k):
                sp.wait_ge(mT_ready, it + 1)
                for n, q in enumerate((qs, qc)):
                    sp.dma_start(q[k][R:R + 1, :, :].bitcast(F32), mT[k][n * 4 * TT:(n + 1) * 4 * TT, :].bitcast(F32)).then_inc(row_in[k], 16)

            sp.wait_ge(ones_set, 1)
            for n in range(K):
                load_self(n, n)
                load_cross(n, n)
                load_v(n, n)
            rows(0, 0)

            def body(it, k, follow):
                if follow >= 2:
                    sp.wait_ge(st_done, it * 2 * CH + 2 * TT)
                    load_self(it + 2, k)
                if follow >= 1:
                    rows(it + 1, 1 - k)
                if follow >= 2:
                    sp.wait_ge(st_done, it * 2 * CH + 2 * CH)
                    load_cross(it + 2, k)
                    sp.wait_ge(pv_done, it * CH + CH)
                    load_v(it + 2, k)

            steps(sp, body)

        @block.gpsimd
        def _(pool):
            def body(it, k, follow):
                pool.wait_ge(div_done, 2 * it + 2)
                nc.gpsimd.tensor_tensor(y[k][:, :, :], y[k][:, :, :], div[:, :, :], ALU.mult).then_inc(scaled, 1)
                pool.wait_ge(scaled, it + 1)
                nc.gpsimd.tensor_tensor(y[k][:, 0, :], y[k][:, 0, :], y[k][:, 1, :], ALU.add).then_inc(z_ready, 1)
                pool.wait_ge(z_ready, it + 1)
                pool.dma_start(g["z1"][it], y[k][:, 0, :]).then_inc(stored[k], 16)

            steps(pool, body)
            for k in range(K):
                pool.wait_ge(stored[k], 16 * STEPS // K)

        @block.vector
        def _(dve):
            for k in range(K):
                nc.vector.memset(ks[k][R:R + 1, :, :].bitcast(F32), 1.0)
                last = nc.vector.memset(kc[k][R:R + 1, :, :].bitcast(F32), 1.0)
            last.then_inc(ones_set, 1)

            def maxima(it, k):
                for j in range(RED):
                    slot = (k * MJ + j) % 2
                    dve.wait_ge(max_mm, it * MJ + j + 1)
                    if j < 4 * TT:
                        dst, w = negm[k][:, j:j + 1], P * (j % TT + 1)
                    else:
                        n = j - 4 * TT
                        dst, w = part[k][:, n // 4, n % 4:n % 4 + 1], KCOLS[n % 4][1]
                    nc.vector.tensor_reduce(dst, pM[:, slot, 0:w], AX.X, ALU.max, negate=True).then_inc(max_red, 1)
                dve.wait_ge(max_red, it * RED + RED)
                nc.vector.tensor_reduce(negm[k][:, 4 * TT:8 * TT], part[k][:, :, :], AX.X, ALU.min).then_inc(comb, 1)
                dve.wait_ge(max_mm, it * MJ + MJ)
                slot = (k * MJ + RED) % 2
                nc.vector.tensor_copy(mT[k][:, :], pM[0:8 * TT, slot, 0:P]).then_inc(mT_ready, 1)

            maxima(0, 0)

            def body(it, k, follow):
                if follow >= 1:
                    maxima(it + 1, 1 - k)
                dve.wait_ge(y_ready, 2 * it + 2)
                dve.wait_ge(scaled, it)
                dve.sem_inc(passed, 1)
                nc.vector.stream_shuffle(div[:, :, :], y[k][:, :, :], [HW + n % HW for n in range(2 * HW)]).then_inc(div_done, 1)
                dve.wait_ge(div_done, 2 * it + 1)
                nc.vector.reciprocal(div[:, :, :], div[:, :, :]).then_inc(div_done, 1)

            steps(dve, body)

        def chunk(c):
            if c < TT:
                return 0, c, c * P, P
            return 1, c - TT, 0, P if c < CH - 1 else LAST

        @block.scalar
        def _(act):
            with act.Fori(0, STEPS // K) as m:
                for k in range(K):
                    it = m * K + k
                    for c in range(CH):
                        _, _, lo, n = chunk(c)
                        ring = (k * CH + c) % 2
                        for a in range(2):
                            act.wait_ge(st_done, (it * CH + c) * 2 + a + 1)
                            nc.scalar.activation(prob[0:n, ring, 2 * a:2 * a + 2, lo:S], pS[0:n, a, :, lo:S], ACT.Exp,
                                                 scale=HW ** -0.5).then_inc(exp_done, 1)
                        if c == TT + 1:
                            act.wait_ge(stored[k], m * 16)
                            act.wait_ge(pv_done, it * CH + TT)
                            nc.scalar.activation(y[k][:, 0, :], pY[:, 0, :], ACT.Copy).then_inc(y_ready, 1)
                    act.wait_ge(pv_done, it * CH + CH)
                    nc.scalar.activation(y[k][:, 1, :], pY[:, 1, :], ACT.Copy).then_inc(y_ready, 1)

        @block.tensor
        def _(pe):
            def max_job(it, k, j):
                slot = (k * MJ + j) % 2
                if j == 0:
                    pe.wait_ge(in_self[k], (it // K) * 128 + 128)
                if j == 4 * TT:
                    pe.wait_ge(in_cross[k], (it // K) * 128 + 128)
                if j >= 2:
                    pe.wait_ge(max_red, it * RED + j - 1)
                elif not isinstance(it, int) or it > 0:
                    if j == 0:
                        pe.wait_ge(max_red, it * RED)
                    else:
                        pe.wait_ge(mT_ready, it)
                if j < 4 * TT:
                    h, t = j // TT, j % TT
                    nc.tensor.matmul(pM[:, slot, 0:P * (t + 1)], qs[k][0:R, h, t * P:(t + 1) * P], ks[k][0:R, h, 0:P * (t + 1)],
                                     start=True, stop=False)
                    nc.tensor.matmul(pM[:, slot, P * t:P * (t + 1)], g["identb"][:, :], g["mask_n"][:, :],
                                     start=False, stop=True).then_inc(max_mm, 1)
                elif j < RED:
                    n = j - 4 * TT
                    h, t, (lo, w) = n // 4 // TT, n // 4 % TT, KCOLS[n % 4]
                    nc.tensor.matmul(pM[:, slot, 0:w], qc[k][0:R, h, t * P:(t + 1) * P], kc[k][0:R, h, lo:lo + w],
                                     start=True, stop=True).then_inc(max_mm, 1)
                else:
                    pe.wait_ge(comb, it + 1)
                    nc.tensor.transpose(pM[0:8 * TT, slot, 0:P], negm[k][:, :], g["ident"][:, :]).then_inc(max_mm, 1)

            for j in range(MJ):
                max_job(0, 0, j)

            def scores(it, k, c):
                cross, j, lo, n = chunk(c)
                if c == 0:
                    pe.wait_ge(row_in[k], (it // K) * 32 + 32)
                keys, qry = (kc, qc) if cross else (ks, qs)
                for a in range(2):
                    if c > 0:
                        pe.wait_ge(exp_done, (it * CH + c) * 2 + a - 1)
                    for h in range(2):
                        last = nc.tensor.matmul(pS[0:n, a, h, lo:S], keys[k][:, 2 * a + h, j * P:j * P + n], qry[k][:, 2 * a + h, lo:S],
                                                start=True, stop=bool(cross))
                        if not cross:
                            last = nc.tensor.matmul(pS[:, a, h, lo:lo + P], g["identb"][:, :], g["mask_t"][:, :],
                                                    start=False, stop=True)
                    last.then_inc(st_done, 1)

            def values(it, k, c):
                cross, j, lo, n = chunk(c)
                if c == 0:
                    pe.wait_ge(in_v[k], (it // K) * 32 + 32)
                if j == 0:
                    pe.wait_ge(y_ready, 2 * it)
                pe.wait_ge(exp_done, (it * CH + c) * 2 + 2)
                ring = (k * CH + c) % 2
                for h in range(4):
                    last = nc.tensor.matmul(pY[32 * h:32 * h + 32, cross, lo:S], v[k][0:n, c, 32 * h:32 * h + 32],
                                            prob[0:n, ring, h, lo:S], start=j == 0, stop=c in (TT - 1, CH - 1))
                last.then_inc(pv_done, 1)

            def body(it, k, follow):
                jobs = list(range(MJ)) if follow >= 1 else []
                for c in range(CH):
                    scores(it, k, c)
                    if c:
                        values(it, k, c - 1)
                    for _ in range(min(6, len(jobs))):
                        max_job(it + 1, 1 - k, jobs.pop(0))
                values(it, k, CH - 1)

            steps(pe, body)


def route_stage(nc, g, i):
    with ExitStack() as ctx:
        r = Resources(nc, ctx)
        z = r.sb("e_z", [P, QUADS, S], F32)
        x = r.sb("e_x", [P, TT, D], F32)
        rows = r.sb("e_rows", [P, 2, TT, ROW], F32)
        xnT = r.sb("e_xnT", [P, DC, S], F32)
        o = r.sb("e_o", [P, TT, D], F32)
        w = ln_work(r, "e")

        def small(name, dt=F32, shape=(P, TT, NE)):
            return r.sb(f"e_{name}", list(shape), dt)

        lg, wt, rest, eq, s1, s2, gt, both, where, pick = (small(n) for n in (
            "lg", "wt", "rest", "eq", "s1", "s2", "gt", "both", "where", "pick"))
        mask = small("mask", BF16)
        run = small("run", BF16, (P, TT + 1, NE))
        top, tot, noop = (small(n, F32, (P, TT)) for n in ("top", "tot", "noop"))
        idx = small("idx", I32, (P, 2, TT))
        pO = r.ps("e_pO", [P, TT, D])
        pT = r.ps("e_pT", [P, DC, S])
        pL = r.ps("e_pL", [P, TT, NE])
        pC = r.ps("e_pC", [P, TT, NE])
        z_in, chain_s, pad_set, o_done, xn_ready, tr_done, xnT_ready = (r.sem(n) for n in (
            "e_z_in", "e_chain", "e_pad_set", "e_o_done", "e_xn_ready", "e_tr_done", "e_xnT_ready"))
        lg_done, lg_ready, ex_ready, mask_ready, pos_done, copied, sent_ready, o_ready, sent, stored = (r.sem(n) for n in (
            "e_lg_done", "e_lg_ready", "e_ex_ready", "e_mask_ready", "e_pos_done", "e_copied", "e_sent_ready", "e_o_ready",
            "e_sent", "e_stored"))
        block = ctx.enter_context(nc.Block())
        passed = r.sem("e_passed")
        LINKS = 52

        def over_tiles(a):
            return a.unsqueeze(2).broadcast_to([P, TT, NE])

        @block.sync
        def _(sp):
            with sp.Fori(0, B) as b:
                sp.wait_ge(o_done, b)
                sp.dma_start(z[:, :, :], g["z1"][bass.ds(b * QUADS, QUADS)].rearrange("q p n -> p q n")).then_inc(z_in, 16)

        @block.scalar
        def _(act):
            with act.Fori(0, B) as b:
                act.wait_ge(tr_done, b + 1)
                act.wait_ge(lg_done, b)
                for d in range(DC):
                    nc.scalar.activation(xnT[:, d, :], pT[:, d, :], ACT.Copy).then_inc(xnT_ready, 1)
                act.wait_ge(lg_ready, b + 1)
                nc.scalar.activation(wt[:, :, :], lg[:, :, :], ACT.Exp).then_inc(ex_ready, 1)
                act.wait_ge(o_ready, b + 1)
                act.dma_start(g["acc"][bass.ds(b * S, S)].rearrange("(t p) d -> p t d", p=P), o[:, :, :]).then_inc(stored, 16)
            act.wait_ge(stored, B * 16)

        @block.vector
        def _(dve):
            nc.vector.memset(run[:, :, :], 0.0)
            nc.vector.memset(rows[:, :, :, D + 2:ROW], 0.0).then_inc(pad_set, 1)
            dve.wait_ge(pad_set, 1)
            with dve.Fori(0, B) as b:
                chain = Chain(dve, chain_s, b * LINKS, passed)
                link = chain.link
                V = nc.vector
                dve.wait_ge(o_done, b + 1)
                dve.wait_ge(sent, b * 16 * 2 * TT)
                dve.wait_ge(copied, b)
                dve.wait_ge(stored, b * 16)
                link(V.tensor_tensor(x[:, :, :].rearrange("p t d -> p (t d)"), pO[:, :, :].rearrange("p t d -> p (t d)"),
                                     g["x_res"][:, bass.ds(b * (TT * D), TT * D)], ALU.add))
                for t in range(TT):
                    last = V.tensor_tensor(x[:, t, :], x[:, t, :], g["bias_row"][:, 2, :], ALU.add)
                link(last)
                layer_norm(nc, chain, x, rows[:, 0, :, 0:D], w).then_inc(xn_ready, 1)
                dve.wait_ge(lg_done, b + 1)
                link(V.tensor_tensor(lg[:, :, :], pL[:, :, :], g["router_bias"][:, :].unsqueeze(1).broadcast_to([P, TT, NE]), ALU.add))
                link(V.tensor_reduce(top[:, :], lg[:, :, :], AX.X, ALU.max))
                V.tensor_tensor(lg[:, :, :], lg[:, :, :], over_tiles(top[:, :]), ALU.subtract).then_inc(lg_ready, 1)
                dve.wait_ge(ex_ready, b + 1)
                link(V.tensor_reduce(tot[:, :], wt[:, :, :], AX.X, ALU.add))
                link(V.reciprocal(tot[:, :], tot[:, :]))
                link(V.tensor_tensor(wt[:, :, :], wt[:, :, :], over_tiles(tot[:, :]), ALU.mult))
                src = wt
                for n, sel in enumerate((s1, s2)):
                    m = rows[:, n, :, D]
                    link(V.tensor_reduce(m, src[:, :, :], AX.X, ALU.max))
                    link(V.tensor_tensor(eq[:, :, :], src[:, :, :], over_tiles(m), ALU.is_equal))
                    link(V.tensor_tensor(eq[:, :, :], eq[:, :, :], g["prio"][:, :, :], ALU.mult))
                    link(V.tensor_reduce(top[:, :], eq[:, :, :], AX.X, ALU.max))
                    link(V.tensor_tensor(sel[:, :, :], eq[:, :, :], over_tiles(top[:, :]), ALU.is_equal))
                    if n == 0:
                        link(V.scalar_tensor_tensor(out=rest[:, :, :], in0=sel[:, :, :], scalar=-2.0, in1=wt[:, :, :],
                                                    op0=ALU.mult, op1=ALU.add))
                        src = rest
                link(V.tensor_tensor(both[:, :, :], s1[:, :, :], s2[:, :, :], ALU.add))
                link(V.tensor_scalar(gt[:, :, :], wt[:, :, :], 0.0, None, ALU.is_gt))
                link(V.tensor_tensor(mask[:, :, :], both[:, :, :], gt[:, :, :], ALU.mult))
                link(V.tensor_copy(run[:, 0, :], run[:, TT, :]))
                for t in range(TT):
                    ins = V.tensor_tensor(run[:, t + 1, :], run[:, t, :], mask[:, t, :], ALU.add)
                    if t == TT - 1:
                        ins.then_inc(mask_ready, 1)
                        dve.wait_ge(mask_ready, b + 1)
                    else:
                        link(ins)
                dve.wait_ge(pos_done, b + 1)
                link(V.tensor_scalar(eq[:, :, :], pC[:, :, :], float(CAP), None, ALU.is_lt))
                link(V.tensor_tensor(eq[:, :, :], eq[:, :, :], gt[:, :, :], ALU.mult))
                link(V.tensor_tensor(where[:, :, :], pC[:, :, :], g["slot0"][:, :, :], ALU.add))
                link(V.tensor_tensor(where[:, :, :], where[:, :, :], eq[:, :, :], ALU.mult))
                link(V.tensor_scalar_add(where[:, :, :], where[:, :, :], float(FAR)))
                for n, sel in enumerate((s1, s2)):
                    link(V.tensor_tensor(pick[:, :, :], where[:, :, :], sel[:, :, :], ALU.mult))
                    link(V.tensor_reduce(top[:, :], pick[:, :, :], AX.X, ALU.add))
                    link(V.tensor_copy(idx[:, n, :], top[:, :]))
                for n in range(2):
                    last = V.tensor_copy(rows[:, n, :, D + 1].bitcast(I32), g["tok"][:, :])
                last.then_inc(sent_ready, 1)
                dve.wait_ge(sent_ready, b + 1)
                link(V.tensor_scalar_add(g["tok"][:, :], g["tok"][:, :], float(S)))
                link(V.tensor_tensor(noop[:, :], both[:, :, NX], wt[:, :, NX], ALU.mult))
                for t in range(TT):
                    last = V.scalar_tensor_tensor(out=o[:, t, :], in0=rows[:, 0, t, 0:D], scalar=noop[:, t:t + 1],
                                                  in1=x[:, t, :], op0=ALU.mult, op1=ALU.add)
                last.then_inc(o_ready, 1)
                dve.wait_ge(o_ready, b + 1)
                assert chain.n == LINKS, chain.n

        @block.tensor
        def _(pe):
            with pe.Fori(0, B) as b:
                pe.wait_ge(z_in, b * 16 + 16)
                pe.wait_ge(xn_ready, b)
                for t in range(TT):
                    for q in range(QUADS):
                        last = nc.tensor.matmul(pO[:, t, :], z[:, q, t * P:(t + 1) * P], g["wp"][:, q, :],
                                                start=q == 0, stop=q == QUADS - 1)
                last.then_inc(o_done, 1)
                pe.wait_ge(xn_ready, b + 1)
                pe.wait_ge(xnT_ready, b * DC)
                transpose_tokens(nc, rows[:, 0, :, 0:D], g["ident"], pT).then_inc(tr_done, 1)
                pe.wait_ge(xnT_ready, b * DC + DC)
                for t in range(TT):
                    for d in range(DC):
                        last = nc.tensor.matmul(pL[:, t, :], xnT[:, d, t * P:(t + 1) * P], g["rwT"][:, d, :],
                                                start=d == 0, stop=d == DC - 1)
                last.then_inc(lg_done, 1)
                pe.wait_ge(mask_ready, b + 1)
                for t in range(TT):
                    nc.tensor.matmul(pC[:, t, :], g["before"][:, :], mask[:, t, :], start=True, stop=False)
                    last = nc.tensor.matmul(pC[:, t, :], g["onesb"][:, :], run[:, t, :], start=False, stop=True)
                last.then_inc(pos_done, 1)

        @block.gpsimd
        def _(pool):
            with pool.Fori(0, B) as b:
                pool.wait_ge(xn_ready, b + 1)
                pool.sem_inc(passed, 1)
                nc.gpsimd.tensor_copy(rows[:, 1, :, 0:D], rows[:, 0, :, 0:D]).then_inc(copied, 1)
                pool.wait_ge(sent_ready, b + 1)
                pool.wait_ge(copied, b + 1)
                pool.sem_inc(passed, 1)
                for n in range(2):
                    for t in range(TT):
                        pool.indirect_dma_start(
                            out=g["slot_rows"], out_offset=bass.IndirectOffsetOnAxis(ap=idx[:, n, t:t + 1].bitcast(U32), axis=0),
                            in_=rows[:, n, t, :], in_offset=None, bounds_check=SLOTS - 1, oob_is_err=False).then_inc(sent, 16)
            pool.wait_ge(sent, B * 16 * 2 * TT)


def expert_stage(nc, g, i):
    with ExitStack() as ctx:
        r = Resources(nc, ctx)
        K = 2
        CTT = CAP // P
        wi = [r.sb(f"f_wi_{k}", [P, DC, FI], F32) for k in range(K)]
        wo = [r.sb(f"f_wo_{k}", [P, FC, D], F32) for k in range(K)]
        rows = [r.sb(f"f_rows_{k}", [P, CTT, ROW], F32) for k in range(K)]
        y = [r.sb(f"f_y_{k}", [P, CTT, D], F32) for k in range(K)]
        xT = r.sb("f_xT", [P, DC, CAP], F32)
        hT = r.sb("f_hT", [P, FC, CAP], F32)
        pT = r.ps("f_pT", [P, DC, CAP])
        pH = r.ps("f_pH", [P, 4, CAP])
        pO = r.ps("f_pO", [P, CTT, D])
        loaded = [r.sem(f"f_loaded_{k}") for k in range(K)]
        tr_done, xT_ready, h_done, h_ready, o_done, y_ready, added = (r.sem(n) for n in (
            "f_tr_done", "f_xT_ready", "f_h_done", "f_h_ready", "f_o_done", "f_y_ready", "f_added"))
        out_done, passed = r.sem("f_out_done"), r.sem("f_passed")
        block = ctx.enter_context(nc.Block())

        def experts(engine, body):
            with engine.Fori(0, NX // K) as m:
                for k in range(K):
                    body(m * K + k, k)
            body(NX - 1, 0)

        @block.sync
        def _(sp):
            def body(e, k):
                sp.dma_start(wi[k][:, :, :], i["wi"][e].rearrange("(c p) f -> p c f", p=P)).then_inc(loaded[k], 16)
                sp.dma_start(wo[k][:, :, :], i["wo"][e].rearrange("(c p) d -> p c d", p=P)).then_inc(loaded[k], 16)
                sp.dma_start(rows[k][:, :, :], g["slot_rows"][bass.ds(e * CAP, CAP)].rearrange("(t p) c -> p t c", p=P)).then_inc(loaded[k], 16)

            for k in range(K):
                body(k, k)
            with sp.Fori(0, NX // K - 1) as m:
                for k in range(K):
                    sp.wait_ge(o_done, m * K + k + 1)
                    sp.wait_ge(added, (m * K + k + 1) * 16 * CTT)
                    body(m * K + k + K, k)
            sp.wait_ge(o_done, NX - 2)
            sp.wait_ge(added, (NX - 2) * 16 * CTT)
            body(NX - 1, 0)
            sp.wait_ge(added, NX * 16 * CTT)
            sp.dma_start(i["out"].rearrange("b s d -> (b s) d"), g["acc"][0:B * S]).then_inc(out_done, 16)
            sp.wait_ge(out_done, 16)

        @block.tensor
        def _(pe):
            def body(e, k):
                pe.wait_ge(loaded[k], (e // K) * 48 + 48)
                pe.wait_ge(xT_ready, e * DC)
                for d in range(DC):
                    for t in range(CTT):
                        last = nc.tensor.transpose(pT[:, d, t * P:(t + 1) * P], rows[k][:, t, d * P:(d + 1) * P], g["ident"][:, :])
                last.then_inc(tr_done, 1)
                pe.wait_ge(xT_ready, e * DC + DC)
                for f in range(FC):
                    if f >= 4:
                        pe.wait_ge(h_ready, e * FC + f - 3)
                    for d in range(DC):
                        last = nc.tensor.matmul(pH[:, f % 4, :], wi[k][:, d, f * P:(f + 1) * P], xT[:, d, :],
                                                start=d == 0, stop=d == DC - 1)
                    last.then_inc(h_done, 1)
                pe.wait_ge(h_ready, e * FC + FC)
                pe.wait_ge(y_ready, e)
                for t in range(CTT):
                    for f in range(FC):
                        last = nc.tensor.matmul(pO[:, t, :], hT[:, f, t * P:(t + 1) * P], wo[k][:, f, :],
                                                start=f == 0, stop=f == FC - 1)
                last.then_inc(o_done, 1)

            experts(pe, body)

        @block.scalar
        def _(act):
            def body(e, k):
                act.wait_ge(tr_done, e + 1)
                act.wait_ge(h_done, e * FC)
                for d in range(DC):
                    nc.scalar.activation(xT[:, d, :], pT[:, d, :], ACT.Copy).then_inc(xT_ready, 1)
                act.wait_ge(o_done, e)
                for f in range(FC):
                    act.wait_ge(h_done, e * FC + f + 1)
                    nc.scalar.activation(hT[:, f, :], pH[:, f % 4, :], ACT.Relu).then_inc(h_ready, 1)

            experts(act, body)

        @block.vector
        def _(dve):
            def body(e, k):
                dve.wait_ge(o_done, e + 1)
                dve.wait_ge(added, e * 16 * CTT)
                for t in range(CTT):
                    last = nc.vector.tensor_scalar(y[k][:, t, :], pO[:, t, :], rows[k][:, t, D:D + 1], None, ALU.mult)
                last.then_inc(y_ready, 1)

            experts(dve, body)

        @block.gpsimd
        def _(pool):
            def body(e, k):
                pool.wait_ge(y_ready, e + 1)
                pool.wait_ge(added, e * 16 * CTT)
                pool.sem_inc(passed, 1)
                for t in range(CTT):
                    pool.indirect_dma_start(
                        out=g["acc"], out_offset=bass.IndirectOffsetOnAxis(ap=rows[k][:, t, D + 1:D + 2].bitcast(U32), axis=0),
                        in_=y[k][:, t, :], in_offset=None, bounds_check=B * S + SLOTS - 1, oob_is_err=True,
                        compute_op=ALU.add).then_inc(added, 16)

            experts(pool, body)


def decoder_layer(nc, i):
    with ExitStack() as ctx:
        r = Resources(nc, ctx)

        def dram(name, shape, dt):
            return nc.dram_tensor(name, shape, dt, kind="Internal").ap()

        g = {
            "lat_h": dram("lat_h", [B, P, S], F32), "lat_l": dram("lat_l", [B, LD, S], F32),
            "lat_v": dram("lat_v", [B, P, TT, LD], F32),
            "q0h": dram("q0h", [B * PAIRS, P, S], F32), "q0l": dram("q0l", [B * PAIRS, P, S], F32),
            "z0": dram("z0", [B * PAIRS, P, S], F32),
            "s1h": dram("s1h", [3, B * QUADS, 4 * HW, S], F32), "s1l": dram("s1l", [3, B * QUADS, 4 * HW, S], F32),
            "c1h": dram("c1h", [B * QUADS, 4 * HW, SCP], F32), "c1l": dram("c1l", [B * QUADS, 4 * HW, SCP], F32),
            "v1": dram("v1", [B * QUADS, P, CH, 4 * 2 * HW], F32), "z1": dram("z1", [B * QUADS, P, S], F32),
            "slot_rows": dram("slot_rows", [SLOTS, ROW], F32), "acc": dram("acc", [B * S + SLOTS, D], F32),
            "ident": r.sb("ident", [P, P], F32), "identb": r.sb("identb", [P, P], BF16),
            "mask_t": r.sb("mask_t", [P, P], BF16), "mask_n": r.sb("mask_n", [P, P], BF16),
            "before": r.sb("before", [P, P], BF16), "onesb": r.sb("onesb", [P, P], BF16), "ones": r.sb("ones", [P, P], F32),
            "tok": r.sb("tok", [P, TT], I32), "slot0": r.sb("slot0", [P, TT, NE], I32), "prio": r.sb("prio", [P, TT, NE], I32),
            "bias_col": r.sb("bias_col", [P, 4, DC], F32), "bias_row": r.sb("bias_row", [P, 3, D], F32),
            "router_bias": r.sb("router_bias", [P, NE], F32), "rwT": r.sb("rwT", [P, DC, NE], F32),
            "wp": r.sb("wp", [P, QUADS, D], F32), "x_res": r.sb("x_res", [P, B * TT * D], F32),
        }
        with ExitStack() as early:
            re = Resources(nc, early)
            for name in ("xWq", "xWk", "xWcq", "xWv"):
                g[name] = re.sb(name, [P, DC, D], F32)
            for name in ("xWck", "xWcv"):
                g[name] = re.sb(name, [P, D], F32)
            g["wdd"] = re.sb("wdd", [P, DC, 2, LD], F32)
            g["wt"] = re.sb("wt", [P, DC, H0 * LD], F32)
            g["wvo"] = re.sb("wvo", [P, PAIRS, D], F32)
            prepare(nc, g, i)
            latent_stage(nc, g, i)
            latent_attention(nc, g)
            cross_stage(nc, g, i)
        mixed_attention(nc, g)
        route_stage(nc, g, i)
        expert_stage(nc, g, i)


INPUTS = {"x": "x", "ctx_512": "ctx", "L0_attn_Wq": "Wq", "L0_attn_Wkv_down": "Wkv_down", "L0_attn_Wk_up": "Wk_up",
          "L0_attn_Wv_up": "Wv_up", "L0_attn_Wout": "Wout", "L0_xattn_Wk": "xWk", "L0_xattn_bk": "xbk", "L0_xattn_Wq": "xWq",
          "L0_xattn_bq": "xbq", "L0_xattn_Wv": "xWv", "L0_xattn_bv": "xbv", "L0_xattn_Wck": "xWck", "L0_xattn_bck": "xbck",
          "L0_xattn_Wcq": "xWcq", "L0_xattn_bcq": "xbcq", "L0_xattn_Wcv": "xWcv", "L0_xattn_bcv": "xbcv",
          "L0_xattn_Wp": "xWp", "L0_xattn_bp": "xbp", "L0_ffn_router_w": "router_w", "L0_ffn_router_b": "router_b",
          "L0_ffn_experts_inter": "wi", "L0_ffn_experts_out": "wo"}


def kernel(**inputs):
    import numpy as np
    import concourse.bacc as bacc
    from concourse.bass_utils import run_bass_kernel_spmd

    nc = bacc.Bacc("TRN2", target_bir_lowering=False, num_devices=1)
    arrays, aps = {}, {}
    for name, short in INPUTS.items():
        a = np.ascontiguousarray(inputs[name])
        arrays[f"in_{name}"] = a
        aps[short] = nc.dram_tensor(f"in_{name}", a.shape, mybir.dt.from_np(a.dtype), kind="ExternalInput").ap()
    aps["out"] = nc.dram_tensor("out", [B, S, D], F32, kind="ExternalOutput").ap()
    decoder_layer(nc, aps)
    result = run_bass_kernel_spmd(nc, [arrays], core_ids=[0])
    return result.results[0]["out"]
```

```python
from contextlib import ExitStack

import concourse.bass as bass
from concourse import mybir

F32 = mybir.dt.float32
F32R = mybir.dt.float32r
BF16 = mybir.dt.bfloat16
I32 = mybir.dt.int32
U32 = mybir.dt.uint32
ALU = mybir.AluOpType
ACT = mybir.ActivationFunctionType
AX = mybir.AxisListType

P = 128
B, S, D = 8, 512, 256
DC = D // P
TT = S // P
H0, HD, LD = 16, 64, 64
PAIRS = H0 // 2
H1, HW = 16, 16
QUADS = H1 // 4
SC, CW = 1601, 128
SCP = SC + 1
CT = -(-SC // P)
LAST = SC - (CT - 1) * P
CH = TT + CT
NE, NX, FI = 8, 7, 1024
FC = FI // P
CAP = (B * S) // NE
SLOTS = NX * CAP
ROW = D + 4
FAR = 65536
MASKED = -1e30
EPS = 1e-5
RSQRT_SEED = 0x5F3759DF
KCOLS = [(0, 400), (400, 400), (800, 400), (1200, 402)]


class Resources:
    def __init__(self, nc, ctx):
        self.nc, self.ctx = nc, ctx

    def sb(self, name, shape, dt):
        return self.ctx.enter_context(self.nc.sbuf_tensor(name, shape, dt))

    def ps(self, name, shape, dt=F32):
        return self.ctx.enter_context(self.nc.psum_tensor(name, shape, dt))

    def sem(self, name):
        return self.ctx.enter_context(self.nc.semaphore(name))


class Chain:

    def __init__(self, engine, sem, first, passed=None):
        self.engine, self.sem, self.first, self.n, self.passed = engine, sem, first, 0, passed

    def link(self, ins, apart=False):
        self.n += 1
        ins.then_inc(self.sem, 1)
        self.engine.wait_ge(self.sem, self.first + self.n)
        if apart:
            self.engine.sem_inc(self.passed, 1)


def at_least(engine, sem, value):
    if not isinstance(value, int) or value > 0:
        engine.wait_ge(sem, value)


def wait_apart(engine, passed, sem, value):
    engine.wait_ge(sem, value)
    engine.sem_inc(passed, 1)


def batches(engine, body):
    body(0)
    with engine.Fori(1, B) as b:
        body(b)


def slotted_steps(engine, count, slots, body):
    for n in range(slots):
        body(n, n, slots)
    with engine.Fori(1, count // slots - 1) as m:
        for k in range(slots):
            body(m * slots + k, k, slots)
    for k in range(slots):
        body(count - slots + k, k, slots - 1 - k)


LN_LINKS = 14


def layer_norm(nc, chain, x, xn, w):
    n0 = chain.n
    link = chain.link
    for t in range(TT):
        last = nc.vector.bn_stats(w["stats"][:, t, :], x[:, t, :])
    link(last, apart=True)
    for t in range(TT):
        last = nc.vector.bn_aggr(w["mv"][:, t, :], w["stats"][:, t, :])
    link(last)
    var, y, a = w["var"][:, :], w["rstd"][:, :], w["newton"][:, :]
    link(nc.vector.tensor_scalar_add(var, w["mv"][:, :, 1], EPS))
    link(nc.vector.tensor_scalar(a.bitcast(I32), var.bitcast(I32), 1, None, ALU.logical_shift_right))
    link(nc.vector.tensor_scalar(y.bitcast(I32), a.bitcast(I32), -1.0, float(RSQRT_SEED), ALU.mult, ALU.add))
    for _ in range(3):
        link(nc.vector.scalar_tensor_tensor(out=a, in0=y, scalar=-0.5, in1=y, op0=ALU.mult, op1=ALU.mult))
        link(nc.vector.tensor_tensor(a, a, var, ALU.mult))
        link(nc.vector.scalar_tensor_tensor(out=y, in0=a, scalar=1.5, in1=y, op0=ALU.add, op1=ALU.mult))
    for t in range(TT):
        last = nc.vector.tensor_scalar(xn[:, t, :], x[:, t, :], w["mv"][:, t, 0:1], w["rstd"][:, t:t + 1],
                                       ALU.subtract, ALU.mult)
    assert chain.n - n0 == LN_LINKS
    return last


def ln_work(r, tag):
    return {"stats": r.sb(f"stats_{tag}", [P, TT, 6], F32), "mv": r.sb(f"mv_{tag}", [P, TT, 2], F32),
            "var": r.sb(f"var_{tag}", [P, TT], F32), "rstd": r.sb(f"rstd_{tag}", [P, TT], F32),
            "newton": r.sb(f"newton_{tag}", [P, TT], F32)}


def transpose_tokens(nc, xn, ident, pT):
    for d in range(DC):
        for t in range(TT):
            last = nc.tensor.transpose(pT[:, d, t * P:(t + 1) * P], xn[:, t, d * P:(d + 1) * P], ident[:, :])
    return last


def prepare(nc, g, i):
    with ExitStack() as ctx:
        r = Resources(nc, ctx)
        wq = r.sb("p_wq", [P, DC, H0 * HD], F32)
        wk = r.sb("p_wk", [LD, H0 * HD], F32)
        wv = r.sb("p_wv", [LD, H0 * HD], F32)
        wo = r.sb("p_wo", [P, PAIRS, D], F32)
        wqT = r.sb("p_wqT", [P, PAIRS, D], F32)
        wkB = r.sb("p_wkB", [P, PAIRS, P], F32)
        wvB = r.sb("p_wvB", [P, PAIRS, P], F32)
        rw = r.sb("p_rw", [NE, D], F32)
        none_tok = r.sb("p_none_tok", [P, SLOTS // P, 1], I32)
        empty = r.sb("p_empty", [P, SLOTS // P, ROW], F32)
        pA = r.ps("p_pA", [P, 4, 512])
        pB = r.ps("p_pB", [P, 4, 512])
        in_wq, in_up, in_wo, in_x, in_rw = (r.sem(n) for n in ("in_wq", "in_up", "in_wo", "in_x", "in_rw"))
        id_set, const_set, zero_set, empty_set = (r.sem(n) for n in ("id_set", "const_set", "zero_set", "empty_set"))
        empty_out = r.sem("empty_out")
        wqT_tr, wqT_done, up_tr, up_done, rw_tr, rw_done = (r.sem(n) for n in (
            "wqT_tr", "wqT_done", "up_tr", "up_done", "rw_tr", "rw_done"))
        wt_mm, wt_done, wvo_mm, wvo_done = (r.sem(n) for n in ("wt_mm", "wt_done", "wvo_mm", "wvo_done"))
        block = ctx.enter_context(nc.Block())

        @block.sync
        def _(sp):
            sp.dma_start(wq[:, :, :], i["Wq"].rearrange("(c p) h k -> p c (h k)", p=P)).then_inc(in_wq, 16)
            sp.dma_start(wk[:, :], i["Wk_up"].rearrange("c h k -> c (h k)")).then_inc(in_up, 16)
            sp.dma_start(wv[:, :], i["Wv_up"].rearrange("c h k -> c (h k)")).then_inc(in_up, 16)
            sp.dma_start(rw[:, :], i["router_w"]).then_inc(in_rw, 16)
            sp.dma_start(wo[:, :, :], i["Wout"].rearrange("(g a) k o -> (a k) g o", a=2)).then_inc(in_wo, 16)
            for half in range(2):
                sp.dma_start(g["wdd"][:, :, half, :], i["Wkv_down"].rearrange("(c p) n -> p c n", p=P)).then_inc(in_x, 16)
            for name, dst in (("xWq", "xWq"), ("xWk", "xWk"), ("xWcq", "xWcq"), ("xWv", "xWv"), ("xWp", "wp")):
                sp.dma_start(g[dst][:, :, :], i[name].rearrange("(c p) n -> p c n", p=P)).then_inc(in_x, 16)
            for name in ("xWck", "xWcv"):
                sp.dma_start(g[name][:, :], i[name]).then_inc(in_x, 16)
            for n, name in enumerate(("xbq", "xbk", "xbcq", "xbck")):
                sp.dma_start(g["bias_col"][:, n, :], i[name].rearrange("(c p) -> p c", p=P),
                             allow_slow_non_contiguous=True).then_inc(in_x, 16)
            for n, name in enumerate(("xbv", "xbcv", "xbp")):
                sp.dma_start(g["bias_row"][:, n, :], i[name].partition_broadcast(P)).then_inc(in_x, 16)
            sp.dma_start(g["router_bias"][:, :], i["router_b"].partition_broadcast(P)).then_inc(in_x, 16)
            sp.wait_ge(empty_set, 2)
            sp.dma_start(g["slot_rows"].rearrange("(p n) c -> p n c", p=P), empty[:, :, :]).then_inc(empty_out, 16)
            sp.dma_start(g["acc"][B * S:B * S + SLOTS].rearrange("(p n) c -> p n c", p=P), empty[:, :, 0:D]).then_inc(empty_out, 16)
            sp.wait_ge(in_x, 16 * 17)
            sp.wait_ge(empty_out, 32)

        @block.gpsimd
        def _(pool):
            nc.gpsimd.memset(g["ident"][:, :], 0.0).then_inc(id_set, 1)
            nc.gpsimd.memset(g["identb"][:, :], 0.0).then_inc(id_set, 1)
            nc.gpsimd.memset(g["mask_t"][:, :], 0.0).then_inc(id_set, 1)
            nc.gpsimd.memset(g["mask_n"][:, :], 0.0).then_inc(id_set, 1)
            nc.gpsimd.memset(g["before"][:, :], 1.0).then_inc(id_set, 1)
            pool.wait_ge(id_set, 5)
            for m in ("ident", "identb"):
                nc.gpsimd.affine_select(out=g[m][:, :], in_=g[m][:, :], compare_op=ALU.not_equal, fill=1.0, base=0,
                                        pattern=[[-1, P]], channel_multiplier=1).then_inc(const_set, 1)
            nc.gpsimd.affine_select(out=g["mask_t"][:, :], in_=g["mask_t"][:, :], compare_op=ALU.is_ge, fill=MASKED,
                                    base=0, pattern=[[1, P]], channel_multiplier=-1).then_inc(const_set, 1)
            nc.gpsimd.affine_select(out=g["mask_n"][:, :], in_=g["mask_n"][:, :], compare_op=ALU.is_ge, fill=MASKED,
                                    base=0, pattern=[[-1, P]], channel_multiplier=1).then_inc(const_set, 1)
            nc.gpsimd.affine_select(out=g["before"][:, :], in_=g["before"][:, :], compare_op=ALU.is_gt, fill=0.0,
                                    base=0, pattern=[[1, P]], channel_multiplier=-1).then_inc(const_set, 1)
            nc.gpsimd.iota(g["tok"][:, :], pattern=[[P, TT]], base=0, channel_multiplier=1).then_inc(const_set, 1)
            nc.gpsimd.iota(g["slot0"][:, :, :], pattern=[[0, TT], [CAP, NE]], base=-FAR, channel_multiplier=0).then_inc(const_set, 1)
            nc.gpsimd.iota(g["prio"][:, :, :], pattern=[[0, TT], [-1, NE]], base=NE, channel_multiplier=0).then_inc(const_set, 1)
            nc.gpsimd.iota(none_tok[:, :, :], pattern=[[1, SLOTS // P], [0, 1]], base=B * S,
                           channel_multiplier=SLOTS // P).then_inc(const_set, 1)
            pool.wait_ge(const_set, 9)

        @block.vector
        def _(dve):
            nc.vector.memset(empty[:, :, :], 0.0).then_inc(empty_set, 1)
            dve.wait_ge(empty_set, 1)
            dve.wait_ge(const_set, 9)
            nc.vector.tensor_copy(empty[:, :, D + 1:D + 2].bitcast(I32), none_tok[:, :, :]).then_inc(empty_set, 1)
            nc.vector.memset(wkB[:, :, :], 0.0)
            nc.vector.memset(wvB[:, :, :], 0.0).then_inc(zero_set, 1)
            nc.vector.memset(g["ones"][:, :], 1.0)
            nc.vector.memset(g["onesb"][:, :], 1.0).then_inc(zero_set, 1)
            for n in range(4):
                dve.wait_ge(wqT_tr, n + 1)
                nc.vector.tensor_copy(wqT[:, 2 * n:2 * n + 2, :], pA[:, n, :].rearrange("p (a b) -> p a b", a=2)).then_inc(wqT_done, 1)
            dve.wait_ge(zero_set, 1)
            for n, dst in enumerate((wkB, wvB)):
                dve.wait_ge(up_tr, n + 1)
                for a in range(2):
                    last = nc.vector.tensor_copy(dst[a * HD:(a + 1) * HD, :, a * LD:(a + 1) * LD],
                                                 pB[a * HD:(a + 1) * HD, n, :].rearrange("p (g c) -> p g c", g=PAIRS))
                last.then_inc(up_done, 1)
            dve.wait_ge(rw_tr, 1)
            nc.vector.tensor_copy(g["rwT"][:, :, :], pB[:, 2, 0:DC * NE].rearrange("p (c e) -> p c e", c=DC)).then_inc(rw_done, 1)
            for n in range(4):
                dve.wait_ge(wt_mm, n + 1)
                nc.vector.tensor_copy(g["wt"][:, n // 2, (n % 2) * 512:(n % 2) * 512 + 512], pA[:, n, :]).then_inc(wt_done, 1)
            for n in range(4):
                dve.wait_ge(wvo_mm, n + 1)
                nc.vector.tensor_copy(g["wvo"][:, 2 * n:2 * n + 2, :], pB[:, n, :].rearrange("p (a b) -> p a b", a=2)).then_inc(wvo_done, 1)
            dve.wait_ge(wvo_done, 4)

        @block.tensor
        def _(pe):
            pe.wait_ge(const_set, 2)
            pe.wait_ge(in_wq, 16)
            for n in range(4):
                for a in range(2):
                    for c in range(DC):
                        last = nc.tensor.transpose(pA[:, n, a * D + c * P:a * D + (c + 1) * P],
                                                   wq[:, c, (2 * n + a) * P:(2 * n + a + 1) * P], g["ident"][:, :])
                last.then_inc(wqT_tr, 1)
            pe.wait_ge(in_up, 32)
            for n, w in enumerate((wk, wv)):
                for q in range(PAIRS):
                    last = nc.tensor.transpose(pB[:, n, q * LD:(q + 1) * LD], w[:, q * P:(q + 1) * P], g["ident"][0:LD, 0:LD])
                last.then_inc(up_tr, 1)
            pe.wait_ge(in_rw, 16)
            for c in range(DC):
                last = nc.tensor.transpose(pB[:, 2, c * NE:(c + 1) * NE], rw[:, c * P:(c + 1) * P], g["ident"][0:NE, 0:NE])
            last.then_inc(rw_tr, 1)
            pe.wait_ge(wqT_done, 4)
            pe.wait_ge(up_done, 2)
            for n in range(4):
                for q in range(4):
                    pair = (n % 2) * 4 + q
                    last = nc.tensor.matmul(pA[:, n, q * P:(q + 1) * P], wqT[:, pair, (n // 2) * P:(n // 2 + 1) * P],
                                            wkB[:, pair, :], start=True, stop=True)
                last.then_inc(wt_mm, 1)
            pe.wait_ge(in_wo, 16)
            pe.wait_ge(rw_done, 1)
            for n in range(4):
                for a in range(2):
                    last = nc.tensor.matmul(pB[:, n, a * D:(a + 1) * D], wvB[:, 2 * n + a, :], wo[:, 2 * n + a, :],
                                            start=True, stop=True)
                last.then_inc(wvo_mm, 1)


def latent_stage(nc, g, i):
    with ExitStack() as ctx:
        r = Resources(nc, ctx)
        x = r.sb("a_x", [P, TT, D], F32)
        xn = r.sb("a_xn", [P, TT, D], F32)
        xnT = r.sb("a_xnT", [P, DC, S], F32)
        w = ln_work(r, "a")
        qh = r.sb("a_qh", [P, PAIRS, S], F32R)
        ql = r.sb("a_ql", [P, PAIRS, S], F32R)
        lh = r.sb("a_lh", [P, S], F32R)
        ll = r.sb("a_ll", [LD, S], F32R)
        v = r.sb("a_v", [P, TT, LD], F32)
        pT = r.ps("a_pT", [P, DC, S])
        pL = r.ps("a_pL", [P, S])
        pV = r.ps("a_pV", [P, TT, LD])
        pQ = r.ps("a_pQ", [P, 4, S])
        x_in, chain_s, xn_ready, tr_done, xnT_ready = (r.sem(n) for n in ("a_x_in", "a_chain", "a_xn_ready", "a_tr_done", "a_xnT_ready"))
        lat_done, v_done, q_done, high, low, v_ready = (r.sem(n) for n in ("a_lat_done", "a_v_done", "a_q_done", "a_high", "a_low", "a_v_ready"))
        stored, passed = r.sem("a_stored"), r.sem("a_passed")
        block = ctx.enter_context(nc.Block())
        JOBS = PAIRS + 1
        STORES = 5

        @block.sync
        def _(sp):
            def batch(b):
                at_least(sp, xn_ready, b)
                sp.dma_start(x[:, :, :], i["x"][b].rearrange("(t p) d -> p t d", p=P)).then_inc(x_in, 16)

            batches(sp, batch)

        @block.vector
        def _(dve):
            def batch(b):
                chain = Chain(dve, chain_s, b * LN_LINKS, passed)
                at_least(dve, x_in, b * 16 + 16)
                at_least(dve, tr_done, b)
                layer_norm(nc, chain, x, xn, w).then_inc(xn_ready, 1)
                at_least(dve, stored, b * 16 * STORES)
                at_least(dve, high, b * JOBS + 1)
                nc.vector.tensor_tensor(ll[:, :], pL[0:LD, :], lh[0:LD, :].bitcast(F32), ALU.subtract).then_inc(low, 1)
                at_least(dve, v_done, b + 1)
                nc.vector.tensor_copy(v[:, :, :], pV[:, :, :]).then_inc(v_ready, 1)
                for q in range(PAIRS):
                    at_least(dve, high, b * JOBS + q + 2)
                    nc.vector.tensor_tensor(ql[:, q, :], pQ[:, q % 4, :], qh[:, q, :].bitcast(F32), ALU.subtract).then_inc(low, 1)

            batches(dve, batch)

        @block.scalar
        def _(act):
            def batch(b):
                at_least(act, tr_done, b + 1)
                at_least(act, q_done, b * PAIRS)
                for d in range(DC):
                    nc.scalar.activation(xnT[:, d, :], pT[:, d, :], ACT.Copy).then_inc(xnT_ready, 1)
                at_least(act, stored, b * 16 * STORES)
                at_least(act, lat_done, b + 1)
                nc.scalar.activation(lh[:, :], pL[:, :], ACT.Copy).then_inc(high, 1)
                for q in range(PAIRS):
                    at_least(act, q_done, b * PAIRS + q + 1)
                    nc.scalar.activation(qh[:, q, :], pQ[:, q % 4, :], ACT.Copy).then_inc(high, 1)

            batches(act, batch)

        @block.tensor
        def _(pe):
            def batch(b):
                at_least(pe, xn_ready, b + 1)
                at_least(pe, xnT_ready, b * DC)
                transpose_tokens(nc, xn, g["ident"], pT).then_inc(tr_done, 1)
                at_least(pe, xnT_ready, b * DC + DC)
                at_least(pe, low, b * JOBS)
                for d in range(DC):
                    last = nc.tensor.matmul(pL[:, :], g["wdd"][:, d, :, :], xnT[:, d, :], start=d == 0, stop=d == DC - 1)
                last.then_inc(lat_done, 1)
                at_least(pe, v_ready, b)
                for t in range(TT):
                    for d in range(DC):
                        last = nc.tensor.matmul(pV[:, t, :], xnT[:, d, t * P:(t + 1) * P], g["wdd"][:, d, 0, :],
                                                start=d == 0, stop=d == DC - 1)
                last.then_inc(v_done, 1)
                for q in range(PAIRS):
                    if q >= 4:
                        at_least(pe, low, b * JOBS + q - 2)
                    for d in range(DC):
                        last = nc.tensor.matmul(pQ[:, q % 4, :], g["wt"][:, d, q * P:(q + 1) * P], xnT[:, d, :],
                                                start=d == 0, stop=d == DC - 1)
                    last.then_inc(q_done, 1)

            batches(pe, batch)

        @block.gpsimd
        def _(pool):
            def batch(b):
                at_least(pool, v_ready, b + 1)
                pool.dma_start(g["lat_h"][b], lh[:, :].bitcast(F32)).then_inc(stored, 16)
                pool.dma_start(g["lat_l"][b], ll[:, :].bitcast(F32)).then_inc(stored, 16)
                pool.dma_start(g["lat_v"][b], v[:, :, :]).then_inc(stored, 16)
                at_least(pool, low, b * JOBS + JOBS)
                pool.dma_start(g["q0h"][bass.ds(b * PAIRS, PAIRS)].rearrange("q p n -> p q n"), qh[:, :, :].bitcast(F32)).then_inc(stored, 16)
                pool.dma_start(g["q0l"][bass.ds(b * PAIRS, PAIRS)].rearrange("q p n -> p q n"), ql[:, :, :].bitcast(F32)).then_inc(stored, 16)

            batches(pool, batch)
            pool.wait_ge(stored, B * 16 * STORES)


def latent_attention(nc, g):
    with ExitStack() as ctx:
        r = Resources(nc, ctx)
        K = 4
        q1 = [r.sb(f"b_q1_{k}", [P, 2, S], F32R) for k in range(K)]
        R = 96
        q2 = [r.sb(f"b_q2_{k}", [R + 1, 2, S], F32R) for k in range(K)]
        k1 = [r.sb(f"b_k1_{k}", [P, S], F32R) for k in range(K)]
        k2 = [r.sb(f"b_k2_{k}", [R + 1, S], F32R) for k in range(K)]
        v = [r.sb(f"b_v_{k}", [P, TT, LD], F32) for k in range(K)]
        negm = [r.sb(f"b_negm_{k}", [P, 2 * TT], F32) for k in range(K)]
        mT = [r.sb(f"b_mT_{k}", [2 * TT, P], F32R) for k in range(K)]
        z = [r.sb(f"b_z_{k}", [P, S], F32) for k in range(K)]
        prob = r.sb("b_prob", [P, TT, 2, S], F32)
        y = [r.sb(f"b_y_{k}", [P, 2, S], F32) for k in range(2)]
        rec = [r.sb(f"b_rec_{k}", [P, S], F32) for k in range(2)]
        pM = r.ps("b_pM", [P, 2, S])
        pS = r.ps("b_pS", [P, 2, 2, S])
        pY = r.ps("b_pY", [P, 2, S])
        loaded, row_in, stored = ([r.sem(f"b_{n}_{k}") for k in range(K)] for n in ("loaded", "row_in", "stored"))
        ones_set, max_mm, max_red, mT_ready = (r.sem(n) for n in ("b_ones_set", "b_max_mm", "b_max_red", "b_mT_ready"))
        st_done, exp_done, pv_done, y_ready, rec_done, z_ready = (r.sem(n) for n in (
            "b_st_done", "b_exp_done", "b_pv_done", "b_y_ready", "b_rec_done", "b_z_ready"))
        block = ctx.enter_context(nc.Block())
        STEPS = B * PAIRS
        MJ = 2 * TT + 1
        LOADS = 6

        PIECES = 4

        def is_first(it):
            return isinstance(it, int) and it == 0

        def steps(engine, body):
            slotted_steps(engine, STEPS, K, body)

        @block.sync
        def _(sp):
            def load(it, k):
                for src, dst in ((g["q0h"], q1[k][0:LD]), (g["q0l"], q1[k][LD:P]), (g["q0h"], q2[k][0:LD])):
                    sp.dma_start(dst.bitcast(F32), src[it].rearrange("(a d) n -> d a n", a=2)).then_inc(loaded[k], 16)
                sp.dma_start(k1[k][:, :].bitcast(F32), g["lat_h"][it // PAIRS]).then_inc(loaded[k], 16)
                sp.dma_start(k2[k][0:LD, :].bitcast(F32), g["lat_l"][it // PAIRS]).then_inc(loaded[k], 16)
                sp.dma_start(v[k][:, :, :], g["lat_v"][it // PAIRS]).then_inc(loaded[k], 16)

            def row(it, k):
                sp.wait_ge(mT_ready, it + 1)
                sp.dma_start(q2[k][R:R + 1, :, :].bitcast(F32), mT[k][:, :].bitcast(F32)).then_inc(row_in[k], 16)

            sp.wait_ge(ones_set, 1)
            for n in range(3):
                load(n, n)
            row(0, 0)
            row(1, 1)

            def body(it, k, follow):
                if follow >= 3:
                    at_least(sp, pv_done, it * TT)
                    load(it + 3, (k + 3) % K)
                if follow >= 2:
                    row(it + 2, (k + 2) % K)

            steps(sp, body)

        @block.gpsimd
        def _(pool):
            def body(it, k, follow):
                pool.wait_ge(rec_done, PIECES * it + PIECES)
                at_least(pool, stored[k], (it // K) * 16)
                nc.gpsimd.tensor_tensor(z[k][:, :], y[k % 2][:, 0, :], rec[k % 2][:, :], ALU.mult).then_inc(z_ready, 1)
                pool.wait_ge(z_ready, it + 1)
                pool.dma_start(g["z0"][it], z[k][:, :]).then_inc(stored[k], 16)

            steps(pool, body)
            for k in range(K):
                pool.wait_ge(stored[k], 16 * STEPS // K)

        @block.vector
        def _(dve):
            for k in range(K):
                for stack in (q2[k][LD:R, :, :], k2[k][LD:R, :]):
                    last = nc.vector.memset(stack.bitcast(F32), 0.0)
                last = nc.vector.memset(k2[k][R:R + 1, :].bitcast(F32), 1.0)
            last.then_inc(ones_set, 1)

            def read_max(it, k, j):
                slot = (k * MJ + j) % 2
                dve.wait_ge(max_mm, it * MJ + j + 1)
                if j < 2 * TT:
                    nc.vector.tensor_reduce(negm[k][:, j:j + 1], pM[:, slot, 0:P * (j % TT + 1)], AX.X, ALU.max,
                                            negate=True).then_inc(max_red, 1)
                else:
                    nc.vector.tensor_copy(mT[k][:, :], pM[0:2 * TT, slot, 0:P]).then_inc(mT_ready, 1)

            def reciprocals(it, k, piece):
                if piece == 0:
                    dve.wait_ge(y_ready, it + 1)
                part = slice(piece * S // PIECES, (piece + 1) * S // PIECES)
                nc.vector.reciprocal(rec[k % 2][:, part], y[k % 2][:, 1, part]).then_inc(rec_done, 1)

            for n in range(2):
                for j in range(MJ):
                    read_max(n, n, j)

            def body(it, k, follow):
                for j in range(MJ):
                    if follow >= 2:
                        read_max(it + 2, (k + 2) % K, j)
                    if not is_first(it) and j % 2 == 1:
                        reciprocals(it - 1, k - 1, j // 2)

            steps(dve, body)
            for piece in range(PIECES):
                reciprocals(STEPS - 1, K - 1, piece)

        @block.scalar
        def _(act):
            def copy_sums(it, k):
                act.wait_ge(pv_done, it * TT + TT)
                at_least(act, z_ready, it - 1)
                nc.scalar.activation(y[k % 2][:, :, :], pY[:, :, :], ACT.Copy).then_inc(y_ready, 1)

            def body(it, k, follow):
                for j in range(TT):
                    act.wait_ge(st_done, it * TT + j + 1)
                    nc.scalar.activation(prob[:, j, :, P * j:S], pS[:, j % 2, :, P * j:S], ACT.Exp, scale=HD ** -0.5).then_inc(exp_done, 1)
                    if j == 0 and not is_first(it):
                        copy_sums(it - 1, k - 1)

            steps(act, body)
            copy_sums(STEPS - 1, K - 1)

        @block.tensor
        def _(pe):
            def max_job(it, k, j):
                slot = (k * MJ + j) % 2
                if j == 0:
                    pe.wait_ge(loaded[k], (it // K) * (16 * LOADS) + 16 * LOADS)
                if not (isinstance(it, int) and it == 0 and j < 2):
                    if j >= 2:
                        pe.wait_ge(max_red, it * (MJ - 1) + j - 1)
                    elif j == 1:
                        pe.wait_ge(mT_ready, it)
                    else:
                        pe.wait_ge(max_red, it * (MJ - 1))
                if j < 2 * TT:
                    h, t = j // TT, j % TT
                    nc.tensor.matmul(pM[:, slot, 0:P * (t + 1)], q1[k][:, h, t * P:(t + 1) * P], k1[k][:, 0:P * (t + 1)],
                                     start=True, stop=False)
                    nc.tensor.matmul(pM[:, slot, P * t:P * (t + 1)], g["identb"][:, :], g["mask_n"][:, :],
                                     start=False, stop=True).then_inc(max_mm, 1)
                else:
                    pe.wait_ge(max_red, it * (MJ - 1) + MJ - 1)
                    nc.tensor.transpose(pM[0:2 * TT, slot, 0:P], negm[k][:, :], g["ident"][:, :]).then_inc(max_mm, 1)

            for n in range(2):
                for j in range(MJ):
                    max_job(n, n, j)

            def scores(it, k, j, then):
                if j == 0:
                    pe.wait_ge(row_in[k], (it // K) * 16 + 16)
                if j >= 2:
                    pe.wait_ge(exp_done, it * TT + j - 1)
                for h in range(2):
                    out = pS[:, j % 2, h, P * j:S]
                    nc.tensor.matmul(out, k1[k][:, P * j:P * (j + 1)], q1[k][:, h, P * j:S], start=True, stop=False)
                    nc.tensor.matmul(out, k2[k][:, P * j:P * (j + 1)], q2[k][:, h, P * j:S], start=False, stop=False)
                    last = nc.tensor.matmul(pS[:, j % 2, h, P * j:P * (j + 1)], g["identb"][:, :], g["mask_t"][:, :],
                                            start=False, stop=True)
                    if h == 1:
                        last.then_inc(st_done, 1)
                    then(1)

            def values(it, k, j):
                pe.wait_ge(exp_done, it * TT + j + 1)
                if j == 0:
                    at_least(pe, y_ready, it)
                for n, w in enumerate((v[k][:, j, :], g["ones"][:, 0:LD])):
                    for h in range(2):
                        last = nc.tensor.matmul(pY[h * LD:(h + 1) * LD, n, P * j:S], w, prob[:, j, h, P * j:S],
                                                start=j == 0, stop=j == TT - 1)
                last.then_inc(pv_done, 1)

            def body(it, k, follow):
                made = 0

                def some(n):
                    nonlocal made
                    for j in range(made, min(made + n, MJ if follow >= 2 else 0)):
                        max_job(it + 2, (k + 2) % K, j)
                    made += n

                scores(it, k, 0, some)
                scores(it, k, 1, some)
                values(it, k, 0)
                some(1)
                scores(it, k, 2, some)
                values(it, k, 1)
                scores(it, k, 3, some)
                values(it, k, 2)
                values(it, k, 3)

            steps(pe, body)


def cross_stage(nc, g, i):
    with ExitStack() as ctx:
        r = Resources(nc, ctx)
        z = r.sb("c_z", [P, PAIRS, S], F32)
        x = r.sb("c_x", [P, TT, D], F32)
        xn = r.sb("c_xn", [P, TT, D], F32)
        xnT = r.sb("c_xnT", [P, DC, S], F32)
        c = r.sb("c_ctx", [P, CT, CW], F32)
        cT = r.sb("c_ctxT", [P, SC], F32)
        w = ln_work(r, "c")
        sh = r.sb("c_sh", [P, 3, DC, S], F32R)
        sl = r.sb("c_sl", [P, 3, DC, S], F32R)
        ch = r.sb("c_ch", [P, DC, SCP], F32R)
        cl = r.sb("c_cl", [P, DC, SCP], F32R)
        vx = r.sb("c_vx", [P, CH, H1, 2 * HW], F32)
        pO = r.ps("c_pO", [P, TT, D])
        pT = r.ps("c_pT", [P, DC, S])
        pJ = r.ps("c_pJ", [P, 4, 512])
        z_in, x_in, c_in, chain_s, ones_set = (r.sem(n) for n in ("c_z_in", "c_x_in", "c_c_in", "c_chain", "c_ones_set"))
        o_done, xn_ready, tr_done, xnT_ready = (r.sem(n) for n in ("c_o_done", "c_xn_ready", "c_tr_done", "c_xnT_ready"))
        job_done, high, low, vals, ctr = (r.sem(n) for n in ("c_job_done", "c_high", "c_low", "c_vals", "c_ctr"))
        keys_out, cvals_out, vals_out, passed = (r.sem(n) for n in ("c_keys_out", "c_cvals_out", "c_vals_out", "c_passed"))
        splits_out = [r.sem(f"c_splits_out_{t}") for t in range(3)]
        block = ctx.enter_context(nc.Block())

        jobs = [("ctx", n) for n in range(-(-CT // 4))]
        jobs += [("key", m, n) for m in range(DC) for n in range(4)]
        jobs += [("cval", n) for n in range(-(-CT // 2))]
        jobs += [("split", t, m) for t in range(3) for m in range(DC)]
        jobs += [("val", n) for n in range(TT // 2)]
        NJ = len(jobs)
        kinds = {"ctx": ("ctx",), "split": ("key", "split"), "value": ("cval", "val")}

        def count(kind, upto):
            return sum(1 for q in jobs[:upto] if q[0] in kinds[kind])

        NCTX, NSPL, NVAL = (count(n, NJ) for n in ("ctx", "split", "value"))
        NCOL = [(0, 400), (400, 400), (800, 400), (1200, 401)]
        NKEY, NCV = sum(q[0] == "key" for q in jobs), sum(q[0] == "cval" for q in jobs)

        def freed(engine, b, n):
            kind = jobs[n][0]
            if kind == "ctx":
                engine.wait_ge(ctr, b * NCTX + count("ctx", n + 1))
            elif kind in ("key", "split"):
                engine.wait_ge(low, b * NSPL + count("split", n + 1))
            else:
                engine.wait_ge(vals, b * NVAL + count("value", n + 1))

        @block.sync
        def _(sp):
            def load_context(b):
                sp.dma_start(c[:, 0:CT - 1, :], i["ctx"][b, 0:(CT - 1) * P].rearrange("(t p) d -> p t d", p=P)).then_inc(c_in, 16)
                sp.dma_start(c[0:LAST, CT - 1, :], i["ctx"][b, (CT - 1) * P:SC]).then_inc(c_in, 16)

            def load_z(b):
                sp.dma_start(z[:, :, :], g["z0"][bass.ds(b * PAIRS, PAIRS)].rearrange("q p n -> p q n")).then_inc(z_in, 16)

            def load_x(b):
                sp.dma_start(x[:, :, :], i["x"][b].rearrange("(t p) d -> p t d", p=P)).then_inc(x_in, 16)

            def batch(b, follow):
                if follow:
                    wait_apart(sp, passed, ctr, b * NCTX + NCTX)
                    load_context(b + 1)
                    wait_apart(sp, passed, o_done, b + 1)
                    load_z(b + 1)
                    wait_apart(sp, passed, xn_ready, b + 1)
                    load_x(b + 1)
                wait_apart(sp, passed, low, b * NSPL + NKEY)
                for src, dst in ((ch, g["c1h"]), (cl, g["c1l"])):
                    view = dst[bass.ds(b * QUADS, QUADS)].rearrange("(m a) r n -> (a r) m n", a=2)
                    sp.dma_start(view[:, :, 0:SC], src[:, :, 0:SC].bitcast(F32)).then_inc(keys_out, 16)
                    sp.dma_start(view[:, :, SC:SCP], src[:, :, SC - 1:SC].bitcast(F32), allow_slow_non_contiguous=True).then_inc(keys_out, 16)
                wait_apart(sp, passed, vals, b * NVAL + NCV)
                sp.wait_ge(ones_set, 1)
                for q in range(QUADS):
                    view = g["v1"][b * QUADS + q].rearrange("p c (h n) -> p c h n", h=4)
                    sp.dma_start(view[:, TT:CH - 1], vx[:, TT:CH - 1, 4 * q:4 * q + 4, :]).then_inc(cvals_out, 16)
                    sp.dma_start(view[0:LAST, CH - 1], vx[0:LAST, CH - 1, 4 * q:4 * q + 4, :]).then_inc(cvals_out, 16)
                for t in range(3):
                    wait_apart(sp, passed, low, b * NSPL + NKEY + (t + 1) * DC)
                    for src, dst in ((sh, g["s1h"]), (sl, g["s1l"])):
                        sp.dma_start(dst[t, bass.ds(b * QUADS, QUADS)].rearrange("(m a) r n -> (a r) m n", a=2),
                                     src[:, t, :, :].bitcast(F32)).then_inc(splits_out[t], 16)
                wait_apart(sp, passed, vals, b * NVAL + NVAL)
                for q in range(QUADS):
                    view = g["v1"][b * QUADS + q].rearrange("p c (h n) -> p c h n", h=4)
                    sp.dma_start(view[:, 0:TT], vx[:, 0:TT, 4 * q:4 * q + 4, :]).then_inc(vals_out, 16)

            load_context(0)
            load_z(0)
            load_x(0)
            with sp.Fori(0, B - 1) as b:
                batch(b, True)
            batch(B - 1, False)
            sp.wait_ge(keys_out, B * 64)
            sp.wait_ge(cvals_out, B * 32 * QUADS)
            for t in range(3):
                sp.wait_ge(splits_out[t], B * 32)
            sp.wait_ge(vals_out, B * 16 * QUADS)

        @block.gpsimd
        def _(pool):
            nc.gpsimd.memset(vx[:, :, :, HW:2 * HW], 1.0).then_inc(ones_set, 1)

        @block.scalar
        def _(act):
            def batch(b):
                for n, job in enumerate(jobs):
                    if job[0] == "ctx":
                        if n == 0:
                            at_least(act, job_done, b * NJ)
                        at_least(act, job_done, b * NJ + n + 1)
                        lo, hi = job[1] * 512, min(SC, job[1] * 512 + 512)
                        nc.scalar.activation(cT[:, lo:hi], pJ[:, n % 4, 0:hi - lo], ACT.Copy).then_inc(ctr, 1)
                    if job == ("split", 0, 0):
                        at_least(act, tr_done, b + 1)
                        for d in range(DC):
                            nc.scalar.activation(xnT[:, d, :], pT[:, d, :], ACT.Copy).then_inc(xnT_ready, 1)
                    if job[0] in ("key", "split"):
                        if job == ("key", 0, 0):
                            at_least(act, keys_out, b * 64)
                        if job[0] == "split" and job[2] == 0:
                            at_least(act, splits_out[job[1]], b * 32)
                        at_least(act, job_done, b * NJ + n + 1)
                        if job[0] == "key":
                            lo, wd = NCOL[job[2]]
                            dst, src, bias = ch[:, job[1], lo:lo + wd], pJ[:, n % 4, 0:wd], g["bias_col"][:, 3, job[1]:job[1] + 1]
                        else:
                            dst, src, bias = sh[:, job[1], job[2], :], pJ[:, n % 4, :], g["bias_col"][:, job[1], job[2]:job[2] + 1]
                        nc.scalar.activation(dst, src, ACT.Identity, bias=bias).then_inc(high, 1)

            batches(act, batch)

        @block.vector
        def _(dve):
            dve.wait_ge(ones_set, 1)
            def batch(b):
                chain = Chain(dve, chain_s, b * (LN_LINKS + 1), passed)

                def norm():
                    at_least(dve, x_in, b * 16 + 16)
                    at_least(dve, o_done, b + 1)
                    at_least(dve, tr_done, b)
                    res = g["x_res"][:, bass.ds(b * (TT * D), TT * D)]
                    chain.link(nc.vector.tensor_tensor(x[:, :, :].rearrange("p t d -> p (t d)"), x[:, :, :].rearrange("p t d -> p (t d)"),
                                                       pO[:, :, :].rearrange("p t d -> p (t d)"), ALU.add))
                    nc.vector.tensor_copy(res, x[:, :, :].rearrange("p t d -> p (t d)"))
                    layer_norm(nc, chain, x, xn, w).then_inc(xn_ready, 1)

                for n, job in enumerate(jobs):
                    if n == 4:
                        norm()
                    if job[0] in ("key", "split"):
                        at_least(dve, high, b * NSPL + count("split", n + 1))
                        if job[0] == "key":
                            lo, wd = NCOL[job[2]]
                            dst, hi_, src, bias = (cl[:, job[1], lo:lo + wd], ch[:, job[1], lo:lo + wd], pJ[:, n % 4, 0:wd],
                                                   g["bias_col"][:, 3, job[1]:job[1] + 1])
                        else:
                            dst, hi_, src, bias = (sl[:, job[1], job[2], :], sh[:, job[1], job[2], :], pJ[:, n % 4, :],
                                                   g["bias_col"][:, job[1], job[2]:job[2] + 1])
                        nc.vector.scalar_tensor_tensor(out=dst, in0=src, scalar=bias, in1=hi_.bitcast(F32),
                                                       op0=ALU.add, op1=ALU.subtract).then_inc(low, 1)
                    if job[0] in ("cval", "val"):
                        if job[1] == 0:
                            done, each = (cvals_out, 32) if job[0] == "cval" else (vals_out, 16)
                            at_least(dve, done, b * each * QUADS)
                        at_least(dve, job_done, b * NJ + n + 1)
                        for a in range(2):
                            tile = 2 * job[1] + a
                            if job[0] == "cval" and tile >= CT:
                                continue
                            rows = LAST if job[0] == "cval" and tile == CT - 1 else P
                            at, row = (tile + TT, 1) if job[0] == "cval" else (tile, 0)
                            last = nc.vector.tensor_tensor(
                                vx[0:rows, at, :, 0:HW], pJ[0:rows, n % 4, a * D:(a + 1) * D].rearrange("p (h n) -> p h n", h=H1),
                                g["bias_row"][0:rows, row, :].rearrange("p (h n) -> p h n", h=H1), ALU.add)
                        last.then_inc(vals, 1)

            batches(dve, batch)

        @block.tensor
        def _(pe):
            def batch(b):
                for n, job in enumerate(jobs):
                    if n >= 4:
                        freed(pe, b, n - 4)
                    if n == 0:
                        at_least(pe, c_in, b * 32 + 32)
                        at_least(pe, low, b * NSPL)
                        at_least(pe, vals, b * NVAL)
                    slot = pJ[:, n % 4, :]
                    if job[0] == "ctx":
                        for q in range(4):
                            t = job[1] * 4 + q
                            if t < CT:
                                rows = P if t < CT - 1 else LAST
                                last = nc.tensor.transpose(slot[:, q * P:q * P + rows], c[0:rows, t, :], g["ident"][0:rows, 0:rows])
                        last.then_inc(job_done, 1)
                    if n == 3:
                        at_least(pe, z_in, b * 16 + 16)
                        at_least(pe, xn_ready, b)
                        for t in range(TT):
                            for q in range(PAIRS):
                                last = nc.tensor.matmul(pO[:, t, :], z[:, q, t * P:(t + 1) * P], g["wvo"][:, q, :],
                                                        start=q == 0, stop=q == PAIRS - 1)
                        last.then_inc(o_done, 1)
                    if job[0] == "key":
                        at_least(pe, ctr, b * NCTX + NCTX)
                        lo, wd = NCOL[job[2]]
                        nc.tensor.matmul(slot[:, 0:wd], g["xWck"][:, job[1] * P:(job[1] + 1) * P], cT[:, lo:lo + wd],
                                         start=True, stop=True).then_inc(job_done, 1)
                    if job[0] == "cval":
                        for a in range(2):
                            t = 2 * job[1] + a
                            if t < CT:
                                rows = P if t < CT - 1 else LAST
                                last = nc.tensor.matmul(slot[0:rows, a * D:(a + 1) * D], cT[:, t * P:t * P + rows], g["xWcv"][:, :],
                                                        start=True, stop=True)
                        last.then_inc(job_done, 1)
                    if job == ("split", 0, 0):
                        at_least(pe, xn_ready, b + 1)
                        at_least(pe, xnT_ready, b * DC)
                        transpose_tokens(nc, xn, g["ident"], pT).then_inc(tr_done, 1)
                        at_least(pe, xnT_ready, b * DC + DC)
                    if job[0] == "split":
                        wt = g[("xWq", "xWk", "xWcq")[job[1]]]
                        for d in range(DC):
                            last = nc.tensor.matmul(slot, wt[:, d, job[2] * P:(job[2] + 1) * P], xnT[:, d, :],
                                                    start=d == 0, stop=d == DC - 1)
                        last.then_inc(job_done, 1)
                    if job[0] == "val":
                        for a in range(2):
                            t = 2 * job[1] + a
                            for d in range(DC):
                                last = nc.tensor.matmul(slot[:, a * D:(a + 1) * D], xnT[:, d, t * P:(t + 1) * P], g["xWv"][:, d, :],
                                                        start=d == 0, stop=d == DC - 1)
                        last.then_inc(job_done, 1)

            batches(pe, batch)


def mixed_attention(nc, g):
    with ExitStack() as ctx:
        r = Resources(nc, ctx)
        K = 2
        R = 96
        qs = [r.sb(f"d_qs_{k}", [R + 1, 4, S], F32R) for k in range(K)]
        ks = [r.sb(f"d_ks_{k}", [R + 1, 4, S], F32R) for k in range(K)]
        qc = [r.sb(f"d_qc_{k}", [R + 1, 4, S], F32R) for k in range(K)]
        kc = [r.sb(f"d_kc_{k}", [R + 1, 4, SCP], F32R) for k in range(K)]
        v = [r.sb(f"d_v_{k}", [P, CH, 4 * 2 * HW], F32) for k in range(K)]
        part = [r.sb(f"d_part_{k}", [P, 4 * TT, 4], F32) for k in range(K)]
        negm = [r.sb(f"d_negm_{k}", [P, 8 * TT], F32) for k in range(K)]
        mT = [r.sb(f"d_mT_{k}", [4 * TT, 2, P], F32R) for k in range(K)]
        z = [r.sb(f"d_z_{k}", [P, TT * 4, HW], F32) for k in range(K)]
        prob = r.sb("d_prob", [P, 2, 4, S], F32)
        y = r.sb("d_y", [P, 2, S], F32)
        rec = r.sb("d_rec", [P, 2, TT * 4], F32)
        mean = r.sb("d_mean", [P, TT * 4, HW], F32)
        RING = 3
        pM = r.ps("d_pM", [P, RING, S])
        pS = r.ps("d_pS", [P, 2, 2, S])
        pY = r.ps("d_pY", [P, S])
        in_self, in_cross, in_v, self_row, cross_row, stored = (
            [r.sem(f"d_{n}_{k}") for k in range(K)] for n in ("in_self", "in_cross", "in_v", "self_row", "cross_row", "stored"))
        ones_set, job_done, job_read, comb = (r.sem(n) for n in ("d_ones_set", "d_job_done", "d_job_read", "d_comb"))
        st_done, exp_done, pv_done, y_ready, rec_done, mean_done, z_part = (r.sem(n) for n in (
            "d_st_done", "d_exp_done", "d_pv_done", "d_y_ready", "d_rec_done", "d_mean_done", "d_z_part"))
        block = ctx.enter_context(nc.Block())
        STEPS = B * QUADS
        SELF, NK = 4 * TT, len(KCOLS)
        MAXIMA = ([("self", n) for n in range(SELF)] + [("turn", 0)]
                  + [("cross", n) for n in range(SELF * NK)] + [("turn", 1)])
        MJ = len(MAXIMA)
        EARLY, LATE = 8, 44

        def is_first(it, n=0):
            return isinstance(it, int) and it == n

        def step_jobs(first, last):
            jobs = list(MAXIMA) if not last else []
            if not first:
                jobs.insert(min(EARLY, len(jobs)), ("sums", 1))
            jobs.insert(min(LATE, len(jobs)), ("sums", 0))
            return jobs

        def first_job(it):
            return MJ if is_first(it) else MJ - 1 + (MJ + 2) * it

        def turned(it, which):
            return first_job(it) + step_jobs(is_first(it), False).index(("turn", which)) + 1

        def before(it, n):
            if n >= RING:
                return RING
            jobs_before = MJ if is_first(it) else MJ + 1 if is_first(it, 1) else MJ + 2
            return n + jobs_before - max(m for m in range(jobs_before) if m % RING == n)

        def steps(engine, body):
            slotted_steps(engine, STEPS, K, body)

        @block.sync
        def _(sp):
            def stack(dst, parts, it, sem):
                for row, src in enumerate(parts):
                    sp.dma_start(dst[row * HW:(row + 1) * HW, :, :].bitcast(F32), src[it].rearrange("(h d) n -> d h n", h=4)).then_inc(sem, 16)

            def load_self(it, k):
                stack(qs[k], [g["s1h"][0], g["s1h"][0], g["s1l"][0], g["s1l"][0]], it, in_self[k])
                stack(ks[k], [g["s1h"][1], g["s1l"][1], g["s1h"][1], g["s1l"][1]], it, in_self[k])

            def load_cross(it, k):
                stack(qc[k], [g["s1h"][2], g["s1h"][2], g["s1l"][2], g["s1l"][2]], it, in_cross[k])
                stack(kc[k], [g["c1h"], g["c1l"], g["c1h"], g["c1l"]], it, in_cross[k])

            def load_v(it, k):
                sp.dma_start(v[k][:, 0:CH - 1, :], g["v1"][it][:, 0:CH - 1]).then_inc(in_v[k], 16)
                sp.dma_start(v[k][0:LAST, CH - 1, :], g["v1"][it][0:LAST, CH - 1]).then_inc(in_v[k], 16)

            def row(k, which):
                q, done = ((qs, self_row), (qc, cross_row))[which]
                sp.dma_start(q[k][R:R + 1, :, :].bitcast(F32), mT[k][:, which, :].bitcast(F32)).then_inc(done[k], 16)

            sp.wait_ge(ones_set, 1)
            for n in range(K):
                load_self(n, n)
                load_cross(n, n)
                load_v(n, n)
            sp.wait_ge(job_read, MJ)
            row(0, 0)
            row(0, 1)

            def body(it, k, follow):
                if follow >= 2:
                    sp.wait_ge(st_done, it * 2 * CH + 2 * TT)
                    load_self(it + 2, k)
                if follow >= 1:
                    sp.wait_ge(job_read, turned(it, 0))
                    row(1 - k, 0)
                    sp.wait_ge(job_read, turned(it, 1))
                    row(1 - k, 1)
                if follow >= 2:
                    sp.wait_ge(st_done, it * 2 * CH + 2 * CH)
                    load_cross(it + 2, k)
                    sp.wait_ge(pv_done, it * CH + CH)
                    load_v(it + 2, k)

            steps(sp, body)

        @block.gpsimd
        def _(pool):
            def body(it, k, follow):
                pool.wait_ge(z_part, 2 * it + 2)
                pool.dma_start(g["z1"][it], z[k][:, :, :].rearrange("p a b -> p (a b)")).then_inc(stored[k], 16)

            steps(pool, body)
            for k in range(K):
                pool.wait_ge(stored[k], 16 * STEPS // K)

        @block.vector
        def _(dve):
            for k in range(K):
                for stack in (qs, qc, ks, kc):
                    last = nc.vector.memset(stack[k][4 * HW:R, :, :].bitcast(F32), 0.0)
                for stack in (ks, kc):
                    last = nc.vector.memset(stack[k][R:R + 1, :, :].bitcast(F32), 1.0)
            last.then_inc(ones_set, 1)

            def read_max(k, kind, n, number, slot):
                dve.wait_ge(job_done, number + 1)
                if kind == "self":
                    nc.vector.tensor_reduce(negm[k][:, n:n + 1], pM[:, slot, 0:P * (n % TT + 1)], AX.X, ALU.max,
                                            negate=True).then_inc(job_read, 1)
                elif kind == "cross":
                    nc.vector.tensor_reduce(part[k][:, n // NK, n % NK:n % NK + 1], pM[:, slot, 0:KCOLS[n % NK][1]], AX.X,
                                            ALU.max, negate=True).then_inc(job_read, 1)
                    if n == SELF * NK - 1:
                        dve.wait_ge(job_read, number + 1)
                        nc.vector.tensor_reduce(negm[k][:, SELF:2 * SELF], part[k][:, :, :], AX.X, ALU.min).then_inc(comb, 1)
                else:
                    nc.vector.tensor_copy(mT[k][:, n, :], pM[0:SELF, slot, 0:P]).then_inc(job_read, 1)

            def read_sums(it, k, cross, number, slot):
                sums = pM[:, slot, :].rearrange("p (a b) -> p a b", b=2 * HW)
                dve.wait_ge(job_done, number + 1)
                nc.vector.reciprocal(rec[:, cross, :], sums[:, :, HW]).then_inc(rec_done, 1)
                dve.wait_ge(rec_done, 2 * it + cross + 1)
                factor = rec[:, cross, :].unsqueeze(2).broadcast_to([P, TT * 4, HW])
                if not cross:
                    at_least(dve, stored[k], it // K * 16)
                    nc.vector.tensor_tensor(z[k][:, :, :], sums[:, :, 0:HW], factor, ALU.mult).then_inc(job_read, 1)
                    dve.wait_ge(job_read, number + 1)
                    dve.sem_inc(z_part, 1)
                else:
                    nc.vector.tensor_tensor(mean[:, :, :], sums[:, :, 0:HW], factor, ALU.mult).then_inc(job_read, 1)
                    dve.wait_ge(job_read, number + 1)
                    nc.vector.tensor_tensor(z[k][:, :, :], z[k][:, :, :], mean[:, :, :], ALU.add).then_inc(z_part, 1)

            for number, (kind, n) in enumerate(MAXIMA):
                read_max(0, kind, n, number, number % RING)

            def body(it, k, follow):
                for n, (kind, m) in enumerate(step_jobs(is_first(it), follow == 0)):
                    number, slot = first_job(it) + n, n % RING
                    if kind != "sums":
                        read_max(1 - k, kind, m, number, slot)
                    else:
                        read_sums(it - m, 1 - k if m else k, m, number, slot)

            steps(dve, body)
            n = len(step_jobs(False, True))
            read_sums(STEPS - 1, (STEPS - 1) % K, 1, first_job(STEPS - 1) + n, n % RING)

        def chunk(c):
            if c < TT:
                return 0, c, c * P, P
            return 1, c - TT, 0, P if c < CH - 1 else LAST

        @block.scalar
        def _(act):
            def copy_sums(it, cross):
                act.wait_ge(pv_done, it * CH + (CH if cross else TT))
                at_least(act, z_part, 2 * it - 1 + cross)
                nc.scalar.activation(y[:, cross, :], pY[:, :], ACT.Copy).then_inc(y_ready, 1)

            def body(it, k, follow):
                for c in range(CH):
                    _, _, lo, n = chunk(c)
                    for a in range(2):
                        act.wait_ge(st_done, (it * CH + c) * 2 + a + 1)
                        nc.scalar.activation(prob[0:n, (k * CH + c) % 2, 2 * a:2 * a + 2, lo:S], pS[0:n, a, :, lo:S], ACT.Exp,
                                             scale=HW ** -0.5).then_inc(exp_done, 1)
                    if c == 0 and not is_first(it):
                        copy_sums(it - 1, 1)
                    if c == TT:
                        copy_sums(it, 0)

            steps(act, body)
            copy_sums(STEPS - 1, 1)

        @block.tensor
        def _(pe):
            def slot_read(it, n, number):
                at_least(pe, job_read, number - before(it, n) + 1)

            def make_max(it, k, kind, n, number, slot):
                if kind == "self":
                    if n == 0:
                        pe.wait_ge(in_self[k], (it // K) * 128 + 128)
                    h, t = n // TT, n % TT
                    nc.tensor.matmul(pM[:, slot, 0:P * (t + 1)], qs[k][0:R, h, t * P:(t + 1) * P], ks[k][0:R, h, 0:P * (t + 1)],
                                     start=True, stop=False)
                    nc.tensor.matmul(pM[:, slot, P * t:P * (t + 1)], g["identb"][:, :], g["mask_n"][:, :],
                                     start=False, stop=True).then_inc(job_done, 1)
                elif kind == "cross":
                    if n == 0:
                        pe.wait_ge(in_cross[k], (it // K) * 128 + 128)
                    (lo, w), h, t = KCOLS[n % NK], n // NK // TT, n // NK % TT
                    nc.tensor.matmul(pM[:, slot, 0:w], qc[k][0:R, h, t * P:(t + 1) * P], kc[k][0:R, h, lo:lo + w],
                                     start=True, stop=True).then_inc(job_done, 1)
                elif n == 0:
                    pe.wait_ge(job_read, number)
                    nc.tensor.transpose(pM[0:SELF, slot, 0:P], negm[k][:, 0:SELF], g["ident"][:, :]).then_inc(job_done, 1)
                else:
                    pe.wait_ge(comb, it + 1)
                    nc.tensor.transpose(pM[0:SELF, slot, 0:P], negm[k][:, SELF:2 * SELF], g["ident"][:, :]).then_inc(job_done, 1)

            def make_sums(it, cross, slot):
                pe.wait_ge(y_ready, 2 * it + cross + 1)
                for t in range(TT):
                    last = nc.tensor.transpose(pM[:, slot, t * P:(t + 1) * P], y[:, cross, t * P:(t + 1) * P], g["ident"][:, :])
                last.then_inc(job_done, 1)

            for n, (kind, m) in enumerate(MAXIMA):
                if n >= RING:
                    pe.wait_ge(job_read, n - RING + 1)
                make_max(0, 0, kind, m, n, n % RING)

            def values(it, k, c):
                cross, j, lo, n = chunk(c)
                if c == 0:
                    pe.wait_ge(in_v[k], (it // K) * 32 + 32)
                if j == 0:
                    at_least(pe, y_ready, 2 * it + cross)
                pe.wait_ge(exp_done, (it * CH + c) * 2 + 2)
                for h in range(4):
                    last = nc.tensor.matmul(pY[32 * h:32 * h + 32, lo:S], v[k][0:n, c, 32 * h:32 * h + 32],
                                            prob[0:n, (k * CH + c) % 2, h, lo:S], start=j == 0, stop=c in (TT - 1, CH - 1))
                last.then_inc(pv_done, 1)

            def body(it, k, follow):
                jobs = step_jobs(is_first(it), follow == 0)
                shares, made = 5 * CH - 3, 0

                def jobs_upto(share):
                    nonlocal made
                    upto = min(len(jobs), -(-len(jobs) * share // shares)) if follow else (share >= shares // 2) + (share > 8)
                    for n in range(made, min(upto, len(jobs))):
                        kind, m = jobs[n]
                        number = first_job(it) + n
                        slot_read(it, n, number)
                        if kind != "sums":
                            make_max(it + 1, 1 - k, kind, m, number, n % RING)
                        else:
                            make_sums(it - m, m, n % RING)
                    made = max(made, upto)

                share = 0
                for c in range(CH):
                    cross, j, lo, n = chunk(c)
                    keys, qry = (kc, qc) if cross else (ks, qs)
                    if j == 0:
                        pe.wait_ge((cross_row if cross else self_row)[k], (it // K) * 16 + 16)
                    for h in range(4):
                        a = h // 2
                        if h % 2 == 0 and c > 0:
                            pe.wait_ge(exp_done, (it * CH + c) * 2 + a - 1)
                        last = nc.tensor.matmul(pS[0:n, a, h % 2, lo:S], keys[k][:, h, j * P:j * P + n], qry[k][:, h, lo:S],
                                                start=True, stop=bool(cross))
                        if not cross:
                            last = nc.tensor.matmul(pS[:, a, h % 2, lo:lo + P], g["identb"][:, :], g["mask_t"][:, :],
                                                    start=False, stop=True)
                        if h % 2 == 1:
                            last.then_inc(st_done, 1)
                        share += 1
                        jobs_upto(share)
                    if c:
                        values(it, k, c - 1)
                    share += 1
                    jobs_upto(share)
                values(it, k, CH - 1)
                assert made >= len(jobs)

            steps(pe, body)
            n = len(step_jobs(False, True))
            slot_read(STEPS - 1, n, first_job(STEPS - 1) + n)
            make_sums(STEPS - 1, 1, n % RING)


def route_stage(nc, g, i):
    with ExitStack() as ctx:
        r = Resources(nc, ctx)
        z = r.sb("e_z", [P, TT, D], F32)
        zT = r.sb("e_zT", [P, DC, S], F32)
        x = r.sb("e_x", [P, TT, D], F32)
        rows = r.sb("e_rows", [P, 2, TT, ROW], F32)
        xnT = r.sb("e_xnT", [P, DC, S], F32)
        o = r.sb("e_o", [P, TT, D], F32)
        w = ln_work(r, "e")

        def small(name, dt=F32, shape=(P, TT, NE)):
            return r.sb(f"e_{name}", list(shape), dt)

        lg, wt, rest, eq, s1, s2, gt, both, where, pick = (small(n) for n in (
            "lg", "wt", "rest", "eq", "s1", "s2", "gt", "both", "where", "pick"))
        mask = small("mask", BF16)
        run = small("run", BF16, (P, TT + 1, NE))
        top, tot, noop = (small(n, F32, (P, TT)) for n in ("top", "tot", "noop"))
        idx = small("idx", I32, (P, 2, TT))
        pO = r.ps("e_pO", [P, TT, D])
        pT = r.ps("e_pT", [P, DC, S])
        pL = r.ps("e_pL", [P, TT, NE])
        pC = r.ps("e_pC", [P, TT, NE])
        z_in, chain_s, pad_set, o_done, xn_ready, tr_done, xnT_ready = (r.sem(n) for n in (
            "e_z_in", "e_chain", "e_pad_set", "e_o_done", "e_xn_ready", "e_tr_done", "e_xnT_ready"))
        lg_done, lg_ready, ex_ready, mask_ready, pos_done, copied, sent_ready, o_ready, sent, stored = (r.sem(n) for n in (
            "e_lg_done", "e_lg_ready", "e_ex_ready", "e_mask_ready", "e_pos_done", "e_copied", "e_sent_ready", "e_o_ready",
            "e_sent", "e_stored"))
        zt_done, zT_ready, passed = r.sem("e_zt_done"), r.sem("e_zT_ready"), r.sem("e_passed")
        block = ctx.enter_context(nc.Block())
        LINKS = 52

        def over_tiles(a):
            return a.unsqueeze(2).broadcast_to([P, TT, NE])

        @block.sync
        def _(sp):
            def batch(b):
                at_least(sp, zt_done, b)
                for q in range(QUADS):
                    sp.dma_start(z[:, :, q * 4 * HW:(q + 1) * 4 * HW],
                                 g["z1"][b * QUADS + q].rearrange("p (t n) -> p t n", t=TT)).then_inc(z_in, 16)

            batches(sp, batch)

        @block.scalar
        def _(act):
            def batch(b):
                at_least(act, zt_done, b + 1)
                at_least(act, o_done, b)
                for d in range(DC):
                    nc.scalar.activation(zT[:, d, :], pT[:, d, :], ACT.Copy).then_inc(zT_ready, 1)
                at_least(act, tr_done, b + 1)
                at_least(act, lg_done, b)
                for d in range(DC):
                    nc.scalar.activation(xnT[:, d, :], pT[:, d, :], ACT.Copy).then_inc(xnT_ready, 1)
                at_least(act, lg_ready, b + 1)
                nc.scalar.activation(wt[:, :, :], lg[:, :, :], ACT.Exp).then_inc(ex_ready, 1)
                at_least(act, o_ready, b + 1)
                act.dma_start(g["acc"][bass.ds(b * S, S)].rearrange("(t p) d -> p t d", p=P), o[:, :, :]).then_inc(stored, 16)

            batches(act, batch)
            act.wait_ge(stored, B * 16)

        @block.vector
        def _(dve):
            nc.vector.memset(run[:, :, :], 0.0)
            nc.vector.memset(rows[:, :, :, D + 2:ROW], 0.0).then_inc(pad_set, 1)
            dve.wait_ge(pad_set, 1)
            def batch(b):
                chain = Chain(dve, chain_s, b * LINKS, passed)
                link = chain.link
                V = nc.vector
                at_least(dve, o_done, b + 1)
                at_least(dve, sent, b * 16 * 2 * TT)
                at_least(dve, copied, b)
                at_least(dve, stored, b * 16)
                link(V.tensor_tensor(x[:, :, :].rearrange("p t d -> p (t d)"), pO[:, :, :].rearrange("p t d -> p (t d)"),
                                     g["x_res"][:, bass.ds(b * (TT * D), TT * D)], ALU.add))
                for t in range(TT):
                    last = V.tensor_tensor(x[:, t, :], x[:, t, :], g["bias_row"][:, 2, :], ALU.add)
                link(last)
                layer_norm(nc, chain, x, rows[:, 0, :, 0:D], w).then_inc(xn_ready, 1)
                at_least(dve, lg_done, b + 1)
                link(V.tensor_tensor(lg[:, :, :], pL[:, :, :], g["router_bias"][:, :].unsqueeze(1).broadcast_to([P, TT, NE]), ALU.add))
                link(V.tensor_reduce(top[:, :], lg[:, :, :], AX.X, ALU.max))
                V.tensor_tensor(lg[:, :, :], lg[:, :, :], over_tiles(top[:, :]), ALU.subtract).then_inc(lg_ready, 1)
                at_least(dve, ex_ready, b + 1)
                link(V.tensor_reduce(tot[:, :], wt[:, :, :], AX.X, ALU.add))
                link(V.reciprocal(tot[:, :], tot[:, :]))
                link(V.tensor_tensor(wt[:, :, :], wt[:, :, :], over_tiles(tot[:, :]), ALU.mult))
                src = wt
                for n, sel in enumerate((s1, s2)):
                    m = rows[:, n, :, D]
                    link(V.tensor_reduce(m, src[:, :, :], AX.X, ALU.max))
                    link(V.tensor_tensor(eq[:, :, :], src[:, :, :], over_tiles(m), ALU.is_equal))
                    link(V.tensor_tensor(eq[:, :, :], eq[:, :, :], g["prio"][:, :, :], ALU.mult))
                    link(V.tensor_reduce(top[:, :], eq[:, :, :], AX.X, ALU.max))
                    link(V.tensor_tensor(sel[:, :, :], eq[:, :, :], over_tiles(top[:, :]), ALU.is_equal))
                    if n == 0:
                        link(V.scalar_tensor_tensor(out=rest[:, :, :], in0=sel[:, :, :], scalar=-2.0, in1=wt[:, :, :],
                                                    op0=ALU.mult, op1=ALU.add))
                        src = rest
                link(V.tensor_tensor(both[:, :, :], s1[:, :, :], s2[:, :, :], ALU.add))
                link(V.tensor_scalar(gt[:, :, :], wt[:, :, :], 0.0, None, ALU.is_gt))
                link(V.tensor_tensor(mask[:, :, :], both[:, :, :], gt[:, :, :], ALU.mult))
                link(V.tensor_copy(run[:, 0, :], run[:, TT, :]))
                for t in range(TT):
                    ins = V.tensor_tensor(run[:, t + 1, :], run[:, t, :], mask[:, t, :], ALU.add)
                    if t == TT - 1:
                        ins.then_inc(mask_ready, 1)
                        at_least(dve, mask_ready, b + 1)
                    else:
                        link(ins)
                at_least(dve, pos_done, b + 1)
                link(V.tensor_scalar(eq[:, :, :], pC[:, :, :], float(CAP), None, ALU.is_lt))
                link(V.tensor_tensor(eq[:, :, :], eq[:, :, :], gt[:, :, :], ALU.mult))
                link(V.tensor_tensor(where[:, :, :], pC[:, :, :], g["slot0"][:, :, :], ALU.add))
                link(V.tensor_tensor(where[:, :, :], where[:, :, :], eq[:, :, :], ALU.mult))
                link(V.tensor_scalar_add(where[:, :, :], where[:, :, :], float(FAR)))
                for n, sel in enumerate((s1, s2)):
                    link(V.tensor_tensor(pick[:, :, :], where[:, :, :], sel[:, :, :], ALU.mult))
                    link(V.tensor_reduce(top[:, :], pick[:, :, :], AX.X, ALU.add))
                    link(V.tensor_copy(idx[:, n, :], top[:, :]))
                for n in range(2):
                    last = V.tensor_copy(rows[:, n, :, D + 1].bitcast(I32), g["tok"][:, :])
                last.then_inc(sent_ready, 1)
                at_least(dve, sent_ready, b + 1)
                link(V.tensor_scalar_add(g["tok"][:, :], g["tok"][:, :], float(S)))
                link(V.tensor_tensor(noop[:, :], both[:, :, NX], wt[:, :, NX], ALU.mult))
                for t in range(TT):
                    last = V.scalar_tensor_tensor(out=o[:, t, :], in0=rows[:, 0, t, 0:D], scalar=noop[:, t:t + 1],
                                                  in1=x[:, t, :], op0=ALU.mult, op1=ALU.add)
                last.then_inc(o_ready, 1)
                at_least(dve, o_ready, b + 1)
                assert chain.n == LINKS, chain.n

            batches(dve, batch)

        @block.tensor
        def _(pe):
            def batch(b):
                at_least(pe, z_in, b * 16 * QUADS + 16 * QUADS)
                at_least(pe, xnT_ready, b * DC)
                for d in range(DC):
                    for t in range(TT):
                        last = nc.tensor.transpose(pT[:, d, t * P:(t + 1) * P], z[:, t, d * P:(d + 1) * P], g["ident"][:, :])
                last.then_inc(zt_done, 1)
                at_least(pe, zT_ready, b * DC + DC)
                at_least(pe, xn_ready, b)
                for t in range(TT):
                    for d in range(DC):
                        last = nc.tensor.matmul(pO[:, t, :], zT[:, d, t * P:(t + 1) * P], g["wp"][:, d, :],
                                                start=d == 0, stop=d == DC - 1)
                last.then_inc(o_done, 1)
                at_least(pe, xn_ready, b + 1)
                transpose_tokens(nc, rows[:, 0, :, 0:D], g["ident"], pT).then_inc(tr_done, 1)
                at_least(pe, xnT_ready, b * DC + DC)
                for t in range(TT):
                    for d in range(DC):
                        last = nc.tensor.matmul(pL[:, t, :], xnT[:, d, t * P:(t + 1) * P], g["rwT"][:, d, :],
                                                start=d == 0, stop=d == DC - 1)
                last.then_inc(lg_done, 1)
                at_least(pe, mask_ready, b + 1)
                for t in range(TT):
                    nc.tensor.matmul(pC[:, t, :], g["before"][:, :], mask[:, t, :], start=True, stop=False)
                    last = nc.tensor.matmul(pC[:, t, :], g["onesb"][:, :], run[:, t, :], start=False, stop=True)
                last.then_inc(pos_done, 1)

            batches(pe, batch)

        @block.gpsimd
        def _(pool):
            def batch(b):
                at_least(pool, xn_ready, b + 1)
                pool.sem_inc(passed, 1)
                nc.gpsimd.tensor_copy(rows[:, 1, :, 0:D], rows[:, 0, :, 0:D]).then_inc(copied, 1)
                at_least(pool, sent_ready, b + 1)
                at_least(pool, copied, b + 1)
                pool.sem_inc(passed, 1)
                for n in range(2):
                    for t in range(TT):
                        pool.indirect_dma_start(
                            out=g["slot_rows"], out_offset=bass.IndirectOffsetOnAxis(ap=idx[:, n, t:t + 1].bitcast(U32), axis=0),
                            in_=rows[:, n, t, :], in_offset=None, bounds_check=SLOTS - 1, oob_is_err=False).then_inc(sent, 16)

            batches(pool, batch)
            pool.wait_ge(sent, B * 16 * 2 * TT)


def expert_stage(nc, g, i):
    with ExitStack() as ctx:
        r = Resources(nc, ctx)
        K = 2
        CTT = CAP // P
        wi = [r.sb(f"f_wi_{k}", [P, DC, FI], F32) for k in range(K)]
        wo = [r.sb(f"f_wo_{k}", [P, FC, D], F32) for k in range(K)]
        rows = [r.sb(f"f_rows_{k}", [P, CTT, ROW], F32) for k in range(K)]
        y = [r.sb(f"f_y_{k}", [P, CTT, D], F32) for k in range(K)]
        xT = r.sb("f_xT", [P, DC, CAP], F32)
        hT = r.sb("f_hT", [P, FC, CAP], F32)
        pT = r.ps("f_pT", [P, DC, CAP])
        pH = r.ps("f_pH", [P, 4, CAP])
        pO = r.ps("f_pO", [P, CTT, D])
        loaded = [r.sem(f"f_loaded_{k}") for k in range(K)]
        tr_done, xT_ready, h_done, h_ready, o_done, y_ready, added = (r.sem(n) for n in (
            "f_tr_done", "f_xT_ready", "f_h_done", "f_h_ready", "f_o_done", "f_y_ready", "f_added"))
        out_done, passed = r.sem("f_out_done"), r.sem("f_passed")
        block = ctx.enter_context(nc.Block())

        def experts(engine, body):
            for k in range(K):
                body(k, k)
            with engine.Fori(1, NX // K) as m:
                for k in range(K):
                    body(m * K + k, k)
            body(NX - 1, 0)

        @block.sync
        def _(sp):
            def body(e, k):
                sp.dma_start(wi[k][:, :, :], i["wi"][e].rearrange("(c p) f -> p c f", p=P)).then_inc(loaded[k], 16)
                sp.dma_start(wo[k][:, :, :], i["wo"][e].rearrange("(c p) d -> p c d", p=P)).then_inc(loaded[k], 16)
                sp.dma_start(rows[k][:, :, :], g["slot_rows"][bass.ds(e * CAP, CAP)].rearrange("(t p) c -> p t c", p=P)).then_inc(loaded[k], 16)

            for k in range(K):
                body(k, k)
            with sp.Fori(0, NX // K - 1) as m:
                for k in range(K):
                    sp.wait_ge(o_done, m * K + k + 1)
                    sp.wait_ge(added, (m * K + k + 1) * 16 * CTT)
                    body(m * K + k + K, k)
            sp.wait_ge(o_done, NX - 2)
            sp.wait_ge(added, (NX - 2) * 16 * CTT)
            body(NX - 1, 0)
            sp.wait_ge(added, NX * 16 * CTT)
            sp.dma_start(i["out"].rearrange("b s d -> (b s) d"), g["acc"][0:B * S]).then_inc(out_done, 16)
            sp.wait_ge(out_done, 16)

        @block.tensor
        def _(pe):
            def body(e, k):
                pe.wait_ge(loaded[k], (e // K) * 48 + 48)
                at_least(pe, xT_ready, e * DC)
                for d in range(DC):
                    for t in range(CTT):
                        last = nc.tensor.transpose(pT[:, d, t * P:(t + 1) * P], rows[k][:, t, d * P:(d + 1) * P], g["ident"][:, :])
                last.then_inc(tr_done, 1)
                pe.wait_ge(xT_ready, e * DC + DC)
                for f in range(FC):
                    if f >= 4:
                        pe.wait_ge(h_ready, e * FC + f - 3)
                    for d in range(DC):
                        last = nc.tensor.matmul(pH[:, f % 4, :], wi[k][:, d, f * P:(f + 1) * P], xT[:, d, :],
                                                start=d == 0, stop=d == DC - 1)
                    last.then_inc(h_done, 1)
                pe.wait_ge(h_ready, e * FC + FC)
                at_least(pe, y_ready, e)
                for t in range(CTT):
                    for f in range(FC):
                        last = nc.tensor.matmul(pO[:, t, :], hT[:, f, t * P:(t + 1) * P], wo[k][:, f, :],
                                                start=f == 0, stop=f == FC - 1)
                last.then_inc(o_done, 1)

            experts(pe, body)

        @block.scalar
        def _(act):
            def body(e, k):
                act.wait_ge(tr_done, e + 1)
                at_least(act, h_done, e * FC)
                for d in range(DC):
                    nc.scalar.activation(xT[:, d, :], pT[:, d, :], ACT.Copy).then_inc(xT_ready, 1)
                at_least(act, o_done, e)
                for f in range(FC):
                    act.wait_ge(h_done, e * FC + f + 1)
                    nc.scalar.activation(hT[:, f, :], pH[:, f % 4, :], ACT.Relu).then_inc(h_ready, 1)

            experts(act, body)

        @block.vector
        def _(dve):
            def body(e, k):
                dve.wait_ge(o_done, e + 1)
                at_least(dve, added, e * 16 * CTT)
                for t in range(CTT):
                    last = nc.vector.tensor_scalar(y[k][:, t, :], pO[:, t, :], rows[k][:, t, D:D + 1], None, ALU.mult)
                last.then_inc(y_ready, 1)

            experts(dve, body)

        @block.gpsimd
        def _(pool):
            def body(e, k):
                pool.wait_ge(y_ready, e + 1)
                at_least(pool, added, e * 16 * CTT)
                pool.sem_inc(passed, 1)
                for t in range(CTT):
                    pool.indirect_dma_start(
                        out=g["acc"], out_offset=bass.IndirectOffsetOnAxis(ap=rows[k][:, t, D + 1:D + 2].bitcast(U32), axis=0),
                        in_=y[k][:, t, :], in_offset=None, bounds_check=B * S + SLOTS - 1, oob_is_err=True,
                        compute_op=ALU.add).then_inc(added, 16)

            experts(pool, body)


def decoder_layer(nc, i):
    with ExitStack() as ctx:
        r = Resources(nc, ctx)

        def dram(name, shape, dt):
            return nc.dram_tensor(name, shape, dt, kind="Internal").ap()

        g = {
            "lat_h": dram("lat_h", [B, P, S], F32), "lat_l": dram("lat_l", [B, LD, S], F32),
            "lat_v": dram("lat_v", [B, P, TT, LD], F32),
            "q0h": dram("q0h", [B * PAIRS, P, S], F32), "q0l": dram("q0l", [B * PAIRS, P, S], F32),
            "z0": dram("z0", [B * PAIRS, P, S], F32),
            "s1h": dram("s1h", [3, B * QUADS, 4 * HW, S], F32), "s1l": dram("s1l", [3, B * QUADS, 4 * HW, S], F32),
            "c1h": dram("c1h", [B * QUADS, 4 * HW, SCP], F32), "c1l": dram("c1l", [B * QUADS, 4 * HW, SCP], F32),
            "v1": dram("v1", [B * QUADS, P, CH, 4 * 2 * HW], F32), "z1": dram("z1", [B * QUADS, P, TT * 4 * HW], F32),
            "slot_rows": dram("slot_rows", [SLOTS, ROW], F32), "acc": dram("acc", [B * S + SLOTS, D], F32),
            "ident": r.sb("ident", [P, P], F32), "identb": r.sb("identb", [P, P], BF16),
            "mask_t": r.sb("mask_t", [P, P], BF16), "mask_n": r.sb("mask_n", [P, P], BF16),
            "before": r.sb("before", [P, P], BF16), "onesb": r.sb("onesb", [P, P], BF16), "ones": r.sb("ones", [P, P], F32),
            "tok": r.sb("tok", [P, TT], I32), "slot0": r.sb("slot0", [P, TT, NE], I32), "prio": r.sb("prio", [P, TT, NE], I32),
            "bias_col": r.sb("bias_col", [P, 4, DC], F32), "bias_row": r.sb("bias_row", [P, 3, D], F32),
            "router_bias": r.sb("router_bias", [P, NE], F32), "rwT": r.sb("rwT", [P, DC, NE], F32),
            "wp": r.sb("wp", [P, DC, D], F32), "x_res": r.sb("x_res", [P, B * TT * D], F32),
        }
        with ExitStack() as early:
            re = Resources(nc, early)
            for name in ("xWq", "xWk", "xWcq", "xWv"):
                g[name] = re.sb(name, [P, DC, D], F32)
            for name in ("xWck", "xWcv"):
                g[name] = re.sb(name, [P, D], F32)
            g["wdd"] = re.sb("wdd", [P, DC, 2, LD], F32)
            g["wt"] = re.sb("wt", [P, DC, H0 * LD], F32)
            g["wvo"] = re.sb("wvo", [P, PAIRS, D], F32)
            prepare(nc, g, i)
            latent_stage(nc, g, i)
            latent_attention(nc, g)
            cross_stage(nc, g, i)
        mixed_attention(nc, g)
        route_stage(nc, g, i)
        expert_stage(nc, g, i)


INPUTS = {"x": "x", "ctx_512": "ctx", "L0_attn_Wq": "Wq", "L0_attn_Wkv_down": "Wkv_down", "L0_attn_Wk_up": "Wk_up",
          "L0_attn_Wv_up": "Wv_up", "L0_attn_Wout": "Wout", "L0_xattn_Wk": "xWk", "L0_xattn_bk": "xbk", "L0_xattn_Wq": "xWq",
          "L0_xattn_bq": "xbq", "L0_xattn_Wv": "xWv", "L0_xattn_bv": "xbv", "L0_xattn_Wck": "xWck", "L0_xattn_bck": "xbck",
          "L0_xattn_Wcq": "xWcq", "L0_xattn_bcq": "xbcq", "L0_xattn_Wcv": "xWcv", "L0_xattn_bcv": "xbcv",
          "L0_xattn_Wp": "xWp", "L0_xattn_bp": "xbp", "L0_ffn_router_w": "router_w", "L0_ffn_router_b": "router_b",
          "L0_ffn_experts_inter": "wi", "L0_ffn_experts_out": "wo"}


def kernel(**inputs):
    import numpy as np
    import concourse.bacc as bacc
    from concourse.bass_utils import run_bass_kernel_spmd

    nc = bacc.Bacc("TRN2", target_bir_lowering=False, num_devices=1)
    arrays, aps = {}, {}
    for name, short in INPUTS.items():
        a = np.ascontiguousarray(inputs[name])
        arrays[f"in_{name}"] = a
        aps[short] = nc.dram_tensor(f"in_{name}", a.shape, mybir.dt.from_np(a.dtype), kind="ExternalInput").ap()
    aps["out"] = nc.dram_tensor("out", [B, S, D], F32, kind="ExternalOutput").ap()
    decoder_layer(nc, aps)
    result = run_bass_kernel_spmd(nc, [arrays], core_ids=[0])
    return result.results[0]["out"]
```

```python
from contextlib import ExitStack

import concourse.bass as bass
from concourse import mybir

F32 = mybir.dt.float32
F32R = mybir.dt.float32r
BF16 = mybir.dt.bfloat16
I32 = mybir.dt.int32
U32 = mybir.dt.uint32
ALU = mybir.AluOpType
ACT = mybir.ActivationFunctionType
AX = mybir.AxisListType

P = 128
B, S, D = 8, 512, 256
DC = D // P
TT = S // P
H0, HD, LD = 16, 64, 64
PAIRS = H0 // 2
H1, HW = 16, 16
QUADS = H1 // 4
SC, CW = 1601, 128
SCP = SC + 1
CT = -(-SC // P)
LAST = SC - (CT - 1) * P
CH = TT + CT
NE, NX, FI = 8, 7, 1024
FC = FI // P
CAP = (B * S) // NE
SLOTS = NX * CAP
ROW = D + 4
FAR = 65536
WEIGHT_SLOTS = 2
MASKED = -1e30
EPS = 1e-5
RSQRT_SEED = 0x5F3759DF
KCOLS = [(0, 400), (400, 400), (800, 400), (1200, 402)]


class Resources:
    def __init__(self, nc, ctx):
        self.nc, self.ctx = nc, ctx

    def sb(self, name, shape, dt):
        return self.ctx.enter_context(self.nc.sbuf_tensor(name, shape, dt))

    def ps(self, name, shape, dt=F32):
        return self.ctx.enter_context(self.nc.psum_tensor(name, shape, dt))

    def sem(self, name):
        return self.ctx.enter_context(self.nc.semaphore(name))


class Chain:

    def __init__(self, engine, sem, first, passed=None):
        self.engine, self.sem, self.first, self.n, self.passed = engine, sem, first, 0, passed

    def link(self, ins, apart=False):
        self.n += 1
        ins.then_inc(self.sem, 1)
        self.engine.wait_ge(self.sem, self.first + self.n)
        if apart:
            self.engine.sem_inc(self.passed, 1)


def at_least(engine, sem, value):
    if not isinstance(value, int) or value > 0:
        engine.wait_ge(sem, value)


def wait_apart(engine, passed, sem, value):
    engine.wait_ge(sem, value)
    engine.sem_inc(passed, 1)


def batches(engine, body):
    body(0)
    with engine.Fori(1, B) as b:
        body(b)


def slotted_steps(engine, count, slots, body):
    for n in range(slots):
        body(n, n, slots)
    with engine.Fori(1, count // slots - 1) as m:
        for k in range(slots):
            body(m * slots + k, k, slots)
    for k in range(slots):
        body(count - slots + k, k, slots - 1 - k)


LN_LINKS = 14


def norm_stats(nc, chain, x, w):
    link = chain.link
    for t in range(TT):
        last = nc.vector.bn_stats(w["stats"][:, t, :], x[:, t, :])
    link(last, apart=True)
    for t in range(TT):
        last = nc.vector.bn_aggr(w["mv"][:, t, :], w["stats"][:, t, :])
    link(last)


def norm_root(nc, chain, w):
    link = chain.link
    var, y, a = w["var"][:, :], w["rstd"][:, :], w["newton"][:, :]
    link(nc.vector.tensor_scalar_add(var, w["mv"][:, :, 1], EPS))
    link(nc.vector.tensor_scalar(a.bitcast(I32), var.bitcast(I32), 1, None, ALU.logical_shift_right))
    link(nc.vector.tensor_scalar(y.bitcast(I32), a.bitcast(I32), -1.0, float(RSQRT_SEED), ALU.mult, ALU.add))
    for _ in range(3):
        link(nc.vector.scalar_tensor_tensor(out=a, in0=y, scalar=-0.5, in1=y, op0=ALU.mult, op1=ALU.mult))
        link(nc.vector.tensor_tensor(a, a, var, ALU.mult))
        link(nc.vector.scalar_tensor_tensor(out=y, in0=a, scalar=1.5, in1=y, op0=ALU.add, op1=ALU.mult))


def norm_apply(nc, x, xn, w):
    for t in range(TT):
        last = nc.vector.tensor_scalar(xn[:, t, :], x[:, t, :], w["mv"][:, t, 0:1], w["rstd"][:, t:t + 1],
                                       ALU.subtract, ALU.mult)
    return last


def layer_norm(nc, chain, x, xn, w, xn_free=None):
    n0 = chain.n
    norm_stats(nc, chain, x, w)
    norm_root(nc, chain, w)
    assert chain.n - n0 == LN_LINKS
    if xn_free:
        at_least(chain.engine, *xn_free)
    return norm_apply(nc, x, xn, w)


def ln_work(r, tag):
    return {"stats": r.sb(f"stats_{tag}", [P, TT, 6], F32), "mv": r.sb(f"mv_{tag}", [P, TT, 2], F32),
            "var": r.sb(f"var_{tag}", [P, TT], F32), "rstd": r.sb(f"rstd_{tag}", [P, TT], F32),
            "newton": r.sb(f"newton_{tag}", [P, TT], F32)}


def three_passes(nc, out, lhs, rhs, start, stop):
    nc.tensor.matmul(out, lhs[1], rhs[0], start=start, stop=False)
    nc.tensor.matmul(out, lhs[0], rhs[1], start=False, stop=False)
    return nc.tensor.matmul(out, lhs[0], rhs[0], start=False, stop=stop)


def transpose_tokens(nc, xn, ident, pT):
    for d in range(DC):
        for t in range(TT):
            last = nc.tensor.transpose(pT[:, d, t * P:(t + 1) * P], xn[:, t, d * P:(d + 1) * P], ident[:, :])
    return last


def prepare(nc, g, i):
    with ExitStack() as ctx:
        r = Resources(nc, ctx)
        wq = r.sb("p_wq", [P, DC, H0 * HD], F32)
        wk = r.sb("p_wk", [LD, H0 * HD], F32)
        wv = r.sb("p_wv", [LD, H0 * HD], F32)
        wo = r.sb("p_wo", [P, PAIRS, D], F32)
        wqT = r.sb("p_wqT", [P, PAIRS, D], F32)
        wkB = r.sb("p_wkB", [P, PAIRS, P], F32)
        wvB = r.sb("p_wvB", [P, PAIRS, P], F32)
        rw = r.sb("p_rw", [NE, D], F32)
        wdd = r.sb("p_wdd", [P, DC, 2, LD], F32)
        none_tok = r.sb("p_none_tok", [P, SLOTS // P, 1], I32)
        empty = g["empty"]
        pA = r.ps("p_pA", [P, 4, 512])
        pB = r.ps("p_pB", [P, 4, 512])
        in_dd, dd_high, dd_done, wt_high = (r.sem(n) for n in ("in_dd", "dd_high", "dd_done", "wt_high"))
        in_wq, in_up, in_wo, in_x, in_rw = (r.sem(n) for n in ("in_wq", "in_up", "in_wo", "in_x", "in_rw"))
        id_set, const_set, zero_set, empty_set = (r.sem(n) for n in ("id_set", "const_set", "zero_set", "empty_set"))
        wqT_tr, wqT_done, up_tr, up_done, rw_tr, rw_done = (r.sem(n) for n in (
            "wqT_tr", "wqT_done", "up_tr", "up_done", "rw_tr", "rw_done"))
        wt_mm, wt_done, wvo_mm, wvo_done = (r.sem(n) for n in ("wt_mm", "wt_done", "wvo_mm", "wvo_done"))
        block = ctx.enter_context(nc.Block())

        @block.sync
        def _(sp):
            sp.dma_start(wq[:, :, :], i["Wq"].rearrange("(c p) h k -> p c (h k)", p=P)).then_inc(in_wq, 16)
            sp.dma_start(wk[:, :], i["Wk_up"].rearrange("c h k -> c (h k)")).then_inc(in_up, 16)
            sp.dma_start(wv[:, :], i["Wv_up"].rearrange("c h k -> c (h k)")).then_inc(in_up, 16)
            sp.dma_start(rw[:, :], i["router_w"]).then_inc(in_rw, 16)
            sp.dma_start(wo[:, :, :], i["Wout"].rearrange("(g a) k o -> (a k) g o", a=2)).then_inc(in_wo, 16)
            for half in range(2):
                sp.dma_start(wdd[:, :, half, :], i["Wkv_down"].rearrange("(c p) n -> p c n", p=P)).then_inc(in_dd, 16)
            for name, dst in (("xWq", "xWq"), ("xWk", "xWk"), ("xWcq", "xWcq"), ("xWv", "xWv"), ("xWp", "wp")):
                sp.dma_start(g[dst][:, :, :], i[name].rearrange("(c p) n -> p c n", p=P)).then_inc(in_x, 16)
            for name in ("xWck", "xWcv"):
                sp.dma_start(g[name][:, :], i[name]).then_inc(in_x, 16)
            for n, name in enumerate(("xbq", "xbk", "xbcq", "xbck")):
                sp.dma_start(g["bias_col"][:, n, :], i[name].rearrange("(c p) -> p c", p=P),
                             allow_slow_non_contiguous=True).then_inc(in_x, 16)
            for n, name in enumerate(("xbv", "xbcv", "xbp")):
                sp.dma_start(g["bias_row"][:, n, :], i[name].partition_broadcast(P)).then_inc(in_x, 16)
            sp.dma_start(g["router_bias"][:, :], i["router_b"].partition_broadcast(P)).then_inc(in_x, 16)
            sp.wait_ge(empty_set, 2)
            sp.dma_start(g["slot_rows"].rearrange("(p n) c -> p n c", p=P), empty[:, :, :]).then_inc(g["empty_out"], 16)
            sp.wait_ge(in_x, 16 * 15)

        @block.gpsimd
        def _(pool):
            nc.gpsimd.memset(g["ident"][:, :], 0.0).then_inc(id_set, 1)
            nc.gpsimd.memset(g["identb"][:, :], 0.0).then_inc(id_set, 1)
            nc.gpsimd.memset(g["mask_t"][:, :], 0.0).then_inc(id_set, 1)
            nc.gpsimd.memset(g["mask_n"][:, :], 0.0).then_inc(id_set, 1)
            nc.gpsimd.memset(g["before"][:, :], 1.0).then_inc(id_set, 1)
            pool.wait_ge(id_set, 5)
            for m in ("ident", "identb"):
                nc.gpsimd.affine_select(out=g[m][:, :], in_=g[m][:, :], compare_op=ALU.not_equal, fill=1.0, base=0,
                                        pattern=[[-1, P]], channel_multiplier=1).then_inc(const_set, 1)
            nc.gpsimd.affine_select(out=g["mask_t"][:, :], in_=g["mask_t"][:, :], compare_op=ALU.is_ge, fill=MASKED,
                                    base=0, pattern=[[1, P]], channel_multiplier=-1).then_inc(const_set, 1)
            nc.gpsimd.affine_select(out=g["mask_n"][:, :], in_=g["mask_n"][:, :], compare_op=ALU.is_ge, fill=MASKED,
                                    base=0, pattern=[[-1, P]], channel_multiplier=1).then_inc(const_set, 1)
            nc.gpsimd.affine_select(out=g["before"][:, :], in_=g["before"][:, :], compare_op=ALU.is_gt, fill=0.0,
                                    base=0, pattern=[[1, P]], channel_multiplier=-1).then_inc(const_set, 1)
            nc.gpsimd.iota(g["tok"][:, :], pattern=[[P, TT]], base=0, channel_multiplier=1).then_inc(const_set, 1)
            nc.gpsimd.iota(g["slot0"][:, :, :], pattern=[[0, TT], [CAP, NE]], base=-FAR, channel_multiplier=0).then_inc(const_set, 1)
            nc.gpsimd.iota(g["prio"][:, :, :], pattern=[[0, TT], [-1, NE]], base=NE, channel_multiplier=0).then_inc(const_set, 1)
            nc.gpsimd.iota(none_tok[:, :, :], pattern=[[1, SLOTS // P], [0, 1]], base=B * S,
                           channel_multiplier=SLOTS // P).then_inc(const_set, 1)
            pool.wait_ge(const_set, 9)

        @block.vector
        def _(dve):
            nc.vector.memset(empty[:, :, :], 0.0).then_inc(empty_set, 1)
            dve.wait_ge(empty_set, 1)
            dve.wait_ge(const_set, 9)
            nc.vector.tensor_copy(empty[:, :, D + 1:D + 2].bitcast(I32), none_tok[:, :, :]).then_inc(empty_set, 1)
            nc.vector.memset(wkB[:, :, :], 0.0)
            nc.vector.memset(wvB[:, :, :], 0.0).then_inc(zero_set, 1)
            nc.vector.memset(g["ones"][:, :], 1.0)
            nc.vector.memset(g["onesb"][:, :], 1.0).then_inc(zero_set, 1)
            for n in range(4):
                dve.wait_ge(wqT_tr, n + 1)
                nc.vector.tensor_copy(wqT[:, 2 * n:2 * n + 2, :], pA[:, n, :].rearrange("p (a b) -> p a b", a=2)).then_inc(wqT_done, 1)
            dve.wait_ge(zero_set, 1)
            for n, dst in enumerate((wkB, wvB)):
                dve.wait_ge(up_tr, n + 1)
                for a in range(2):
                    last = nc.vector.tensor_copy(dst[a * HD:(a + 1) * HD, :, a * LD:(a + 1) * LD],
                                                 pB[a * HD:(a + 1) * HD, n, :].rearrange("p (g c) -> p g c", g=PAIRS))
                last.then_inc(up_done, 1)
            dve.wait_ge(rw_tr, 1)
            nc.vector.tensor_copy(g["rwT"][:, :, :], pB[:, 2, 0:DC * NE].rearrange("p (c e) -> p c e", c=DC)).then_inc(rw_done, 1)
            for n in range(4):
                dve.wait_ge(wt_mm, n + 1)
                high, low = (g[name][:, n // 2, (n % 2) * 512:(n % 2) * 512 + 512] for name in ("wth", "wtl"))
                nc.vector.tensor_copy(high, pA[:, n, :]).then_inc(wt_high, 1)
                dve.wait_ge(wt_high, n + 1)
                nc.vector.tensor_tensor(low, pA[:, n, :], high.bitcast(F32), ALU.subtract).then_inc(wt_done, 1)
            dve.wait_ge(in_dd, 32)
            nc.vector.tensor_copy(g["ddh"][:, :, :, :], wdd[:, :, :, :]).then_inc(dd_high, 1)
            dve.wait_ge(dd_high, 1)
            nc.vector.tensor_tensor(g["ddl"][:, :, :, :], wdd[:, :, :, :], g["ddh"][:, :, :, :].bitcast(F32), ALU.subtract).then_inc(dd_done, 1)
            for n in range(4):
                dve.wait_ge(wvo_mm, n + 1)
                nc.vector.tensor_copy(g["wvo"][:, 2 * n:2 * n + 2, :], pB[:, n, :].rearrange("p (a b) -> p a b", a=2)).then_inc(wvo_done, 1)
            dve.wait_ge(wvo_done, 4)
            dve.wait_ge(wt_done, 4)
            dve.wait_ge(dd_done, 1)

        @block.tensor
        def _(pe):
            pe.wait_ge(const_set, 2)
            pe.wait_ge(in_wq, 16)
            for n in range(4):
                for a in range(2):
                    for c in range(DC):
                        last = nc.tensor.transpose(pA[:, n, a * D + c * P:a * D + (c + 1) * P],
                                                   wq[:, c, (2 * n + a) * P:(2 * n + a + 1) * P], g["ident"][:, :])
                last.then_inc(wqT_tr, 1)
            pe.wait_ge(in_up, 32)
            for n, w in enumerate((wk, wv)):
                for q in range(PAIRS):
                    last = nc.tensor.transpose(pB[:, n, q * LD:(q + 1) * LD], w[:, q * P:(q + 1) * P], g["ident"][0:LD, 0:LD])
                last.then_inc(up_tr, 1)
            pe.wait_ge(in_rw, 16)
            for c in range(DC):
                last = nc.tensor.transpose(pB[:, 2, c * NE:(c + 1) * NE], rw[:, c * P:(c + 1) * P], g["ident"][0:NE, 0:NE])
            last.then_inc(rw_tr, 1)
            pe.wait_ge(wqT_done, 4)
            pe.wait_ge(up_done, 2)
            for n in range(4):
                for q in range(4):
                    pair = (n % 2) * 4 + q
                    last = nc.tensor.matmul(pA[:, n, q * P:(q + 1) * P], wqT[:, pair, (n // 2) * P:(n // 2 + 1) * P],
                                            wkB[:, pair, :], start=True, stop=True)
                last.then_inc(wt_mm, 1)
            pe.wait_ge(in_wo, 16)
            pe.wait_ge(rw_done, 1)
            for n in range(4):
                for a in range(2):
                    last = nc.tensor.matmul(pB[:, n, a * D:(a + 1) * D], wvB[:, 2 * n + a, :], wo[:, 2 * n + a, :],
                                            start=True, stop=True)
                last.then_inc(wvo_mm, 1)


def latent_stage(nc, g, i):
    with ExitStack() as ctx:
        r = Resources(nc, ctx)
        x = r.sb("a_x", [P, TT, D], F32)
        xn = r.sb("a_xn", [P, TT, D], F32)
        K = 2
        xh = [r.sb(f"a_xh_{k}", [P, DC, S], F32R) for k in range(K)]
        xl = [r.sb(f"a_xl_{k}", [P, DC, S], F32R) for k in range(K)]
        w = ln_work(r, "a")
        qh = r.sb("a_qh", [P, PAIRS, S], F32R)
        ql = r.sb("a_ql", [P, PAIRS, S], F32R)
        lh = r.sb("a_lh", [P, S], F32R)
        ll = r.sb("a_ll", [LD, S], F32R)
        v = r.sb("a_v", [P, TT, LD], F32)
        pT = r.ps("a_pT", [P, DC, S])
        pL = r.ps("a_pL", [P, S])
        pV = r.ps("a_pV", [P, TT, LD])
        pQ = r.ps("a_pQ", [P, 4, S])
        x_in, chain_s, xn_ready, tr_done, x_high, x_low = (r.sem(n) for n in (
            "a_x_in", "a_chain", "a_xn_ready", "a_tr_done", "a_x_high", "a_x_low"))
        lat_done, v_done, q_done, high, low, v_ready = (r.sem(n) for n in ("a_lat_done", "a_v_done", "a_q_done", "a_high", "a_low", "a_v_ready"))
        lat_out, passed = r.sem("a_lat_out"), r.sem("a_passed")
        q_out = [r.sem(f"a_q_out_{half}") for half in range(2)]
        block = ctx.enter_context(nc.Block())
        JOBS = PAIRS + 1
        HALF = PAIRS // 2
        NORM_AT, TURN_AT = (0, 2, 4), PAIRS - 2

        @block.sync
        def _(sp):
            def load_x(b):
                sp.dma_start(x[:, :, :], i["x"][b].rearrange("(t p) d -> p t d", p=P)).then_inc(x_in, 16)

            load_x(0)
            sp.wait_ge(xn_ready, 1)
            load_x(1)

            def batch(b, k, follow):
                wait_apart(sp, passed, low, b * JOBS + 1)
                wait_apart(sp, passed, v_ready, b + 1)
                sp.dma_start(g["lat_h"][b], lh[:, :].bitcast(F32)).then_inc(lat_out, 16)
                sp.dma_start(g["lat_l"][b], ll[:, :].bitcast(F32)).then_inc(lat_out, 16)
                sp.dma_start(g["lat_v"][b], v[:, :, :]).then_inc(lat_out, 16)
                for half in range(2):
                    wait_apart(sp, passed, low, b * JOBS + 1 + (half + 1) * HALF)
                    mine = slice(half * HALF, (half + 1) * HALF)
                    for src, dst in ((qh, g["q0h"]), (ql, g["q0l"])):
                        sp.dma_start(dst[bass.ds(b * PAIRS + half * HALF, HALF)].rearrange("q p n -> p q n"),
                                     src[:, mine, :].bitcast(F32)).then_inc(q_out[half], 16)
                    if half == 0 and follow >= 2:
                        wait_apart(sp, passed, xn_ready, b + 2)
                        load_x(b + 2)

            slotted_steps(sp, B, K, batch)
            sp.wait_ge(g["empty_out"], 16)
            sp.wait_ge(lat_out, B * 48)
            for half in range(2):
                sp.wait_ge(q_out[half], B * 32)

        @block.vector
        def _(dve):
            def norm_part(b, chain, part):
                if part == 0:
                    dve.wait_ge(x_in, b * 16 + 16)
                    norm_stats(nc, chain, x, w)
                elif part == 1:
                    norm_root(nc, chain, w)
                else:
                    at_least(dve, tr_done, b)
                    norm_apply(nc, x, xn, w).then_inc(xn_ready, 1)

            def split_x(b, k):
                for d in range(DC):
                    dve.wait_ge(x_high, b * DC + d + 1)
                    nc.vector.tensor_tensor(xl[k][:, d, :], pT[:, d, :], xh[k][:, d, :].bitcast(F32), ALU.subtract).then_inc(x_low, 1)

            chain = Chain(dve, chain_s, 0, passed)
            for part in range(3):
                norm_part(0, chain, part)
            split_x(0, 0)

            def batch(b, k, follow):
                chain = Chain(dve, chain_s, (b + 1) * LN_LINKS, passed)
                at_least(dve, lat_out, b * 48)
                dve.wait_ge(high, b * JOBS + 1)
                nc.vector.tensor_tensor(ll[:, :], pL[0:LD, :], lh[0:LD, :].bitcast(F32), ALU.subtract).then_inc(low, 1)
                for q in range(PAIRS):
                    if q in NORM_AT and follow:
                        norm_part(b + 1, chain, NORM_AT.index(q))
                    if q == TURN_AT and follow:
                        split_x(b + 1, 1 - k)
                    if q % HALF == 0:
                        at_least(dve, q_out[q // HALF], b * 32)
                    dve.wait_ge(high, b * JOBS + q + 2)
                    nc.vector.tensor_tensor(ql[:, q, :], pQ[:, q % 4, :], qh[:, q, :].bitcast(F32), ALU.subtract).then_inc(low, 1)

            slotted_steps(dve, B, K, batch)

        @block.scalar
        def _(act):
            def turned(b, k):
                act.wait_ge(tr_done, b + 1)
                for d in range(DC):
                    nc.scalar.activation(xh[k][:, d, :], pT[:, d, :], ACT.Copy).then_inc(x_high, 1)

            turned(0, 0)

            def batch(b, k, follow):
                at_least(act, lat_out, b * 48)
                act.wait_ge(lat_done, b + 1)
                nc.scalar.activation(lh[:, :], pL[:, :], ACT.Copy).then_inc(high, 1)
                act.wait_ge(v_done, b + 1)
                nc.scalar.activation(v[:, :, :], pV[:, :, :], ACT.Copy).then_inc(v_ready, 1)
                for q in range(PAIRS):
                    if q == TURN_AT and follow:
                        turned(b + 1, 1 - k)
                    if q % HALF == 0:
                        at_least(act, q_out[q // HALF], b * 32)
                    act.wait_ge(q_done, b * PAIRS + q + 1)
                    nc.scalar.activation(qh[:, q, :], pQ[:, q % 4, :], ACT.Copy).then_inc(high, 1)

            slotted_steps(act, B, K, batch)

        @block.tensor
        def _(pe):
            def turn(b):
                pe.wait_ge(xn_ready, b + 1)
                at_least(pe, x_low, b * DC)
                transpose_tokens(nc, xn, g["ident"], pT).then_inc(tr_done, 1)

            turn(0)

            def batch(b, k, follow):
                pe.wait_ge(x_low, b * DC + DC)
                at_least(pe, low, b * JOBS - JOBS + 1)
                for d in range(DC):
                    last = three_passes(nc, pL[:, :], (g["ddh"][:, d, :, :], g["ddl"][:, d, :, :]), (xh[k][:, d, :], xl[k][:, d, :]),
                                        d == 0, d == DC - 1)
                last.then_inc(lat_done, 1)
                at_least(pe, v_ready, b)
                for t in range(TT):
                    for d in range(DC):
                        toks = slice(t * P, (t + 1) * P)
                        last = three_passes(nc, pV[:, t, :], (xh[k][:, d, toks], xl[k][:, d, toks]),
                                            (g["ddh"][:, d, 0, :], g["ddl"][:, d, 0, :]), d == 0, d == DC - 1)
                last.then_inc(v_done, 1)
                for q in range(PAIRS):
                    if q == TURN_AT and follow:
                        turn(b + 1)
                    at_least(pe, low, b * JOBS + q - 2 if q >= 4 else b * JOBS + q - 3)
                    for d in range(DC):
                        cols = slice(q * P, (q + 1) * P)
                        last = three_passes(nc, pQ[:, q % 4, :], (g["wth"][:, d, cols], g["wtl"][:, d, cols]),
                                            (xh[k][:, d, :], xl[k][:, d, :]), d == 0, d == DC - 1)
                    last.then_inc(q_done, 1)

            slotted_steps(pe, B, K, batch)


def latent_attention(nc, g):
    with ExitStack() as ctx:
        r = Resources(nc, ctx)
        K = 4
        q1 = [r.sb(f"b_q1_{k}", [P, 2, S], F32R) for k in range(K)]
        R = 96
        q2 = [r.sb(f"b_q2_{k}", [R + 1, 2, S], F32R) for k in range(K)]
        k1 = [r.sb(f"b_k1_{k}", [P, S], F32R) for k in range(K)]
        k2 = [r.sb(f"b_k2_{k}", [R + 1, S], F32R) for k in range(K)]
        v = [r.sb(f"b_v_{k}", [P, TT, LD], F32) for k in range(K)]
        negm = [r.sb(f"b_negm_{k}", [P, 2 * TT], F32) for k in range(K)]
        mT = [r.sb(f"b_mT_{k}", [2 * TT, P], F32R) for k in range(K)]
        z = [r.sb(f"b_z_{k}", [P, S], F32) for k in range(K)]
        prob = r.sb("b_prob", [P, TT, 2, S], F32)
        y = [r.sb(f"b_y_{k}", [P, 2, S], F32) for k in range(2)]
        rec = [r.sb(f"b_rec_{k}", [P, S], F32) for k in range(2)]
        pM = r.ps("b_pM", [P, 2, S])
        pS = r.ps("b_pS", [P, 2, 2, S])
        pY = r.ps("b_pY", [P, 2, S])
        loaded, row_in, stored = ([r.sem(f"b_{n}_{k}") for k in range(K)] for n in ("loaded", "row_in", "stored"))
        ones_set, max_mm, max_red, mT_ready = (r.sem(n) for n in ("b_ones_set", "b_max_mm", "b_max_red", "b_mT_ready"))
        st_done, exp_done, pv_done, y_ready, rec_done, z_ready = (r.sem(n) for n in (
            "b_st_done", "b_exp_done", "b_pv_done", "b_y_ready", "b_rec_done", "b_z_ready"))
        block = ctx.enter_context(nc.Block())
        STEPS = B * PAIRS
        MJ = 2 * TT + 1
        LOADS = 6

        PIECES = 4

        def is_first(it):
            return isinstance(it, int) and it == 0

        def steps(engine, body):
            slotted_steps(engine, STEPS, K, body)

        @block.sync
        def _(sp):
            def load(it, k):
                for src, dst in ((g["q0h"], q1[k][0:LD]), (g["q0l"], q1[k][LD:P]), (g["q0h"], q2[k][0:LD])):
                    sp.dma_start(dst.bitcast(F32), src[it].rearrange("(a d) n -> d a n", a=2)).then_inc(loaded[k], 16)
                sp.dma_start(k1[k][:, :].bitcast(F32), g["lat_h"][it // PAIRS]).then_inc(loaded[k], 16)
                sp.dma_start(k2[k][0:LD, :].bitcast(F32), g["lat_l"][it // PAIRS]).then_inc(loaded[k], 16)
                sp.dma_start(v[k][:, :, :], g["lat_v"][it // PAIRS]).then_inc(loaded[k], 16)

            def row(it, k):
                sp.wait_ge(mT_ready, it + 1)
                sp.dma_start(q2[k][R:R + 1, :, :].bitcast(F32), mT[k][:, :].bitcast(F32)).then_inc(row_in[k], 16)

            for n in range(3):
                load(n, n)
            row(0, 0)
            row(1, 1)

            def body(it, k, follow):
                if follow >= 3:
                    at_least(sp, pv_done, it * TT)
                    load(it + 3, (k + 3) % K)
                if follow >= 2:
                    row(it + 2, (k + 2) % K)

            steps(sp, body)

        @block.gpsimd
        def _(pool):
            def body(it, k, follow):
                pool.wait_ge(rec_done, PIECES * it + PIECES)
                at_least(pool, stored[k], (it // K) * 16)
                nc.gpsimd.tensor_tensor(z[k][:, :], y[k % 2][:, 0, :], rec[k % 2][:, :], ALU.mult).then_inc(z_ready, 1)
                pool.wait_ge(z_ready, it + 1)
                pool.dma_start(g["z0"][it], z[k][:, :]).then_inc(stored[k], 16)

            steps(pool, body)
            for k in range(K):
                pool.wait_ge(stored[k], 16 * STEPS // K)

        @block.vector
        def _(dve):
            for k in range(K):
                nc.vector.memset(q2[k][LD:R, :, :].bitcast(F32), 0.0)
                last = nc.vector.memset(k2[k][LD:R + 1, :].bitcast(F32), 1.0)
            last.then_inc(ones_set, 1)

            def read_max(it, k, j):
                slot = (k * MJ + j) % 2
                dve.wait_ge(max_mm, it * MJ + j + 1)
                if j < 2 * TT:
                    nc.vector.tensor_reduce(negm[k][:, j:j + 1], pM[:, slot, 0:P * (j % TT + 1)], AX.X, ALU.max,
                                            negate=True).then_inc(max_red, 1)
                else:
                    nc.vector.tensor_copy(mT[k][:, :], pM[0:2 * TT, slot, 0:P]).then_inc(mT_ready, 1)

            def reciprocals(it, k, piece):
                if piece == 0:
                    dve.wait_ge(y_ready, it + 1)
                part = slice(piece * S // PIECES, (piece + 1) * S // PIECES)
                nc.vector.reciprocal(rec[k % 2][:, part], y[k % 2][:, 1, part]).then_inc(rec_done, 1)

            for n in range(2):
                for j in range(MJ):
                    read_max(n, n, j)

            def body(it, k, follow):
                for j in range(MJ):
                    if follow >= 2:
                        read_max(it + 2, (k + 2) % K, j)
                    if not is_first(it) and j >= MJ - PIECES:
                        reciprocals(it - 1, k - 1, j - (MJ - PIECES))

            steps(dve, body)
            for piece in range(PIECES):
                reciprocals(STEPS - 1, K - 1, piece)

        @block.scalar
        def _(act):
            def copy_sums(it, k):
                act.wait_ge(pv_done, it * TT + TT)
                at_least(act, z_ready, it - 1)
                nc.scalar.activation(y[k % 2][:, :, :], pY[:, :, :], ACT.Copy).then_inc(y_ready, 1)

            def body(it, k, follow):
                for j in range(TT):
                    act.wait_ge(st_done, it * TT + j + 1)
                    nc.scalar.activation(prob[:, j, :, P * j:S], pS[:, j % 2, :, P * j:S], ACT.Exp, scale=HD ** -0.5).then_inc(exp_done, 1)
                    if j == 1 and not is_first(it):
                        copy_sums(it - 1, k - 1)

            steps(act, body)
            copy_sums(STEPS - 1, K - 1)

        @block.tensor
        def _(pe):
            def max_job(it, k, j):
                slot = (k * MJ + j) % 2
                if j == 0:
                    pe.wait_ge(loaded[k], (it // K) * (16 * LOADS) + 16 * LOADS)
                if not (isinstance(it, int) and it == 0 and j < 2):
                    if j >= 2:
                        pe.wait_ge(max_red, it * (MJ - 1) + j - 1)
                    elif j == 1:
                        pe.wait_ge(mT_ready, it)
                    else:
                        pe.wait_ge(max_red, it * (MJ - 1))
                if j < 2 * TT:
                    h, t = j // TT, j % TT
                    nc.tensor.matmul(pM[:, slot, 0:P * (t + 1)], q1[k][:, h, t * P:(t + 1) * P], k1[k][:, 0:P * (t + 1)],
                                     start=True, stop=False)
                    nc.tensor.matmul(pM[:, slot, P * t:P * (t + 1)], g["identb"][:, :], g["mask_n"][:, :],
                                     start=False, stop=True).then_inc(max_mm, 1)
                else:
                    pe.wait_ge(max_red, it * (MJ - 1) + MJ - 1)
                    nc.tensor.transpose(pM[0:2 * TT, slot, 0:P], negm[k][:, :], g["ident"][:, :]).then_inc(max_mm, 1)

            for n in range(2):
                for j in range(MJ):
                    max_job(n, n, j)

            def scores(it, k, j, then):
                if j == 0:
                    pe.wait_ge(ones_set, 1)
                    pe.wait_ge(row_in[k], (it // K) * 16 + 16)
                at_least(pe, exp_done, it * TT + j - 1)
                for h in range(2):
                    out = pS[:, j % 2, h, P * j:S]
                    nc.tensor.matmul(out, k1[k][:, P * j:P * (j + 1)], q1[k][:, h, P * j:S], start=True, stop=False)
                    nc.tensor.matmul(out, k2[k][:, P * j:P * (j + 1)], q2[k][:, h, P * j:S], start=False, stop=False)
                    last = nc.tensor.matmul(pS[:, j % 2, h, P * j:P * (j + 1)], g["identb"][:, :], g["mask_t"][:, :],
                                            start=False, stop=True)
                    if h == 1:
                        last.then_inc(st_done, 1)
                    then(1)

            def values(it, k, j):
                pe.wait_ge(exp_done, it * TT + j + 1)
                if j == 0:
                    at_least(pe, y_ready, it)
                for n, w in enumerate((v[k][:, j, :], g["ones"][:, 0:LD])):
                    for h in range(2):
                        last = nc.tensor.matmul(pY[h * LD:(h + 1) * LD, n, P * j:S], w, prob[:, j, h, P * j:S],
                                                start=j == 0, stop=j == TT - 1)
                last.then_inc(pv_done, 1)

            def body(it, k, follow):
                made = 0

                def some(n):
                    nonlocal made
                    for j in range(made, min(made + n, MJ if follow >= 2 else 0)):
                        max_job(it + 2, (k + 2) % K, j)
                    made += n

                for j in range(TT):
                    scores(it, k, j, some)
                    if j >= 2:
                        values(it, k, j - 2)
                    elif not is_first(it):
                        values(it - 1, k - 1, j + 2)
                    if j == 1:
                        some(1)

            steps(pe, body)
            for j in range(TT - 2, TT):
                values(STEPS - 1, K - 1, j)


def cross_stage(nc, g, i):
    with ExitStack() as ctx:
        r = Resources(nc, ctx)
        z = r.sb("c_z", [P, PAIRS, S], F32)
        x = r.sb("c_x", [P, TT, D], F32)
        xn = r.sb("c_xn", [P, TT, D], F32)
        xnT = r.sb("c_xnT", [P, DC, S], F32)
        c = r.sb("c_ctx", [P, CT, CW], F32)
        cT = r.sb("c_ctxT", [P, SC], F32)
        w = ln_work(r, "c")
        sh = r.sb("c_sh", [P, 3, DC, S], F32R)
        sl = r.sb("c_sl", [P, 3, DC, S], F32R)
        ch = r.sb("c_ch", [P, DC, SCP], F32R)
        cl = r.sb("c_cl", [P, DC, SCP], F32R)
        vx = r.sb("c_vx", [P, CH, H1, 2 * HW], F32)
        pO = r.ps("c_pO", [P, TT, D])
        pT = r.ps("c_pT", [P, DC, S])
        pJ = r.ps("c_pJ", [P, 4, 512])
        z_in, x_in, c_in, chain_s, ones_set = (r.sem(n) for n in ("c_z_in", "c_x_in", "c_c_in", "c_chain", "c_ones_set"))
        o_done, xn_ready, tr_done, xnT_ready = (r.sem(n) for n in ("c_o_done", "c_xn_ready", "c_tr_done", "c_xnT_ready"))
        job_done, high, low, vals, ctr = (r.sem(n) for n in ("c_job_done", "c_high", "c_low", "c_vals", "c_ctr"))
        keys_out, cvals_out, vals_out, passed = (r.sem(n) for n in ("c_keys_out", "c_cvals_out", "c_vals_out", "c_passed"))
        splits_out = [r.sem(f"c_splits_out_{t}") for t in range(3)]
        block = ctx.enter_context(nc.Block())

        jobs = [("ctx", n) for n in range(-(-CT // 4))]
        jobs += [("key", m, n) for m in range(DC) for n in range(4)]
        jobs += [("cval", n) for n in range(-(-CT // 2))]
        jobs += [("split", t, m) for t in range(3) for m in range(DC)]
        jobs += [("val", n) for n in range(TT // 2)]
        NJ = len(jobs)
        OUTPUT_AT, NORM_AT, TURN_AT = 0, (0, 1, 8, 13), 17
        kinds = {"ctx": ("ctx",), "split": ("key", "split"), "value": ("cval", "val")}

        def count(kind, upto):
            return sum(1 for q in jobs[:upto] if q[0] in kinds[kind])

        NCTX, NSPL, NVAL = (count(n, NJ) for n in ("ctx", "split", "value"))
        NCOL = [(0, 400), (400, 400), (800, 400), (1200, 401)]
        NKEY, NCV = sum(q[0] == "key" for q in jobs), sum(q[0] == "cval" for q in jobs)

        def freed(engine, b, n):
            kind = jobs[n][0]
            if kind == "ctx":
                engine.wait_ge(ctr, b * NCTX + count("ctx", n + 1))
            elif kind in ("key", "split"):
                engine.wait_ge(low, b * NSPL + count("split", n + 1))
            else:
                engine.wait_ge(vals, b * NVAL + count("value", n + 1))

        @block.sync
        def _(sp):
            def load_context(b):
                sp.dma_start(c[:, 0:CT - 1, :], i["ctx"][b, 0:(CT - 1) * P].rearrange("(t p) d -> p t d", p=P)).then_inc(c_in, 16)
                sp.dma_start(c[0:LAST, CT - 1, :], i["ctx"][b, (CT - 1) * P:SC]).then_inc(c_in, 16)

            def load_z(b):
                sp.dma_start(z[:, :, :], g["z0"][bass.ds(b * PAIRS, PAIRS)].rearrange("q p n -> p q n")).then_inc(z_in, 16)

            def load_x(b):
                sp.dma_start(x[:, :, :], i["x"][b].rearrange("(t p) d -> p t d", p=P)).then_inc(x_in, 16)

            def batch(b, follow):
                if follow:
                    wait_apart(sp, passed, ctr, b * NCTX + NCTX)
                    load_context(b + 1)
                    wait_apart(sp, passed, o_done, b + 1)
                    load_z(b + 1)
                    wait_apart(sp, passed, xn_ready, b + 1)
                    load_x(b + 1)
                wait_apart(sp, passed, low, b * NSPL + NKEY)
                for src, dst in ((ch, g["c1h"]), (cl, g["c1l"])):
                    view = dst[bass.ds(b * QUADS, QUADS)].rearrange("(m a) r n -> (a r) m n", a=2)
                    sp.dma_start(view[:, :, 0:SC], src[:, :, 0:SC].bitcast(F32)).then_inc(keys_out, 16)
                    sp.dma_start(view[:, :, SC:SCP], src[:, :, SC - 1:SC].bitcast(F32), allow_slow_non_contiguous=True).then_inc(keys_out, 16)
                wait_apart(sp, passed, vals, b * NVAL + NCV)
                sp.wait_ge(ones_set, 1)
                for q in range(QUADS):
                    view = g["v1"][b * QUADS + q].rearrange("p c (h n) -> p c h n", h=4)
                    sp.dma_start(view[:, TT:CH - 1], vx[:, TT:CH - 1, 4 * q:4 * q + 4, :]).then_inc(cvals_out, 16)
                    sp.dma_start(view[0:LAST, CH - 1], vx[0:LAST, CH - 1, 4 * q:4 * q + 4, :]).then_inc(cvals_out, 16)
                for t in range(3):
                    wait_apart(sp, passed, low, b * NSPL + NKEY + (t + 1) * DC)
                    for src, dst in ((sh, g["s1h"]), (sl, g["s1l"])):
                        sp.dma_start(dst[t, bass.ds(b * QUADS, QUADS)].rearrange("(m a) r n -> (a r) m n", a=2),
                                     src[:, t, :, :].bitcast(F32)).then_inc(splits_out[t], 16)
                wait_apart(sp, passed, vals, b * NVAL + NVAL)
                for q in range(QUADS):
                    view = g["v1"][b * QUADS + q].rearrange("p c (h n) -> p c h n", h=4)
                    sp.dma_start(view[:, 0:TT], vx[:, 0:TT, 4 * q:4 * q + 4, :]).then_inc(vals_out, 16)

            load_context(0)
            load_z(0)
            load_x(0)
            with sp.Fori(0, B - 1) as b:
                batch(b, True)
            batch(B - 1, False)
            sp.wait_ge(keys_out, B * 64)
            sp.wait_ge(cvals_out, B * 32 * QUADS)
            for t in range(3):
                sp.wait_ge(splits_out[t], B * 32)
            sp.wait_ge(vals_out, B * 16 * QUADS)

        @block.gpsimd
        def _(pool):
            nc.gpsimd.memset(vx[:, :, :, HW:2 * HW], 1.0).then_inc(ones_set, 1)

        @block.scalar
        def _(act):
            def batch(b):
                for n, job in enumerate(jobs):
                    if job[0] == "ctx":
                        if n == 0:
                            at_least(act, job_done, b * NJ)
                        at_least(act, job_done, b * NJ + n + 1)
                        lo, hi = job[1] * 512, min(SC, job[1] * 512 + 512)
                        nc.scalar.activation(cT[:, lo:hi], pJ[:, n % 4, 0:hi - lo], ACT.Copy).then_inc(ctr, 1)
                    if n == TURN_AT:
                        at_least(act, tr_done, b + 1)
                        for d in range(DC):
                            nc.scalar.activation(xnT[:, d, :], pT[:, d, :], ACT.Copy).then_inc(xnT_ready, 1)
                    if job[0] in ("key", "split"):
                        if job == ("key", 0, 0):
                            at_least(act, keys_out, b * 64)
                        if job[0] == "split" and job[2] == 0:
                            at_least(act, splits_out[job[1]], b * 32)
                        at_least(act, job_done, b * NJ + n + 1)
                        if job[0] == "key":
                            lo, wd = NCOL[job[2]]
                            dst, src, bias = ch[:, job[1], lo:lo + wd], pJ[:, n % 4, 0:wd], g["bias_col"][:, 3, job[1]:job[1] + 1]
                        else:
                            dst, src, bias = sh[:, job[1], job[2], :], pJ[:, n % 4, :], g["bias_col"][:, job[1], job[2]:job[2] + 1]
                        nc.scalar.activation(dst, src, ACT.Identity, bias=bias).then_inc(high, 1)

            batches(act, batch)

        @block.vector
        def _(dve):
            dve.wait_ge(ones_set, 1)
            def batch(b):
                chain = Chain(dve, chain_s, b * (LN_LINKS + 1), passed)

                def norm_part(part):
                    if part == 0:
                        at_least(dve, x_in, b * 16 + 16)
                        at_least(dve, o_done, b + 1)
                        res = g["x_res"][:, bass.ds(b * (TT * D), TT * D)]
                        chain.link(nc.vector.tensor_tensor(x[:, :, :].rearrange("p t d -> p (t d)"), x[:, :, :].rearrange("p t d -> p (t d)"),
                                                           pO[:, :, :].rearrange("p t d -> p (t d)"), ALU.add))
                        nc.vector.tensor_tensor(res.rearrange("p (t d) -> p t d", t=TT), x[:, :, :],
                                                g["bias_row"][:, 2, :].unsqueeze(1).broadcast_to([P, TT, D]), ALU.add)
                    elif part == 1:
                        norm_stats(nc, chain, x, w)
                    elif part == 2:
                        norm_root(nc, chain, w)
                    else:
                        at_least(dve, tr_done, b)
                        norm_apply(nc, x, xn, w).then_inc(xn_ready, 1)

                for n, job in enumerate(jobs):
                    if n in NORM_AT:
                        norm_part(NORM_AT.index(n))
                    if job[0] in ("key", "split"):
                        at_least(dve, high, b * NSPL + count("split", n + 1))
                        if job[0] == "key":
                            lo, wd = NCOL[job[2]]
                            dst, hi_, src, bias = (cl[:, job[1], lo:lo + wd], ch[:, job[1], lo:lo + wd], pJ[:, n % 4, 0:wd],
                                                   g["bias_col"][:, 3, job[1]:job[1] + 1])
                        else:
                            dst, hi_, src, bias = (sl[:, job[1], job[2], :], sh[:, job[1], job[2], :], pJ[:, n % 4, :],
                                                   g["bias_col"][:, job[1], job[2]:job[2] + 1])
                        nc.vector.scalar_tensor_tensor(out=dst, in0=src, scalar=bias, in1=hi_.bitcast(F32),
                                                       op0=ALU.add, op1=ALU.subtract).then_inc(low, 1)
                    if job[0] in ("cval", "val"):
                        if job[1] == 0:
                            done, each = (cvals_out, 32) if job[0] == "cval" else (vals_out, 16)
                            at_least(dve, done, b * each * QUADS)
                        at_least(dve, job_done, b * NJ + n + 1)
                        for a in range(2):
                            tile = 2 * job[1] + a
                            if job[0] == "cval" and tile >= CT:
                                continue
                            rows = LAST if job[0] == "cval" and tile == CT - 1 else P
                            at, row = (tile + TT, 1) if job[0] == "cval" else (tile, 0)
                            last = nc.vector.tensor_tensor(
                                vx[0:rows, at, :, 0:HW], pJ[0:rows, n % 4, a * D:(a + 1) * D].rearrange("p (h n) -> p h n", h=H1),
                                g["bias_row"][0:rows, row, :].rearrange("p (h n) -> p h n", h=H1), ALU.add)
                        last.then_inc(vals, 1)

            batches(dve, batch)

        @block.tensor
        def _(pe):
            def batch(b):
                for n, job in enumerate(jobs):
                    if n >= 4:
                        freed(pe, b, n - 4)
                    if n == 0:
                        at_least(pe, c_in, b * 32 + 32)
                        at_least(pe, low, b * NSPL)
                        at_least(pe, vals, b * NVAL)
                    slot = pJ[:, n % 4, :]
                    if job[0] == "ctx":
                        for q in range(4):
                            t = job[1] * 4 + q
                            if t < CT:
                                rows = P if t < CT - 1 else LAST
                                last = nc.tensor.transpose(slot[:, q * P:q * P + rows], c[0:rows, t, :], g["ident"][0:rows, 0:rows])
                        last.then_inc(job_done, 1)
                    if n == OUTPUT_AT:
                        at_least(pe, z_in, b * 16 + 16)
                        at_least(pe, xn_ready, b)
                        for t in range(TT):
                            for q in range(PAIRS):
                                last = nc.tensor.matmul(pO[:, t, :], z[:, q, t * P:(t + 1) * P], g["wvo"][:, q, :],
                                                        start=q == 0, stop=q == PAIRS - 1)
                        last.then_inc(o_done, 1)
                    if job[0] == "key":
                        at_least(pe, ctr, b * NCTX + NCTX)
                        lo, wd = NCOL[job[2]]
                        nc.tensor.matmul(slot[:, 0:wd], g["xWck"][:, job[1] * P:(job[1] + 1) * P], cT[:, lo:lo + wd],
                                         start=True, stop=True).then_inc(job_done, 1)
                    if job[0] == "cval":
                        for a in range(2):
                            t = 2 * job[1] + a
                            if t < CT:
                                rows = P if t < CT - 1 else LAST
                                last = nc.tensor.matmul(slot[0:rows, a * D:(a + 1) * D], cT[:, t * P:t * P + rows], g["xWcv"][:, :],
                                                        start=True, stop=True)
                        last.then_inc(job_done, 1)
                    if n == TURN_AT:
                        at_least(pe, xn_ready, b + 1)
                        at_least(pe, xnT_ready, b * DC)
                        transpose_tokens(nc, xn, g["ident"], pT).then_inc(tr_done, 1)
                    if job == ("split", 0, 0):
                        at_least(pe, xnT_ready, b * DC + DC)
                    if job[0] == "split":
                        wt = g[("xWq", "xWk", "xWcq")[job[1]]]
                        for d in range(DC):
                            last = nc.tensor.matmul(slot, wt[:, d, job[2] * P:(job[2] + 1) * P], xnT[:, d, :],
                                                    start=d == 0, stop=d == DC - 1)
                        last.then_inc(job_done, 1)
                    if job[0] == "val":
                        for a in range(2):
                            t = 2 * job[1] + a
                            for d in range(DC):
                                last = nc.tensor.matmul(slot[:, a * D:(a + 1) * D], xnT[:, d, t * P:(t + 1) * P], g["xWv"][:, d, :],
                                                        start=d == 0, stop=d == DC - 1)
                        last.then_inc(job_done, 1)

            batches(pe, batch)


def mixed_attention(nc, g):
    with ExitStack() as ctx:
        r = Resources(nc, ctx)
        K = 2
        R = 96
        qs = [r.sb(f"d_qs_{k}", [R + 1, 4, S], F32R) for k in range(K)]
        ks = [r.sb(f"d_ks_{k}", [R + 1, 4, S], F32R) for k in range(K)]
        qc = [r.sb(f"d_qc_{k}", [R + 1, 4, S], F32R) for k in range(K)]
        kc = [r.sb(f"d_kc_{k}", [R + 1, 4, SCP], F32R) for k in range(K)]
        v = [r.sb(f"d_v_{k}", [P, CH, 4 * 2 * HW], F32) for k in range(K)]
        part = [r.sb(f"d_part_{k}", [P, 4 * TT, 4], F32) for k in range(K)]
        negm = [r.sb(f"d_negm_{k}", [P, 8 * TT], F32) for k in range(K)]
        mT = [r.sb(f"d_mT_{k}", [4 * TT, 2, P], F32R) for k in range(K)]
        z = [r.sb(f"d_z_{k}", [P, TT * 4, HW], F32) for k in range(K)]
        prob = r.sb("d_prob", [P, 2, 4, S], F32)
        y = r.sb("d_y", [P, 2, S], F32)
        rec = r.sb("d_rec", [P, 2, TT * 4], F32)
        mean = r.sb("d_mean", [P, TT * 4, HW], F32)
        RING = 3
        pM = r.ps("d_pM", [P, RING, S])
        pS = r.ps("d_pS", [P, 2, 2, S])
        pY = r.ps("d_pY", [P, S])
        in_self, in_cross, in_v, self_row, cross_row, stored = (
            [r.sem(f"d_{n}_{k}") for k in range(K)] for n in ("in_self", "in_cross", "in_v", "self_row", "cross_row", "stored"))
        job_done, job_read, comb = (r.sem(n) for n in ("d_job_done", "d_job_read", "d_comb"))
        self_set, cross_set = ([r.sem(f"d_{n}_{k}") for k in range(K)] for n in ("self_set", "cross_set"))
        st_done, exp_done, pv_done, y_ready, rec_done, mean_done, z_part = (r.sem(n) for n in (
            "d_st_done", "d_exp_done", "d_pv_done", "d_y_ready", "d_rec_done", "d_mean_done", "d_z_part"))
        block = ctx.enter_context(nc.Block())
        STEPS = B * QUADS
        SELF, NK = 4 * TT, len(KCOLS)
        CROSS = [("cross", n) for n in range(SELF * NK)]
        MAXIMA = [("self", n) for n in range(SELF)] + CROSS[:4] + [("turn", 0)] + CROSS[4:]
        MJ = len(MAXIMA)
        TURN, EARLY, LATE = 3, 9, 45

        def is_first(it, n=0):
            return isinstance(it, int) and it == n

        def step_jobs(first, last):
            jobs = list(MAXIMA) if not last else []
            jobs.insert(min(TURN, len(jobs)), ("turn", 1))
            if not first:
                jobs.insert(min(EARLY, len(jobs)), ("sums", 1))
            jobs.insert(min(LATE, len(jobs)), ("sums", 0))
            return jobs

        def first_job(it):
            return MJ if is_first(it) else MJ - 1 + (MJ + 3) * it

        def turned(it, which, last=False):
            return first_job(it) + step_jobs(is_first(it), last).index(("turn", which)) + 1

        def before(it, n):
            if n >= RING:
                return RING
            jobs_before = MJ if is_first(it) else MJ + 2 if is_first(it, 1) else MJ + 3
            return n + jobs_before - max(m for m in range(jobs_before) if m % RING == n)

        def steps(engine, body):
            slotted_steps(engine, STEPS, K, body)

        @block.sync
        def _(sp):
            def stack(dst, parts, it, sem):
                for row, src in enumerate(parts):
                    sp.dma_start(dst[row * HW:(row + 1) * HW, :, :].bitcast(F32), src[it].rearrange("(h d) n -> d h n", h=4)).then_inc(sem, 16)

            def load_self(it, k):
                stack(qs[k], [g["s1h"][0], g["s1h"][0], g["s1l"][0], g["s1l"][0]], it, in_self[k])
                stack(ks[k], [g["s1h"][1], g["s1l"][1], g["s1h"][1], g["s1l"][1]], it, in_self[k])

            def load_cross(it, k):
                stack(qc[k], [g["s1h"][2], g["s1h"][2], g["s1l"][2], g["s1l"][2]], it, in_cross[k])
                stack(kc[k], [g["c1h"], g["c1l"], g["c1h"], g["c1l"]], it, in_cross[k])

            def load_v(it, k):
                sp.dma_start(v[k][:, 0:CH - 1, :], g["v1"][it][:, 0:CH - 1]).then_inc(in_v[k], 16)
                sp.dma_start(v[k][0:LAST, CH - 1, :], g["v1"][it][0:LAST, CH - 1]).then_inc(in_v[k], 16)

            def row(k, which):
                q, done = ((qs, self_row), (qc, cross_row))[which]
                sp.dma_start(q[k][R:R + 1, :, :].bitcast(F32), mT[k][:, which, :].bitcast(F32)).then_inc(done[k], 16)

            for n in range(K):
                load_self(n, n)
                load_cross(n, n)
                load_v(n, n)
            sp.wait_ge(job_read, MAXIMA.index(("turn", 0)) + 1)
            row(0, 0)

            def body(it, k, follow):
                sp.wait_ge(job_read, turned(it, 1, follow == 0))
                row(k, 1)
                if follow >= 2:
                    sp.wait_ge(st_done, it * 2 * CH + 2 * TT)
                    load_self(it + 2, k)
                if follow >= 1:
                    sp.wait_ge(job_read, turned(it, 0))
                    row(1 - k, 0)
                if follow >= 2:
                    sp.wait_ge(st_done, it * 2 * CH + 2 * CH)
                    load_cross(it + 2, k)
                    sp.wait_ge(pv_done, it * CH + CH)
                    load_v(it + 2, k)

            steps(sp, body)

        def fill(engine, stack, k, value, done):
            engine.memset(stack[k][4 * HW:R + int(value), :, :].bitcast(F32), value).then_inc(done[k], 1)

        @block.gpsimd
        def _(pool):
            fill(nc.gpsimd, kc, 0, 1.0, cross_set)
            fill(nc.gpsimd, qs, 1, 0.0, self_set)
            fill(nc.gpsimd, ks, 1, 1.0, self_set)
            fill(nc.gpsimd, qc, 1, 0.0, cross_set)
            fill(nc.gpsimd, kc, 1, 1.0, cross_set)

            def body(it, k, follow):
                pool.wait_ge(z_part, 2 * it + 2)
                pool.dma_start(g["z1"][it], z[k][:, :, :].rearrange("p a b -> p (a b)")).then_inc(stored[k], 16)

            steps(pool, body)
            for k in range(K):
                pool.wait_ge(stored[k], 16 * STEPS // K)

        @block.vector
        def _(dve):
            fill(nc.vector, qs, 0, 0.0, self_set)
            fill(nc.vector, ks, 0, 1.0, self_set)
            fill(nc.vector, qc, 0, 0.0, cross_set)

            def read_max(k, kind, n, number, slot):
                dve.wait_ge(job_done, number + 1)
                if kind == "self":
                    nc.vector.tensor_reduce(negm[k][:, n:n + 1], pM[:, slot, 0:P * (n % TT + 1)], AX.X, ALU.max,
                                            negate=True).then_inc(job_read, 1)
                elif kind == "cross":
                    nc.vector.tensor_reduce(part[k][:, n // NK, n % NK:n % NK + 1], pM[:, slot, 0:KCOLS[n % NK][1]], AX.X,
                                            ALU.max, negate=True).then_inc(job_read, 1)
                    if n == SELF * NK - 1:
                        dve.wait_ge(job_read, number + 1)
                        nc.vector.tensor_reduce(negm[k][:, SELF:2 * SELF], part[k][:, :, :], AX.X, ALU.min).then_inc(comb, 1)
                else:
                    nc.vector.tensor_copy(mT[k][:, n, :], pM[0:SELF, slot, 0:P]).then_inc(job_read, 1)

            def read_sums(it, k, cross, number, slot):
                sums = pM[:, slot, :].rearrange("p (a b) -> p a b", b=2 * HW)
                dve.wait_ge(job_done, number + 1)
                nc.vector.reciprocal(rec[:, cross, :], sums[:, :, HW]).then_inc(rec_done, 1)
                dve.wait_ge(rec_done, 2 * it + cross + 1)
                factor = rec[:, cross, :].unsqueeze(2).broadcast_to([P, TT * 4, HW])
                if not cross:
                    at_least(dve, stored[k], it // K * 16)
                    nc.vector.tensor_tensor(z[k][:, :, :], sums[:, :, 0:HW], factor, ALU.mult).then_inc(job_read, 1)
                    dve.wait_ge(job_read, number + 1)
                    dve.sem_inc(z_part, 1)
                else:
                    nc.vector.tensor_tensor(mean[:, :, :], sums[:, :, 0:HW], factor, ALU.mult).then_inc(job_read, 1)
                    dve.wait_ge(job_read, number + 1)
                    nc.vector.tensor_tensor(z[k][:, :, :], z[k][:, :, :], mean[:, :, :], ALU.add).then_inc(z_part, 1)

            for number, (kind, n) in enumerate(MAXIMA):
                read_max(0, kind, n, number, number % RING)

            def body(it, k, follow):
                for n, (kind, m) in enumerate(step_jobs(is_first(it), follow == 0)):
                    number, slot = first_job(it) + n, n % RING
                    if kind != "sums":
                        read_max(k if (kind, m) == ("turn", 1) else 1 - k, kind, m, number, slot)
                    else:
                        read_sums(it - m, 1 - k if m else k, m, number, slot)

            steps(dve, body)
            n = len(step_jobs(False, True))
            read_sums(STEPS - 1, (STEPS - 1) % K, 1, first_job(STEPS - 1) + n, n % RING)

        def chunk(c):
            if c < TT:
                return 0, c, c * P, P
            return 1, c - TT, 0, P if c < CH - 1 else LAST

        @block.scalar
        def _(act):
            def copy_sums(it, cross):
                act.wait_ge(pv_done, it * CH + (CH if cross else TT))
                at_least(act, z_part, 2 * it - 1 + cross)
                nc.scalar.activation(y[:, cross, :], pY[:, :], ACT.Copy).then_inc(y_ready, 1)

            def body(it, k, follow):
                for c in range(CH):
                    _, _, lo, n = chunk(c)
                    for a in range(2):
                        act.wait_ge(st_done, (it * CH + c) * 2 + a + 1)
                        nc.scalar.activation(prob[0:n, (k * CH + c) % 2, 2 * a:2 * a + 2, lo:S], pS[0:n, a, :, lo:S], ACT.Exp,
                                             scale=HW ** -0.5).then_inc(exp_done, 1)
                    if c == 0 and not is_first(it):
                        copy_sums(it - 1, 1)
                    if c == TT:
                        copy_sums(it, 0)

            steps(act, body)
            copy_sums(STEPS - 1, 1)

        @block.tensor
        def _(pe):
            def slot_read(it, n, number):
                at_least(pe, job_read, number - before(it, n) + 1)

            def make_max(it, k, kind, n, number, slot):
                if kind == "self":
                    if n == 0:
                        pe.wait_ge(self_set[k], 2)
                        pe.wait_ge(in_self[k], (it // K) * 128 + 128)
                    h, t = n // TT, n % TT
                    nc.tensor.matmul(pM[:, slot, 0:P * (t + 1)], qs[k][0:R, h, t * P:(t + 1) * P], ks[k][0:R, h, 0:P * (t + 1)],
                                     start=True, stop=False)
                    nc.tensor.matmul(pM[:, slot, P * t:P * (t + 1)], g["identb"][:, :], g["mask_n"][:, :],
                                     start=False, stop=True).then_inc(job_done, 1)
                elif kind == "cross":
                    if n == 0:
                        pe.wait_ge(cross_set[k], 2)
                        pe.wait_ge(in_cross[k], (it // K) * 128 + 128)
                    (lo, w), h, t = KCOLS[n % NK], n // NK // TT, n // NK % TT
                    nc.tensor.matmul(pM[:, slot, 0:w], qc[k][0:R, h, t * P:(t + 1) * P], kc[k][0:R, h, lo:lo + w],
                                     start=True, stop=True).then_inc(job_done, 1)
                elif n == 0:
                    pe.wait_ge(job_read, number - (MAXIMA.index(("turn", 0)) - SELF))
                    nc.tensor.transpose(pM[0:SELF, slot, 0:P], negm[k][:, 0:SELF], g["ident"][:, :]).then_inc(job_done, 1)
                else:
                    pe.wait_ge(comb, it + 1)
                    nc.tensor.transpose(pM[0:SELF, slot, 0:P], negm[k][:, SELF:2 * SELF], g["ident"][:, :]).then_inc(job_done, 1)

            def make_sums(it, cross, slot):
                pe.wait_ge(y_ready, 2 * it + cross + 1)
                for t in range(TT):
                    last = nc.tensor.transpose(pM[:, slot, t * P:(t + 1) * P], y[:, cross, t * P:(t + 1) * P], g["ident"][:, :])
                last.then_inc(job_done, 1)

            for n, (kind, m) in enumerate(MAXIMA):
                if n >= RING:
                    pe.wait_ge(job_read, n - RING + 1)
                make_max(0, 0, kind, m, n, n % RING)

            def values(it, k, c):
                cross, j, lo, n = chunk(c)
                if c == 0:
                    pe.wait_ge(in_v[k], (it // K) * 32 + 32)
                if j == 0:
                    at_least(pe, y_ready, 2 * it + cross)
                pe.wait_ge(exp_done, (it * CH + c) * 2 + 2)
                for h in range(4):
                    last = nc.tensor.matmul(pY[32 * h:32 * h + 32, lo:S], v[k][0:n, c, 32 * h:32 * h + 32],
                                            prob[0:n, (k * CH + c) % 2, h, lo:S], start=j == 0, stop=c in (TT - 1, CH - 1))
                last.then_inc(pv_done, 1)

            def body(it, k, follow):
                jobs = step_jobs(is_first(it), follow == 0)
                shares, made = 5 * CH, 0

                def jobs_upto(share):
                    nonlocal made
                    upto = min(len(jobs), -(-len(jobs) * share // shares)) if follow else (share > 2) + (share > 8) + (share >= shares // 2)
                    for n in range(made, min(upto, len(jobs))):
                        kind, m = jobs[n]
                        number = first_job(it) + n
                        slot_read(it, n, number)
                        if (kind, m) == ("turn", 1):
                            make_max(it, k, kind, m, number, n % RING)
                        elif kind != "sums":
                            make_max(it + 1, 1 - k, kind, m, number, n % RING)
                        else:
                            make_sums(it - m, m, n % RING)
                    made = max(made, upto)

                share = 0
                for c in range(CH):
                    cross, j, lo, n = chunk(c)
                    keys, qry = (kc, qc) if cross else (ks, qs)
                    if j == 0:
                        pe.wait_ge((cross_row if cross else self_row)[k], (it // K) * 16 + 16)
                    for h in range(4):
                        a = h // 2
                        if h % 2 == 0 and c > 0:
                            pe.wait_ge(exp_done, (it * CH + c) * 2 + a - 1)
                        last = nc.tensor.matmul(pS[0:n, a, h % 2, lo:S], keys[k][:, h, j * P:j * P + n], qry[k][:, h, lo:S],
                                                start=True, stop=bool(cross))
                        if not cross:
                            last = nc.tensor.matmul(pS[:, a, h % 2, lo:lo + P], g["identb"][:, :], g["mask_t"][:, :],
                                                    start=False, stop=True)
                        if h % 2 == 1:
                            last.then_inc(st_done, 1)
                        share += 1
                        jobs_upto(share)
                    if c:
                        values(it, k, c - 1)
                    share += 1
                    jobs_upto(share)
                values(it, k, CH - 1)
                assert made >= len(jobs)

            steps(pe, body)
            n = len(step_jobs(False, True))
            slot_read(STEPS - 1, n, first_job(STEPS - 1) + n)
            make_sums(STEPS - 1, 1, n % RING)


def route_stage(nc, g, i):
    with ExitStack() as ctx:
        r = Resources(nc, ctx)
        K = 2
        z = [r.sb(f"e_z_{k}", [P, TT, D], F32) for k in range(K)]
        zT = r.sb("e_zT", [P, DC, S], F32)
        x = [r.sb(f"e_x_{k}", [P, TT, D], F32) for k in range(K)]
        rows = [r.sb(f"e_rows_{k}", [P, 2, TT, ROW], F32) for k in range(K)]
        xnT = r.sb("e_xnT", [P, DC, S], F32)
        o = r.sb("e_o", [P, TT, D], F32)
        w = ln_work(r, "e")

        def small(name, dt=F32, shape=(P, TT, NE)):
            return r.sb(f"e_{name}", list(shape), dt)

        lg, wt, rest, eq, s1, s2, gt, both, where, pick = (small(n) for n in (
            "lg", "wt", "rest", "eq", "s1", "s2", "gt", "both", "where", "pick"))
        mask = small("mask", BF16)
        run = small("run", BF16, (P, TT + 1, NE))
        top, tot, noop = (small(n, F32, (P, TT)) for n in ("top", "tot", "noop"))
        idx = [small(f"idx_{k}", I32, (P, 2, TT)) for k in range(K)]
        pO = r.ps("e_pO", [P, TT, D])
        pT = r.ps("e_pT", [P, DC, S])
        pZ = r.ps("e_pZ", [P, DC, S])
        pL = r.ps("e_pL", [P, TT, NE])
        pC = r.ps("e_pC", [P, TT, NE])
        z_in = [r.sem(f"e_z_in_{k}") for k in range(K)]
        front_chain, back_chain, pad_set, o_done, xn_ready, tr_done, xnT_ready = (r.sem(n) for n in (
            "e_front_chain", "e_back_chain", "e_pad_set", "e_o_done", "e_xn_ready", "e_tr_done", "e_xnT_ready"))
        lg_done, lg_ready, ex_ready, mask_ready, pos_done, copied, sent_ready, o_ready, sent, stored = (r.sem(n) for n in (
            "e_lg_done", "e_lg_ready", "e_ex_ready", "e_mask_ready", "e_pos_done", "e_copied", "e_sent_ready", "e_o_ready",
            "e_sent", "e_stored"))
        zt_done, zT_ready, passed = r.sem("e_zt_done"), r.sem("e_zT_ready"), r.sem("e_passed")
        block = ctx.enter_context(nc.Block())
        FRONT_LINKS, BACK_LINKS = LN_LINKS + 1, 36

        def over_tiles(a):
            return a.unsqueeze(2).broadcast_to([P, TT, NE])

        @block.sync
        def _(sp):
            def load(b, k):
                for q in range(QUADS):
                    sp.dma_start(z[k][:, :, q * 4 * HW:(q + 1) * 4 * HW],
                                 g["z1"][b * QUADS + q].rearrange("p (t n) -> p t n", t=TT)).then_inc(z_in[k], 16)

            for k in range(K):
                load(k, k)
            for k in range(WEIGHT_SLOTS):
                load_weights(sp, g, i, k, k)

            def batch(b, k, follow):
                if follow >= 2:
                    wait_apart(sp, passed, zt_done, b + 1)
                    load(b + 2, k)
                wait_apart(sp, passed, o_ready, b + 1)
                sp.dma_start(i["out"][b].rearrange("(t p) d -> p t d", p=P), o[:, :, :]).then_inc(stored, 16)

            slotted_steps(sp, B, K, batch)
            sp.wait_ge(stored, B * 16)

        @block.scalar
        def _(act):
            def copy_z(b):
                act.wait_ge(zt_done, b + 1)
                at_least(act, o_done, b)
                for d in range(DC):
                    nc.scalar.activation(zT[:, d, :], pZ[:, d, :], ACT.Copy).then_inc(zT_ready, 1)

            for b in range(2):
                copy_z(b)

            def batch(b, k, follow):
                act.wait_ge(tr_done, b + 1)
                for d in range(DC):
                    nc.scalar.activation(xnT[:, d, :], pT[:, d, :], ACT.Copy).then_inc(xnT_ready, 1)
                if follow >= 2:
                    copy_z(b + 2)
                act.wait_ge(lg_ready, b + 1)
                nc.scalar.activation(wt[:, :, :], lg[:, :, :], ACT.Exp).then_inc(ex_ready, 1)

            slotted_steps(act, B, K, batch)

        @block.vector
        def _(dve):
            V = nc.vector
            nc.vector.memset(run[:, :, :], 0.0)
            for k in range(K):
                last = nc.vector.memset(rows[k][:, :, :, D + 2:ROW], 0.0)
            last.then_inc(pad_set, 1)
            dve.wait_ge(pad_set, 1)

            def front(b, k):
                chain = Chain(dve, front_chain, b * FRONT_LINKS, passed)
                dve.wait_ge(o_done, b + 1)
                chain.link(V.tensor_tensor(x[k][:, :, :].rearrange("p t d -> p (t d)"), pO[:, :, :].rearrange("p t d -> p (t d)"),
                                           g["x_res"][:, bass.ds(b * (TT * D), TT * D)], ALU.add))
                layer_norm(nc, chain, x[k], rows[k][:, 0, :, 0:D], w,
                           xn_free=(sent, (b - K + 1) * 16 * 2 * TT)).then_inc(xn_ready, 1)
                assert chain.n == FRONT_LINKS

            front(0, 0)

            def batch(b, k, follow):
                if follow:
                    front(b + 1, 1 - k)
                chain = Chain(dve, back_chain, b * BACK_LINKS, passed)
                link = chain.link
                dve.wait_ge(xn_ready, b + 1)
                dve.wait_ge(lg_done, b + 1)
                link(V.tensor_tensor(lg[:, :, :], pL[:, :, :], g["router_bias"][:, :].unsqueeze(1).broadcast_to([P, TT, NE]), ALU.add))
                link(V.tensor_reduce(top[:, :], lg[:, :, :], AX.X, ALU.max))
                V.tensor_tensor(lg[:, :, :], lg[:, :, :], over_tiles(top[:, :]), ALU.subtract).then_inc(lg_ready, 1)
                dve.wait_ge(ex_ready, b + 1)
                link(V.tensor_reduce(tot[:, :], wt[:, :, :], AX.X, ALU.add))
                link(V.reciprocal(tot[:, :], tot[:, :]))
                link(V.tensor_tensor(wt[:, :, :], wt[:, :, :], over_tiles(tot[:, :]), ALU.mult))
                src = wt
                for n, sel in enumerate((s1, s2)):
                    m = rows[k][:, n, :, D]
                    link(V.tensor_reduce(m, src[:, :, :], AX.X, ALU.max))
                    link(V.tensor_tensor(eq[:, :, :], src[:, :, :], over_tiles(m), ALU.is_equal))
                    link(V.tensor_tensor(eq[:, :, :], eq[:, :, :], g["prio"][:, :, :], ALU.mult))
                    link(V.tensor_reduce(top[:, :], eq[:, :, :], AX.X, ALU.max))
                    link(V.tensor_tensor(sel[:, :, :], eq[:, :, :], over_tiles(top[:, :]), ALU.is_equal))
                    if n == 0:
                        link(V.scalar_tensor_tensor(out=rest[:, :, :], in0=sel[:, :, :], scalar=-2.0, in1=wt[:, :, :],
                                                    op0=ALU.mult, op1=ALU.add))
                        src = rest
                link(V.tensor_tensor(both[:, :, :], s1[:, :, :], s2[:, :, :], ALU.add))
                link(V.tensor_scalar(gt[:, :, :], wt[:, :, :], 0.0, None, ALU.is_gt))
                link(V.tensor_tensor(mask[:, :, :], both[:, :, :], gt[:, :, :], ALU.mult))
                link(V.tensor_copy(run[:, 0, :], run[:, TT, :]))
                for t in range(TT):
                    ins = V.tensor_tensor(run[:, t + 1, :], run[:, t, :], mask[:, t, :], ALU.add)
                    if t == TT - 1:
                        ins.then_inc(mask_ready, 1)
                        dve.wait_ge(mask_ready, b + 1)
                    else:
                        link(ins)
                link(V.tensor_tensor(noop[:, :], both[:, :, NX], wt[:, :, NX], ALU.mult))
                at_least(dve, stored, b * 16)
                for t in range(TT):
                    last = V.scalar_tensor_tensor(out=o[:, t, :], in0=rows[k][:, 0, t, 0:D], scalar=noop[:, t:t + 1],
                                                  in1=x[k][:, t, :], op0=ALU.mult, op1=ALU.add)
                last.then_inc(o_ready, 1)
                for n in range(2):
                    last = V.tensor_copy(rows[k][:, n, :, D + 1].bitcast(I32), g["tok"][:, :])
                link(last)
                link(V.tensor_scalar_add(g["tok"][:, :], g["tok"][:, :], float(S)))
                dve.wait_ge(pos_done, b + 1)
                link(V.tensor_scalar(eq[:, :, :], pC[:, :, :], float(CAP), None, ALU.is_lt))
                link(V.tensor_tensor(eq[:, :, :], eq[:, :, :], gt[:, :, :], ALU.mult))
                link(V.tensor_tensor(where[:, :, :], pC[:, :, :], g["slot0"][:, :, :], ALU.add))
                link(V.tensor_tensor(where[:, :, :], where[:, :, :], eq[:, :, :], ALU.mult))
                link(V.tensor_scalar_add(where[:, :, :], where[:, :, :], float(FAR)))
                for n, sel in enumerate((s1, s2)):
                    link(V.tensor_tensor(pick[:, :, :], where[:, :, :], sel[:, :, :], ALU.mult))
                    link(V.tensor_reduce(top[:, :], pick[:, :, :], AX.X, ALU.add))
                    ins = V.tensor_copy(idx[k][:, n, :], top[:, :])
                    if n == 0:
                        link(ins)
                    else:
                        ins.then_inc(sent_ready, 1)
                        dve.wait_ge(sent_ready, b + 1)
                assert chain.n == BACK_LINKS, chain.n

            slotted_steps(dve, B, K, batch)

        @block.tensor
        def _(pe):
            def turn_z(b, k):
                pe.wait_ge(z_in[k], (b // K) * (16 * QUADS) + 16 * QUADS)
                at_least(pe, zT_ready, b * DC)
                for d in range(DC):
                    for t in range(TT):
                        last = nc.tensor.transpose(pZ[:, d, t * P:(t + 1) * P], z[k][:, t, d * P:(d + 1) * P], g["ident"][:, :])
                last.then_inc(zt_done, 1)

            def output(b):
                pe.wait_ge(zT_ready, b * DC + DC)
                at_least(pe, front_chain, (b - 1) * FRONT_LINKS + 1)
                for t in range(TT):
                    for d in range(DC):
                        last = nc.tensor.matmul(pO[:, t, :], zT[:, d, t * P:(t + 1) * P], g["wp"][:, d, :],
                                                start=d == 0, stop=d == DC - 1)
                last.then_inc(o_done, 1)

            def logits(b, k):
                pe.wait_ge(xn_ready, b + 1)
                at_least(pe, xnT_ready, b * DC)
                transpose_tokens(nc, rows[k][:, 0, :, 0:D], g["ident"], pT).then_inc(tr_done, 1)
                pe.wait_ge(xnT_ready, b * DC + DC)
                at_least(pe, lg_ready, b)
                for t in range(TT):
                    for d in range(DC):
                        last = nc.tensor.matmul(pL[:, t, :], xnT[:, d, t * P:(t + 1) * P], g["rwT"][:, d, :],
                                                start=d == 0, stop=d == DC - 1)
                last.then_inc(lg_done, 1)

            def positions(b):
                pe.wait_ge(mask_ready, b + 1)
                for t in range(TT):
                    nc.tensor.matmul(pC[:, t, :], g["before"][:, :], mask[:, t, :], start=True, stop=False)
                    last = nc.tensor.matmul(pC[:, t, :], g["onesb"][:, :], run[:, t, :], start=False, stop=True)
                last.then_inc(pos_done, 1)

            turn_z(0, 0)
            output(0)
            turn_z(1, 1)

            def batch(b, k, follow):
                if follow:
                    output(b + 1)
                logits(b, k)
                if not (isinstance(b, int) and b == 0):
                    positions(b - 1)
                if follow >= 2:
                    turn_z(b + 2, k)

            slotted_steps(pe, B, K, batch)
            positions(B - 1)

        @block.gpsimd
        def _(pool):
            def batch(b, k, follow):
                wait_apart(pool, passed, xn_ready, b + 1)
                nc.gpsimd.tensor_copy(rows[k][:, 1, :, 0:D], rows[k][:, 0, :, 0:D]).then_inc(copied, 1)
                pool.wait_ge(sent_ready, b + 1)
                wait_apart(pool, passed, copied, b + 1)
                for n in range(2):
                    for t in range(TT):
                        pool.indirect_dma_start(
                            out=g["slot_rows"], out_offset=bass.IndirectOffsetOnAxis(ap=idx[k][:, n, t:t + 1].bitcast(U32), axis=0),
                            in_=rows[k][:, n, t, :], in_offset=None, bounds_check=SLOTS - 1, oob_is_err=False).then_inc(sent, 16)

            slotted_steps(pool, B, K, batch)
            pool.wait_ge(sent, B * 16 * 2 * TT)


def load_weights(sp, g, i, e, k):
    sp.dma_start(g["wi"][k][:, :, :], i["wi"][e].rearrange("(c p) f -> p c f", p=P)).then_inc(g["weights_in"][k], 16)
    sp.dma_start(g["wo"][k][:, :, :], i["wo"][e].rearrange("(c p) d -> p c d", p=P)).then_inc(g["weights_in"][k], 16)


def expert_stage(nc, g, i):
    with ExitStack() as ctx:
        r = Resources(nc, ctx)
        K = WEIGHT_SLOTS
        CTT = CAP // P
        wi, wo, weights_in = g["wi"], g["wo"], g["weights_in"]
        rows = [r.sb(f"f_rows_{k}", [P, CTT, ROW], F32) for k in range(K)]
        y = [r.sb(f"f_y_{k}", [P, CTT, D], F32) for k in range(K)]
        wih, wil = (r.sb(f"f_{n}", [P, DC, FI], F32R) for n in ("wih", "wil"))
        woh, wol = (r.sb(f"f_{n}", [P, FC, D], F32R) for n in ("woh", "wol"))
        xh, xl = (r.sb(f"f_{n}", [P, DC, CAP], F32R) for n in ("xh", "xl"))
        hh, hl = (r.sb(f"f_{n}", [P, FC, CAP], F32R) for n in ("hh", "hl"))
        pT = r.ps("f_pT", [P, DC, CAP])
        pH = r.ps("f_pH", [P, 4, CAP])
        pO = r.ps("f_pO", [P, CTT, D])
        rows_in = [r.sem(f"f_rows_in_{k}") for k in range(K)]
        wi_high, wi_low, wo_high, wo_low, x_high, x_low, h_high, h_low = (r.sem(f"f_{n}") for n in (
            "wi_high", "wi_low", "wo_high", "wo_low", "x_high", "x_low", "h_high", "h_low"))
        tr_done, h_done, o_done, y_ready, added = (r.sem(n) for n in ("f_tr_done", "f_h_done", "f_o_done", "f_y_ready", "f_added"))
        passed = r.sem("f_passed")
        block = ctx.enter_context(nc.Block())
        SPLIT_WO = 2

        def experts(engine, body):
            for k in range(K):
                body(k, k, True)
            with engine.Fori(1, NX // K) as m:
                for k in range(K):
                    body(m * K + k, k, True)
            body(NX - 1, 0, False)

        @block.sync
        def _(sp):
            def load_rows(e, k):
                sp.dma_start(rows[k][:, :, :], g["slot_rows"][bass.ds(e * CAP, CAP)].rearrange("(t p) c -> p t c", p=P)).then_inc(rows_in[k], 16)

            def body(e, k):
                wait_apart(sp, passed, wo_low, e - K + 1)
                load_weights(sp, g, i, e, k)
                wait_apart(sp, passed, added, (e - K + 1) * 16 * CTT)
                load_rows(e, k)

            for k in range(K):
                load_rows(k, k)
            with sp.Fori(1, NX // K) as m:
                for k in range(K):
                    body(m * K + k, k)
            body(NX - 1, 0)
            sp.wait_ge(added, NX * 16 * CTT)

        @block.tensor
        def _(pe):
            def turn(e, k):
                pe.wait_ge(rows_in[k], (e // K) * 16 + 16)
                at_least(pe, x_low, e * DC)
                for d in range(DC):
                    for t in range(CTT):
                        last = nc.tensor.transpose(pT[:, d, t * P:(t + 1) * P], rows[k][:, t, d * P:(d + 1) * P], g["ident"][:, :])
                last.then_inc(tr_done, 1)

            turn(0, 0)

            def body(e, k, follow):
                pe.wait_ge(wi_low, e + 1)
                pe.wait_ge(x_low, e * DC + DC)
                for f in range(FC):
                    at_least(pe, h_low, e * FC + f - 3)
                    for d in range(DC):
                        cols = slice(f * P, (f + 1) * P)
                        last = three_passes(nc, pH[:, f % 4, :], (wih[:, d, cols], wil[:, d, cols]), (xh[:, d, :], xl[:, d, :]),
                                            d == 0, d == DC - 1)
                    last.then_inc(h_done, 1)
                pe.wait_ge(wo_low, e + 1)
                pe.wait_ge(h_low, e * FC + FC)
                at_least(pe, y_ready, e)
                for t in range(CTT):
                    if t == CTT - 1 and follow:
                        turn(e + 1, 1 - k)
                    for f in range(FC):
                        toks = slice(t * P, (t + 1) * P)
                        last = three_passes(nc, pO[:, t, :], (hh[:, f, toks], hl[:, f, toks]), (woh[:, f, :], wol[:, f, :]),
                                            f == 0, f == FC - 1)
                last.then_inc(o_done, 1)

            experts(pe, body)

        @block.scalar
        def _(act):
            def split_wi(e, k):
                act.wait_ge(weights_in[k], (e // K) * 32 + 32)
                at_least(act, h_done, e * FC)
                nc.scalar.activation(wih[:, :, :], wi[k][:, :, :], ACT.Copy).then_inc(wi_high, 1)

            def split_x(e):
                act.wait_ge(tr_done, e + 1)
                for d in range(DC):
                    nc.scalar.activation(xh[:, d, :], pT[:, d, :], ACT.Copy).then_inc(x_high, 1)

            split_wi(0, 0)
            split_x(0)

            def body(e, k, follow):
                for f in range(FC):
                    if f == SPLIT_WO:
                        at_least(act, o_done, e)
                        nc.scalar.activation(woh[:, :, :], wo[k][:, :, :], ACT.Copy).then_inc(wo_high, 1)
                    act.wait_ge(h_done, e * FC + f + 1)
                    if f == 0:
                        at_least(act, o_done, e)
                    nc.scalar.activation(hh[:, f, :], pH[:, f % 4, :], ACT.Relu).then_inc(h_high, 1)
                if follow:
                    split_wi(e + 1, 1 - k)
                    split_x(e + 1)

            experts(act, body)

        @block.vector
        def _(dve):
            def split_wi(e, k):
                dve.wait_ge(wi_high, e + 1)
                nc.vector.tensor_tensor(wil[:, :, :], wi[k][:, :, :], wih[:, :, :].bitcast(F32), ALU.subtract).then_inc(wi_low, 1)

            def split_x(e):
                for d in range(DC):
                    dve.wait_ge(x_high, e * DC + d + 1)
                    nc.vector.tensor_tensor(xl[:, d, :], pT[:, d, :], xh[:, d, :].bitcast(F32), ALU.subtract).then_inc(x_low, 1)

            split_wi(0, 0)
            split_x(0)

            def body(e, k, follow):
                for f in range(FC):
                    if f == SPLIT_WO:
                        dve.wait_ge(wo_high, e + 1)
                        nc.vector.tensor_tensor(wol[:, :, :], wo[k][:, :, :], woh[:, :, :].bitcast(F32), ALU.subtract).then_inc(wo_low, 1)
                    dve.wait_ge(h_high, e * FC + f + 1)
                    nc.vector.scalar_tensor_tensor(out=hl[:, f, :], in0=pH[:, f % 4, :], scalar=0.0, in1=hh[:, f, :].bitcast(F32),
                                                   op0=ALU.max, op1=ALU.subtract).then_inc(h_low, 1)
                if follow:
                    split_wi(e + 1, 1 - k)
                    split_x(e + 1)
                dve.wait_ge(o_done, e + 1)
                at_least(dve, added, (e - K + 1) * 16 * CTT)
                for t in range(CTT):
                    last = nc.vector.tensor_scalar(y[k][:, t, :], pO[:, t, :], rows[k][:, t, D:D + 1], None, ALU.mult)
                last.then_inc(y_ready, 1)

            experts(dve, body)

        @block.gpsimd
        def _(pool):
            def body(e, k, follow):
                pool.wait_ge(y_ready, e + 1)
                at_least(pool, added, e * 16 * CTT)
                pool.sem_inc(passed, 1)
                for t in range(CTT):
                    pool.indirect_dma_start(
                        out=i["out"].rearrange("b s d -> (b s) d"),
                        out_offset=bass.IndirectOffsetOnAxis(ap=rows[k][:, t, D + 1:D + 2].bitcast(U32), axis=0),
                        in_=y[k][:, t, :], in_offset=None, bounds_check=B * S - 1, oob_is_err=False,
                        compute_op=ALU.add).then_inc(added, 16)

            experts(pool, body)


def decoder_layer(nc, i):
    with ExitStack() as ctx:
        r = Resources(nc, ctx)

        def dram(name, shape, dt):
            return nc.dram_tensor(name, shape, dt, kind="Internal").ap()

        g = {
            "lat_h": dram("lat_h", [B, P, S], F32), "lat_l": dram("lat_l", [B, LD, S], F32),
            "lat_v": dram("lat_v", [B, P, TT, LD], F32),
            "q0h": dram("q0h", [B * PAIRS, P, S], F32), "q0l": dram("q0l", [B * PAIRS, P, S], F32),
            "z0": dram("z0", [B * PAIRS, P, S], F32),
            "s1h": dram("s1h", [3, B * QUADS, 4 * HW, S], F32), "s1l": dram("s1l", [3, B * QUADS, 4 * HW, S], F32),
            "c1h": dram("c1h", [B * QUADS, 4 * HW, SCP], F32), "c1l": dram("c1l", [B * QUADS, 4 * HW, SCP], F32),
            "v1": dram("v1", [B * QUADS, P, CH, 4 * 2 * HW], F32), "z1": dram("z1", [B * QUADS, P, TT * 4 * HW], F32),
            "slot_rows": dram("slot_rows", [SLOTS, ROW], F32),
            "ident": r.sb("ident", [P, P], F32), "identb": r.sb("identb", [P, P], BF16),
            "mask_t": r.sb("mask_t", [P, P], BF16), "mask_n": r.sb("mask_n", [P, P], BF16),
            "before": r.sb("before", [P, P], BF16), "onesb": r.sb("onesb", [P, P], BF16), "ones": r.sb("ones", [P, P], F32),
            "tok": r.sb("tok", [P, TT], I32), "slot0": r.sb("slot0", [P, TT, NE], I32), "prio": r.sb("prio", [P, TT, NE], I32),
            "bias_col": r.sb("bias_col", [P, 4, DC], F32), "bias_row": r.sb("bias_row", [P, 3, D], F32),
            "router_bias": r.sb("router_bias", [P, NE], F32), "rwT": r.sb("rwT", [P, DC, NE], F32),
            "wp": r.sb("wp", [P, DC, D], F32),
            "x_res": r.sb("x_res", [P, B * TT * D], F32),
        }
        with ExitStack() as early:
            re = Resources(nc, early)
            for name in ("xWq", "xWk", "xWcq", "xWv"):
                g[name] = re.sb(name, [P, DC, D], F32)
            for name in ("xWck", "xWcv"):
                g[name] = re.sb(name, [P, D], F32)
            g["wvo"] = re.sb("wvo", [P, PAIRS, D], F32)
            with ExitStack() as first:
                g["empty"] = Resources(nc, first).sb("empty", [P, SLOTS // P, ROW], F32)
                g["empty_out"] = Resources(nc, first).sem("empty_out")
                for part in "hl":
                    g[f"wt{part}"] = Resources(nc, first).sb(f"wt{part}", [P, DC, H0 * LD], F32R)
                    g[f"dd{part}"] = Resources(nc, first).sb(f"dd{part}", [P, DC, 2, LD], F32R)
                prepare(nc, g, i)
                latent_stage(nc, g, i)
            latent_attention(nc, g)
            cross_stage(nc, g, i)
        mixed_attention(nc, g)
        late = Resources(nc, ctx)
        g["wi"] = [late.sb(f"wi_{k}", [P, DC, FI], F32) for k in range(WEIGHT_SLOTS)]
        g["wo"] = [late.sb(f"wo_{k}", [P, FC, D], F32) for k in range(WEIGHT_SLOTS)]
        g["weights_in"] = [late.sem(f"weights_in_{k}") for k in range(WEIGHT_SLOTS)]
        route_stage(nc, g, i)
        expert_stage(nc, g, i)


INPUTS = {"x": "x", "ctx_512": "ctx", "L0_attn_Wq": "Wq", "L0_attn_Wkv_down": "Wkv_down", "L0_attn_Wk_up": "Wk_up",
          "L0_attn_Wv_up": "Wv_up", "L0_attn_Wout": "Wout", "L0_xattn_Wk": "xWk", "L0_xattn_bk": "xbk", "L0_xattn_Wq": "xWq",
          "L0_xattn_bq": "xbq", "L0_xattn_Wv": "xWv", "L0_xattn_bv": "xbv", "L0_xattn_Wck": "xWck", "L0_xattn_bck": "xbck",
          "L0_xattn_Wcq": "xWcq", "L0_xattn_bcq": "xbcq", "L0_xattn_Wcv": "xWcv", "L0_xattn_bcv": "xbcv",
          "L0_xattn_Wp": "xWp", "L0_xattn_bp": "xbp", "L0_ffn_router_w": "router_w", "L0_ffn_router_b": "router_b",
          "L0_ffn_experts_inter": "wi", "L0_ffn_experts_out": "wo"}


def kernel(**inputs):
    import numpy as np
    import concourse.bacc as bacc
    from concourse.bass_utils import run_bass_kernel_spmd

    nc = bacc.Bacc("TRN2", target_bir_lowering=False, num_devices=1)
    arrays, aps = {}, {}
    for name, short in INPUTS.items():
        a = np.ascontiguousarray(inputs[name])
        arrays[f"in_{name}"] = a
        aps[short] = nc.dram_tensor(f"in_{name}", a.shape, mybir.dt.from_np(a.dtype), kind="ExternalInput").ap()
    aps["out"] = nc.dram_tensor("out", [B, S, D], F32, kind="ExternalOutput").ap()
    decoder_layer(nc, aps)
    result = run_bass_kernel_spmd(nc, [arrays], core_ids=[0])
    return result.results[0]["out"]
```
